# Optimizing a Trainium2 kernel written in Bass

```python
import numpy as np
import jax
import jax.numpy as jnp

def _softmax(x, axis=-1):
    return jax.nn.softmax(x, axis=axis)

def _gelu(x):
    return jax.nn.gelu(x, approximate=True)

def _silu(x):
    return jax.nn.silu(x)

def _sigmoid(x):
    return jax.nn.sigmoid(x)

def _layernorm(x, axis=-1, eps=1e-05):
    m = jnp.mean(x, axis=axis, keepdims=True)
    v = jnp.var(x, axis=axis, keepdims=True)
    return (x - m) / jnp.sqrt(v + eps)

def _scatter_add(tgt, idx, src, axis=0):
    return tgt.at[idx].add(src)

def _segment_sum(src, seg, n):
    return jax.ops.segment_sum(src, seg, n)
kernel_name = 'mk_xattn_ffn_d4_seqx_r8_dade26'

def setup_inputs(seed: int=0):
    np.random.seed(seed)
    _w = jnp.asarray

    def _rec_inputs():
        import jax
        import jax.numpy as jnp
        _rk = jax.random.key(seed)
        x = -0.0002928 + 1 * jax.random.normal(jax.random.fold_in(_rk, 1), (8, 128, 256), jnp.float32)
        _lenS = 128 - jax.random.randint(jax.random.fold_in(_rk, 7), (8,), 0, max(1, 128 // 4) + 1, jnp.int32)
        _lenS2 = 128 - jax.random.randint(jax.random.fold_in(_rk, 8), (8,), 0, max(1, 128 // 4) + 1, jnp.int32)
        fside_S2_0 = -0.00337071 + 1.01897 * jax.random.normal(jax.random.fold_in(_rk, 11), (128,), jnp.float32)
        _ctx_2048P = jax.random.normal(jax.random.fold_in(_rk, 12), (8, 16, 256), jnp.float32)
        _ctx_2048c = jax.random.dirichlet(jax.random.fold_in(_rk, 512), 0.3 * jnp.ones((16,), jnp.float32), (8, 128))
        _ctx_2048t = jnp.einsum('bsk,bkd->bsd', _ctx_2048c, _ctx_2048P)
        _ctx_2048t = _ctx_2048t * jax.lax.rsqrt(jnp.mean(jnp.square(_ctx_2048t)) + 1e-12) * 0.953939
        ctx_2048 = 0.000675642 + 1.00031 * (_ctx_2048t + 0.3 * jax.random.normal(jax.random.fold_in(_rk, 612), (8, 128, 256), jnp.float32))
        _validS = jnp.arange(128)[None, :] < _lenS[:, None]
        _validS2 = jnp.arange(128)[None, :] < _lenS2[:, None]
        _causal = jnp.tril(jnp.ones((128, 128), dtype=bool))
        mask_SxS2_bc0 = jnp.logical_not(jnp.broadcast_to(_validS2[0:1, :], (128, 128)))
        mask_BxS2_bk0 = jnp.logical_not(jnp.broadcast_to(_validS2[:, :], (8, 128)))
        mask_BxSxS2_ff0 = jnp.where(jnp.ones((8, 128, 128), dtype=bool), 0.0, -1000000000.0).astype(jnp.float32)
        return (x, fside_S2_0, ctx_2048, mask_SxS2_bc0, mask_BxS2_bk0, mask_BxSxS2_ff0)
    x, fside_S2_0, ctx_2048, mask_SxS2_bc0, mask_BxS2_bk0, mask_BxSxS2_ff0 = _rec_inputs()

    def _L0_xattn_setup():
        import jax, jax.numpy as jnp
        import numpy as np
        key = jax.random.key(seed)
        ks = jax.random.split(key, 5)
        B, D, L, NH = (2, 128, 256, 8)
        H = D // NH
        return {'v': jax.random.normal(ks[0], (B, D, L), jnp.float32), 'k': jax.random.normal(ks[1], (H, L), jnp.float32) * 0.1, 'bias': jax.random.normal(ks[2], (D,), jnp.float32), 'x1': jax.random.normal(ks[3], (B, D, L), jnp.float32), 'x2': jax.random.normal(ks[4], (B, D, L), jnp.float32), 'num_heads': NH}
    _L0_xattn_all = _L0_xattn_setup()
    _L0_xattn_in = {k: v for k, v in _L0_xattn_all.items() if k in ('k',)}
    del _L0_xattn_all

    def _L0_ffn_setup():
        import jax, jax.numpy as jnp
        import numpy as np
        EPS = 1e-05

        def _bitlinear(x, w):
            rms = jax.lax.rsqrt(jnp.maximum(jnp.mean(w * w), EPS))
            w_quant = jnp.clip(jnp.round(w * rms), -1.0, 1.0) / rms
            w_quant = jax.lax.stop_gradient(w_quant - w) + w
            scale = 127.0 / jnp.maximum(jnp.max(jnp.abs(x), axis=-1, keepdims=True), EPS)
            x_quant = jnp.clip(jnp.round(x * scale), -128.0, 127.0) / scale
            x_quant = jax.lax.stop_gradient(x_quant - x) + x
            return jnp.einsum('bsd,fd->bsf', x_quant, w_quant)
        key = jax.random.key(seed)
        k1, k2, k3 = jax.random.split(key, 3)
        n_embd, d_ff = (256, 1024)
        B, S = (4, 256)
        x = jax.random.normal(k1, (B, S, n_embd), dtype=jnp.float32)
        w1 = jax.random.normal(k2, (d_ff, n_embd), dtype=jnp.float32) * 0.02
        w2 = jax.random.normal(k3, (n_embd, d_ff), dtype=jnp.float32) * 0.02
        return {'x': x, 'w1': w1, 'w2': w2}
    _L0_ffn_all = _L0_ffn_setup()
    _L0_ffn_in = {k: v for k, v in _L0_ffn_all.items() if k in ('w1', 'w2')}
    del _L0_ffn_all

    def _L1_xattn_setup():
        import jax, jax.numpy as jnp
        import numpy as np
        B, LQ, LKV = (4, 128, 128)
        HID, H, G = (256, 32, 8)
        HD = HID // H
        HPG = H // G
        key = jax.random.key(seed)
        ks = jax.random.split(key, 10)
        s = 0.02
        inp = {'X': jax.random.normal(ks[0], (B, LQ, HID), jnp.float32), 'encoder_output': jax.random.normal(ks[1], (B, LKV, HID), jnp.float32), 'causal_mask': jnp.triu(jnp.ones((LQ, LKV), bool), 1), 'padding_mask': jnp.zeros((B, LKV), bool).at[B // 2:, LKV - LKV // 4:].set(True), 'Wq': jax.random.normal(ks[2], (HID, HID), jnp.float32) * s, 'bq': jnp.zeros((HID,), jnp.float32), 'Wk': jax.random.normal(ks[3], (G * HD, HID), jnp.float32) * s, 'bk': jnp.zeros((G * HD,), jnp.float32), 'Wv': jax.random.normal(ks[4], (G * HD, HID), jnp.float32) * s, 'bv': jnp.zeros((G * HD,), jnp.float32), 'Wo': jax.random.normal(ks[5], (HID, HID), jnp.float32) * s, 'bo': jnp.zeros((HID,), jnp.float32)}
        return inp
    _L1_xattn_all = _L1_xattn_setup()
    _L1_xattn_in = {k: v for k, v in _L1_xattn_all.items() if k in ('Wq', 'bq', 'Wk', 'bk', 'Wv', 'bv', 'Wo', 'bo')}
    del _L1_xattn_all

    def _L1_ffn_setup():
        import jax, jax.numpy as jnp
        import numpy as np
        DIM = 256
        INNER = 1024
        EPS_RMS = 1e-06
        EPS_Q = 1e-05

        def simple_rms_norm(x, dim):
            rms = jnp.sqrt(jnp.mean(x * x, axis=-1, keepdims=True) + EPS_RMS)
            return x / rms * dim ** (-0.5)

        def activation_quant(x):
            scale = 127.0 / jnp.clip(jnp.max(jnp.abs(x), axis=-1, keepdims=True), EPS_Q)
            return jnp.clip(jnp.round(x * scale), -128, 127) / scale

        def weight_quant(w):
            return jnp.sign(w) * jnp.mean(jnp.abs(w))

        def bit_linear(x, w, b, dim_in):
            x_norm = simple_rms_norm(x, dim_in)
            x_q = activation_quant(x_norm)
            w_q = weight_quant(w)
            return jnp.einsum('bsd,od->bso', x_q, w_q) + b
        key = jax.random.key(seed)
        k1, k2, k3, k4, k5 = jax.random.split(key, 5)
        bound1 = 1.0 / np.sqrt(DIM)
        bound2 = 1.0 / np.sqrt(INNER)
        return {'x': jax.random.normal(k1, (4, 256, DIM), dtype=jnp.float32), 'w1': jax.random.uniform(k2, (INNER, DIM), jnp.float32, -bound1, bound1), 'b1': jax.random.uniform(k3, (INNER,), jnp.float32, -bound1, bound1), 'w2': jax.random.uniform(k4, (DIM, INNER), jnp.float32, -bound2, bound2), 'b2': jax.random.uniform(k5, (DIM,), jnp.float32, -bound2, bound2)}
    _L1_ffn_all = _L1_ffn_setup()
    _L1_ffn_in = {k: v for k, v in _L1_ffn_all.items() if k in ('w1', 'b1', 'w2', 'b2')}
    del _L1_ffn_all

    def _L2_xattn_setup():
        import jax, jax.numpy as jnp
        import numpy as np
        NUM_HEADS = 16
        EPS = 1e-08

        def _dyn_quant(x):
            s = jnp.maximum(jnp.max(jnp.abs(x), axis=-1, keepdims=True) / 127.0, EPS)
            q = jnp.clip(jnp.round(x / s), -127.0, 127.0)
            return (q, s)

        def _quant_weight(w):
            s = jnp.maximum(jnp.max(jnp.abs(w), axis=1, keepdims=True) / 127.0, EPS)
            q = jnp.clip(jnp.round(w / s), -127.0, 127.0)
            return (q, s)

        def _w8a8_linear(x, w, b):
            qx, sx = _dyn_quant(x)
            qw, sw = _quant_weight(w)
            y = jnp.einsum('bnc,oc->bno', qx, qw) * (sx * sw[:, 0])
            return y + b
        key = jax.random.key(seed)
        ks = jax.random.split(key, 9)
        B, N, L, C = (2, 512, 64, 256)
        sc = 0.02
        return {'x': jax.random.normal(ks[0], (B, N, C), jnp.float32), 'cond': jax.random.normal(ks[1], (B, L, C), jnp.float32), 'mask': jnp.zeros((B, N, L), jnp.float32), 'wq': jax.random.normal(ks[2], (C, C), jnp.float32) * sc, 'bq': jnp.zeros((C,), jnp.float32), 'wk': jax.random.normal(ks[3], (C, C), jnp.float32) * sc, 'bk': jnp.zeros((C,), jnp.float32), 'wv': jax.random.normal(ks[4], (C, C), jnp.float32) * sc, 'bv': jnp.zeros((C,), jnp.float32), 'wo': jax.random.normal(ks[5], (C, C), jnp.float32) * sc, 'bo': jnp.zeros((C,), jnp.float32)}
    _L2_xattn_all = _L2_xattn_setup()
    _L2_xattn_in = {k: v for k, v in _L2_xattn_all.items() if k in ('wq', 'bq', 'wk', 'bk', 'wv', 'bv', 'wo', 'bo')}
    del _L2_xattn_all

    def _L2_ffn_setup():
        import jax, jax.numpy as jnp
        import numpy as np
        H, I, E, K = (256, 512, 8, 2)
        B, S = (1, 256)

        def _silu_mul(gu):
            d = gu.shape[-1] // 2
            return jax.nn.silu(gu[..., :d]) * gu[..., d:]
        key = jax.random.key(seed)
        ks = jax.random.split(key, 6)
        w_scale = 0.02
        return {'x': jax.random.normal(ks[0], (B, S, H), jnp.float32), 'gate_w': jax.random.normal(ks[1], (H, E), jnp.float32) * w_scale, 'base_gate_up': jax.random.normal(ks[2], (H, 2 * I), jnp.float32) * w_scale, 'base_down': jax.random.normal(ks[3], (I, H), jnp.float32) * w_scale, 'expert_gate_up': jax.random.normal(ks[4], (E, H, 2 * I), jnp.float32) * w_scale, 'expert_down': jax.random.normal(ks[5], (E, I, H), jnp.float32) * w_scale}
    _L2_ffn_all = _L2_ffn_setup()
    _L2_ffn_in = {k: v for k, v in _L2_ffn_all.items() if k in ('gate_w', 'base_gate_up', 'base_down', 'expert_gate_up', 'expert_down')}
    del _L2_ffn_all

    def _L3_xattn_setup():
        import jax, jax.numpy as jnp
        import numpy as np
        N_HEAD = 8
        ALPHA = 5.0
        EPS = 1e-12

        def _l2norm(x, axis):
            n = jnp.sqrt(jnp.sum(x * x, axis=axis, keepdims=True))
            return x / jnp.maximum(n, EPS)
        key = jax.random.key(seed)
        kq, kk, kv = jax.random.split(key, 3)
        B, D, T = (4, 128, 256)
        q = jax.random.normal(kq, (B, D, T), dtype=jnp.float32)
        k = jax.random.normal(kk, (B, D, T), dtype=jnp.float32)
        v = jax.random.normal(kv, (B, D, T), dtype=jnp.float32)
        return {'q': q, 'k': k, 'v': v}
    _L3_xattn_all = _L3_xattn_setup()
    _L3_xattn_in = {k: v for k, v in _L3_xattn_all.items() if k in ()}
    del _L3_xattn_all

    def _L3_ffn_setup():
        import jax, jax.numpy as jnp
        import numpy as np
        E = 32
        K = 6
        H = 256
        I = 128
        T = 256
        CAP = 96
        SCALE = 1.5
        SWIGLU_LIMIT = 10.0
        key = jax.random.key(seed)
        ks = jax.random.split(key, 9)

        def s(k, shape, fan):
            return jax.random.normal(k, shape, jnp.float32) * fan ** (-0.5)
        return {'x': jax.random.normal(ks[0], (1, T, H), jnp.float32), 'gate_w': s(ks[1], (E, H), H), 'bias': jax.random.normal(ks[2], (E,), jnp.float32) * 0.01, 'w_gate': s(ks[3], (E, I, H), H), 'w_up': s(ks[4], (E, I, H), H), 'w_down': s(ks[5], (E, H, I), I), 'sg': s(ks[6], (I, H), H), 'su': s(ks[7], (I, H), H), 'sd': s(ks[8], (H, I), I)}
    _L3_ffn_all = _L3_ffn_setup()
    _L3_ffn_in = {k: v for k, v in _L3_ffn_all.items() if k in ('gate_w', 'bias', 'w_gate', 'w_up', 'w_down', 'sg', 'su', 'sd')}
    del _L3_ffn_all
    return {'x': x, 'fside_S2_0': fside_S2_0, 'ctx_2048': ctx_2048, 'mask_SxS2_bc0': mask_SxS2_bc0, 'mask_BxS2_bk0': mask_BxS2_bk0, 'mask_BxSxS2_ff0': mask_BxSxS2_ff0, 'L0_xattn_k': _L0_xattn_in['k'], 'L0_ffn_w1': _L0_ffn_in['w1'], 'L0_ffn_w2': _L0_ffn_in['w2'], 'L1_xattn_Wq': _L1_xattn_in['Wq'], 'L1_xattn_bq': _L1_xattn_in['bq'], 'L1_xattn_Wk': _L1_xattn_in['Wk'], 'L1_xattn_bk': _L1_xattn_in['bk'], 'L1_xattn_Wv': _L1_xattn_in['Wv'], 'L1_xattn_bv': _L1_xattn_in['bv'], 'L1_xattn_Wo': _L1_xattn_in['Wo'], 'L1_xattn_bo': _L1_xattn_in['bo'], 'L1_ffn_w1': _L1_ffn_in['w1'], 'L1_ffn_b1': _L1_ffn_in['b1'], 'L1_ffn_w2': _L1_ffn_in['w2'], 'L1_ffn_b2': _L1_ffn_in['b2'], 'L2_xattn_wq': _L2_xattn_in['wq'], 'L2_xattn_bq': _L2_xattn_in['bq'], 'L2_xattn_wk': _L2_xattn_in['wk'], 'L2_xattn_bk': _L2_xattn_in['bk'], 'L2_xattn_wv': _L2_xattn_in['wv'], 'L2_xattn_bv': _L2_xattn_in['bv'], 'L2_xattn_wo': _L2_xattn_in['wo'], 'L2_xattn_bo': _L2_xattn_in['bo'], 'L2_ffn_gate_w': _L2_ffn_in['gate_w'], 'L2_ffn_base_gate_up': _L2_ffn_in['base_gate_up'], 'L2_ffn_base_down': _L2_ffn_in['base_down'], 'L2_ffn_expert_gate_up': _L2_ffn_in['expert_gate_up'], 'L2_ffn_expert_down': _L2_ffn_in['expert_down'], 'L3_ffn_gate_w': _L3_ffn_in['gate_w'], 'L3_ffn_bias': _L3_ffn_in['bias'], 'L3_ffn_w_gate': _L3_ffn_in['w_gate'], 'L3_ffn_w_up': _L3_ffn_in['w_up'], 'L3_ffn_w_down': _L3_ffn_in['w_down'], 'L3_ffn_sg': _L3_ffn_in['sg'], 'L3_ffn_su': _L3_ffn_in['su'], 'L3_ffn_sd': _L3_ffn_in['sd']}

def reference(x, fside_S2_0, ctx_2048, mask_SxS2_bc0, mask_BxS2_bk0, mask_BxSxS2_ff0, L0_xattn_k, L0_ffn_w1, L0_ffn_w2, L1_xattn_Wq, L1_xattn_bq, L1_xattn_Wk, L1_xattn_bk, L1_xattn_Wv, L1_xattn_bv, L1_xattn_Wo, L1_xattn_bo, L1_ffn_w1, L1_ffn_b1, L1_ffn_w2, L1_ffn_b2, L2_xattn_wq, L2_xattn_bq, L2_xattn_wk, L2_xattn_bk, L2_xattn_wv, L2_xattn_bv, L2_xattn_wo, L2_xattn_bo, L2_ffn_gate_w, L2_ffn_base_gate_up, L2_ffn_base_down, L2_ffn_expert_gate_up, L2_ffn_expert_down, L3_ffn_gate_w, L3_ffn_bias, L3_ffn_w_gate, L3_ffn_w_up, L3_ffn_w_down, L3_ffn_sg, L3_ffn_su, L3_ffn_sd):
    import jax
    import jax.numpy as jnp

    def _L0_xattn_ref(v, k, bias, x1, x2, num_heads):
        import jax, jax.numpy as jnp
        import numpy as np
        B, D, L = v.shape
        H = D // num_heads
        fft_size = 2 * L
        vr = v.reshape(B, H, num_heads, L)
        x1r = x1.reshape(B, H, num_heads, L)
        x2r = x2.reshape(B, H, num_heads, L)
        kv = vr[:, :, :, None, :] * x2r[:, :, None, :, :]
        k_f = jnp.fft.rfft(k.astype(jnp.float32), n=fft_size)
        y = jnp.fft.irfft(jnp.fft.rfft(kv, n=fft_size) * k_f[None, :, None, None, :], n=fft_size)[..., :L]
        skip = bias.astype(jnp.float32).reshape(H, num_heads)[None, :, :, None, None]
        y = y + kv * skip
        out = jnp.einsum('bhijl,bhil->bhjl', y, x1r)
        return out.reshape(B, D, L)

    def _L0_ffn_ref(x, w1, w2):
        import jax, jax.numpy as jnp
        import numpy as np
        EPS = 1e-05

        def _bitlinear(x, w):
            rms = jax.lax.rsqrt(jnp.maximum(jnp.mean(w * w), EPS))
            w_quant = jnp.clip(jnp.round(w * rms), -1.0, 1.0) / rms
            w_quant = jax.lax.stop_gradient(w_quant - w) + w
            scale = 127.0 / jnp.maximum(jnp.max(jnp.abs(x), axis=-1, keepdims=True), EPS)
            x_quant = jnp.clip(jnp.round(x * scale), -128.0, 127.0) / scale
            x_quant = jax.lax.stop_gradient(x_quant - x) + x
            return jnp.einsum('bsd,fd->bsf', x_quant, w_quant)
        h = _bitlinear(x, w1)
        h = jax.nn.gelu(h, approximate=False)
        out = _bitlinear(h, w2)
        return out

    def _L1_xattn_ref(X, encoder_output, causal_mask, padding_mask, Wq, bq, Wk, bk, Wv, bv, Wo, bo):
        import jax, jax.numpy as jnp
        import numpy as np
        B, LQ, LKV = (4, 128, 128)
        HID, H, G = (256, 32, 8)
        HD = HID // H
        HPG = H // G
        b = X.shape[0]
        q = X @ Wq.T + bq
        k = encoder_output @ Wk.T + bk
        v = encoder_output @ Wv.T + bv
        q = q.reshape(b, LQ, G, HPG, HD).transpose(0, 2, 3, 1, 4)
        k = k.reshape(b, LKV, G, HD).transpose(0, 2, 1, 3)
        v = v.reshape(b, LKV, G, HD).transpose(0, 2, 1, 3)
        scores = jnp.einsum('bgrqd,bgkd->bgrqk', q, k) / jnp.sqrt(jnp.float32(HD))
        scores = jnp.where(causal_mask[None, None, None, :, :], -jnp.inf, scores)
        scores = jnp.where(padding_mask[:, None, None, None, :], -jnp.inf, scores)
        w = jax.nn.softmax(scores, axis=-1)
        out = jnp.einsum('bgrqk,bgkd->bgrqd', w, v)
        out = out.reshape(b, H, LQ, HD).transpose(0, 2, 1, 3).reshape(b, LQ, HID)
        return out @ Wo.T + bo

    def _L1_ffn_ref(x, w1, b1, w2, b2):
        import jax, jax.numpy as jnp
        import numpy as np
        DIM = 256
        INNER = 1024
        EPS_RMS = 1e-06
        EPS_Q = 1e-05

        def simple_rms_norm(x, dim):
            rms = jnp.sqrt(jnp.mean(x * x, axis=-1, keepdims=True) + EPS_RMS)
            return x / rms * dim ** (-0.5)

        def activation_quant(x):
            scale = 127.0 / jnp.clip(jnp.max(jnp.abs(x), axis=-1, keepdims=True), EPS_Q)
            return jnp.clip(jnp.round(x * scale), -128, 127) / scale

        def weight_quant(w):
            return jnp.sign(w) * jnp.mean(jnp.abs(w))

        def bit_linear(x, w, b, dim_in):
            x_norm = simple_rms_norm(x, dim_in)
            x_q = activation_quant(x_norm)
            w_q = weight_quant(w)
            return jnp.einsum('bsd,od->bso', x_q, w_q) + b
        h = bit_linear(x, w1, b1, DIM)
        h = jax.nn.gelu(h, approximate=False)
        return bit_linear(h, w2, b2, INNER)

    def _L2_xattn_ref(x, cond, mask, wq, bq, wk, bk, wv, bv, wo, bo):
        import jax, jax.numpy as jnp
        import numpy as np
        NUM_HEADS = 16
        EPS = 1e-08

        def _dyn_quant(x):
            s = jnp.maximum(jnp.max(jnp.abs(x), axis=-1, keepdims=True) / 127.0, EPS)
            q = jnp.clip(jnp.round(x / s), -127.0, 127.0)
            return (q, s)

        def _quant_weight(w):
            s = jnp.maximum(jnp.max(jnp.abs(w), axis=1, keepdims=True) / 127.0, EPS)
            q = jnp.clip(jnp.round(w / s), -127.0, 127.0)
            return (q, s)

        def _w8a8_linear(x, w, b):
            qx, sx = _dyn_quant(x)
            qw, sw = _quant_weight(w)
            y = jnp.einsum('bnc,oc->bno', qx, qw) * (sx * sw[:, 0])
            return y + b
        B, N, C = x.shape
        L = cond.shape[1]
        H = NUM_HEADS
        D = C // H
        inv_sqrt_d = np.float32(1.0 / np.sqrt(D))
        q = _w8a8_linear(x, wq, bq).reshape(B, N, H, D).transpose(0, 2, 1, 3)
        k = (cond @ wk.T + bk).reshape(B, L, H, D).transpose(0, 2, 1, 3)
        v = (cond @ wv.T + bv).reshape(B, L, H, D).transpose(0, 2, 1, 3)
        scores = jnp.einsum('bhnd,bhld->bhnl', q, k) * inv_sqrt_d + mask[:, None]
        attn = jax.nn.softmax(scores, axis=-1)
        o = jnp.einsum('bhnl,bhld->bhnd', attn, v)
        o = o.transpose(0, 2, 1, 3).reshape(B, N, C)
        return _w8a8_linear(o, wo, bo)

    def _L2_ffn_ref(x, gate_w, base_gate_up, base_down, expert_gate_up, expert_down):
        import jax, jax.numpy as jnp
        import numpy as np
        H, I, E, K = (256, 512, 8, 2)
        B, S = (1, 256)

        def _silu_mul(gu):
            d = gu.shape[-1] // 2
            return jax.nn.silu(gu[..., :d]) * gu[..., d:]
        base_y = _silu_mul(x @ base_gate_up) @ base_down
        b, s, h = x.shape
        xf = x.reshape(-1, h)
        n = xf.shape[0]
        n_exp = gate_w.shape[1]
        probs = jax.nn.softmax((xf @ gate_w).astype(jnp.float32), axis=-1)
        w, idx = jax.lax.top_k(probs, K)
        w = (w / w.sum(axis=-1, keepdims=True)).astype(x.dtype)
        comb = jnp.zeros((n, n_exp), x.dtype).at[jnp.arange(n)[:, None], idx].add(w)
        out = jnp.zeros_like(xf)
        for e in range(n_exp):
            y = _silu_mul(xf @ expert_gate_up[e]) @ expert_down[e]
            out = out + comb[:, e:e + 1] * y
        return out.reshape(b, s, h) + base_y

    def _L3_xattn_ref(q, k, v):
        import jax, jax.numpy as jnp
        import numpy as np
        N_HEAD = 8
        ALPHA = 5.0
        EPS = 1e-12

        def _l2norm(x, axis):
            n = jnp.sqrt(jnp.sum(x * x, axis=axis, keepdims=True))
            return x / jnp.maximum(n, EPS)
        B, D, Tq = q.shape
        Tk = k.shape[-1]
        Dv = v.shape[-2]
        h = N_HEAD
        d = D // h
        dv = Dv // h
        qh = q.reshape(B, h, d, Tq)
        kh = k.reshape(B, h, d, Tk)
        vh = v.reshape(B, h, dv, Tk)
        qn = _l2norm(qh, axis=-2)
        kn = _l2norm(kh, axis=-2)
        qk = ALPHA * jnp.einsum('bhdq,bhdk->bhqk', qn, kn)
        sm = jax.nn.softmax(qk, axis=-1)
        out = jnp.einsum('bhqk,bhdk->bhdq', sm, vh)
        return out.reshape(B, Dv, Tq)

    def _L3_ffn_ref(x, gate_w, bias, w_gate, w_up, w_down, sg, su, sd):
        import jax, jax.numpy as jnp
        import numpy as np
        E = 32
        K = 6
        H = 256
        I = 128
        T = 256
        CAP = 96
        SCALE = 1.5
        SWIGLU_LIMIT = 10.0
        B, S, Hd = x.shape
        h = x.reshape(-1, Hd)
        logits = h @ gate_w.T
        scores = jnp.sqrt(jax.nn.softplus(logits))
        _, topk_idx = jax.lax.top_k(scores + bias[None, :], K)
        topk_w = jnp.take_along_axis(scores, topk_idx, axis=1)
        topk_w = topk_w / jnp.sum(topk_w, axis=-1, keepdims=True)
        topk_w = topk_w * SCALE
        eid = topk_idx.reshape(-1)
        onehot = jax.nn.one_hot(eid, E, dtype=jnp.int32)
        pos = jnp.cumsum(onehot, axis=0) - 1
        pos = jnp.take_along_axis(pos, eid[:, None], axis=1)[:, 0]
        valid = pos < CAP
        pos = jnp.where(valid, pos, CAP)
        h_rep = jnp.repeat(h, K, axis=0)
        xb = jnp.zeros((E, CAP + 1, Hd), x.dtype).at[eid, pos].set(h_rep)
        g = jnp.einsum('ech,eih->eci', xb, w_gate)
        u = jnp.einsum('ech,eih->eci', xb, w_up)
        inter = jax.nn.silu(g) * u
        yb = jnp.einsum('eci,ehi->ech', inter, w_down)
        w_slot = jnp.where(valid, topk_w.reshape(-1), 0.0)
        y = yb[eid, pos] * w_slot[:, None]
        routed = y.reshape(-1, K, Hd).sum(axis=1)
        si = jax.nn.silu(h @ sg.T) * (h @ su.T)
        si = jnp.clip(si, -SWIGLU_LIMIT, SWIGLU_LIMIT)
        shared = si @ sd.T
        return (routed + shared).reshape(B, S, Hd)
    x = x + _L0_xattn_ref(_layernorm(x, axis=-1), L0_xattn_k, fside_S2_0, ctx_2048, ctx_2048, 8)
    x = x + _L0_ffn_ref(_layernorm(x, axis=-1), L0_ffn_w1, L0_ffn_w2)
    x = x + _L1_xattn_ref(_layernorm(x, axis=-1), ctx_2048, mask_SxS2_bc0, mask_BxS2_bk0, L1_xattn_Wq, L1_xattn_bq, L1_xattn_Wk, L1_xattn_bk, L1_xattn_Wv, L1_xattn_bv, L1_xattn_Wo, L1_xattn_bo)
    x = x + _L1_ffn_ref(_layernorm(x, axis=-1), L1_ffn_w1, L1_ffn_b1, L1_ffn_w2, L1_ffn_b2)
    x = x + _L2_xattn_ref(_layernorm(x, axis=-1), ctx_2048, mask_BxSxS2_ff0, L2_xattn_wq, L2_xattn_bq, L2_xattn_wk, L2_xattn_bk, L2_xattn_wv, L2_xattn_bv, L2_xattn_wo, L2_xattn_bo)
    x = x + _L2_ffn_ref(_layernorm(x, axis=-1), L2_ffn_gate_w, L2_ffn_base_gate_up, L2_ffn_base_down, L2_ffn_expert_gate_up, L2_ffn_expert_down)
    x = x + _L3_xattn_ref(_layernorm(x, axis=-1), ctx_2048, ctx_2048)
    x = x + _L3_ffn_ref(_layernorm(x, axis=-1), L3_ffn_gate_w, L3_ffn_bias, L3_ffn_w_gate, L3_ffn_w_up, L3_ffn_w_down, L3_ffn_sg, L3_ffn_su, L3_ffn_sd)
    return x

_drawn_inputs = setup_inputs


def setup_inputs(seed=0):
    import zlib

    import numpy as np

    out = dict(_drawn_inputs(seed))
    spreads = {'L1_xattn_bq': (0.0, 0.8),
     'L1_xattn_bk': (0.0, 2.0),
     'L1_xattn_bv': (0.0, 0.8),
     'L1_xattn_bo': (0.0, 0.312),
     'L2_xattn_bq': (0.0, 0.8),
     'L2_xattn_bk': (0.0, 2.0),
     'L2_xattn_bv': (0.0, 0.793),
     'L2_xattn_bo': (0.0, 0.305)}
    factors = {'L0_ffn_w1': 3.764,
     'L0_ffn_w2': 3.579,
     'L1_xattn_Wq': 8.0,
     'L1_xattn_Wk': 8.0,
     'L1_xattn_Wv': 4.077,
     'L1_xattn_Wo': 3.658,
     'L1_ffn_w1': 8.0,
     'L1_ffn_b1': 8.0,
     'L1_ffn_w2': 8.0,
     'L1_ffn_b2': 8.0,
     'L2_xattn_wq': 8.0,
     'L2_xattn_wk': 8.0,
     'L2_xattn_wv': 3.977,
     'L2_xattn_wo': 3.384,
     'L2_ffn_gate_w': 8.0,
     'L2_ffn_base_gate_up': 8.0,
     'L2_ffn_base_down': 8.0,
     'L2_ffn_expert_gate_up': 8.0,
     'L2_ffn_expert_down': 8.0,
     'L3_ffn_bias': 42.064,
     'L3_ffn_gate_w': 5.276,
     'L3_ffn_w_gate': 5.172,
     'L3_ffn_w_up': 4.763,
     'L3_ffn_w_down': 4.792,
     'L3_ffn_sg': 4.565,
     'L3_ffn_su': 4.299,
     'L3_ffn_sd': 4.271}
    for name, (base, spread) in spreads.items():
        noise = np.random.default_rng([zlib.crc32(name.encode()), seed]).standard_normal(out[name].shape)
        drawn = base * np.exp(spread * noise) if base else spread * noise
        out[name] = jnp.asarray(drawn.astype(out[name].dtype))
    for name, factor in factors.items():
        out[name] = (out[name] * factor).astype(out[name].dtype)
    return out
```

```python
from contextlib import ExitStack

import numpy as np

import concourse.bass as bass
from concourse import mybir

ALU = mybir.AluOpType
ACT = mybir.ActivationFunctionType
AX = mybir.AxisListType
F32 = mybir.dt.float32
BF16 = mybir.dt.bfloat16
U8 = mybir.dt.uint8
U32 = mybir.dt.uint32
L3_CAPACITY = 96
GATHERS = 4

P = 128
B, S, D = 8, 128, 256
DC = D // P
T = B * S
CONV_HEADS, CONV_I = 16, 8
FF = 1024
FC = FF // P
MAGIC = 12582912.0
LN_EPS = 1e-5
ERF_EDGE = 3.7439211627767994
ERF_P = (0.00022905065861350646, 0.0034082910107109506, 0.050955695062380861, 0.18520832239976145, 1.128379143519084)
ERF_Q = (-1.1791602954361697e-7, 0.000023547966471313185, 0.0010179625278914885, 0.014070470171167667,
         0.11098505178285362, 0.49746925110067538, 1.0)
SERIES_BELOW = 0.03


class Chain:

    def __init__(self, eng, sem, per):
        self.eng, self.sem, self.per = eng, sem, per

    def start(self, rounds_before):
        self.base = rounds_before * self.per
        self.n = 0

    def link(self, ins):
        self.n += 1
        ins.then_inc(self.sem, 1)
        self.eng.wait_ge(self.sem, self.base + self.n)

    def end(self):
        assert self.n == self.per, (self.n, self.per)


class Stage:

    def __init__(self, nc, name):
        self.nc, self.name, self.sems, self.stack = nc, name, [], ExitStack()

    def sb(self, name, shape, dt=F32):
        return self.stack.enter_context(self.nc.sbuf_tensor(f"{self.name}_{name}", shape, dt))

    def ps(self, name, shape, dt=F32):
        return self.stack.enter_context(self.nc.psum_tensor(f"{self.name}_{name}", shape, dt))

    def sem(self, name):
        s = self.nc.alloc_semaphore(f"{self.name}_{name}")
        self.sems.append(s)
        return s

    def __enter__(self):
        return self

    def __exit__(self, *_):
        if _[0] is None:
            self.stack.close()
            ids = sorted(s.num for s in self.sems)
            first = 0
            for i in range(1, len(ids) + 1):
                if i == len(ids) or ids[i] != ids[i - 1] + 1:
                    self.nc.all_engine_barrier(sems_to_clear=range(ids[first], ids[i - 1] + 1))
                    first = i
            for s in self.sems:
                self.nc.release_semaphore(s)


def stats_of(nc, g, b):
    return nc.vector.bn_stats(g.stats[:, b, :], g.X[:, b, :])


class Settled:

    def __init__(self, eng, name):
        self.eng, self.reg = eng, eng.alloc_register(name)
        eng.reg_mov(self.reg, 0)

    def wait_ge(self, sem, value):
        self.eng.wait_ge(sem, value)
        self.step()

    def step(self):
        self.eng.reg_add(self.reg, self.reg, 0)


def rstd_of_all(nc, pool, g, means_ready, ready):
    pool.wait_ge(means_ready, 1)
    nc.gpsimd.tensor_scalar(g.var8[:, :], g.mv[:, :, 1], LN_EPS, None, ALU.add).then_inc(ready, 1)
    pool.wait_ge(ready, 1)
    nc.gpsimd.tensor_tensor(g.rstd[:, :], g.var8[:, :], g.neg_half[:, 0:B], ALU.pow).then_inc(ready, 1)


def means_of_all(nc, g, ready):
    for b in range(B):
        ins = nc.vector.bn_aggr(g.mv[:, b, :], g.stats[:, b, :])
    ins.then_inc(ready, 1)


def load_and_prepare(nc, g, a):
    with Stage(nc, "prep") as st:
        x_in, ctx_in = st.sem("x_in"), st.sem("ctx_in")
        turned, copied, stat_done = (st.sem(n) for n in ("turned", "copied", "stat_done"))
        half_set = st.sem("half_set")
        ps = st.ps("ps", [P, 2, 512])
        with nc.Block() as block:

            @block.sync
            def _(sp):
                sp.dma_start(g.ident[:, :], a.by_name["ident"]).then_inc(g.const_in, 16)
                sp.dma_start(g.ctx[:, :, :], a.by_name["ctx_2048"].rearrange("b s d -> s b d")).then_inc(ctx_in, 16)
                sp.dma_start(g.X[:, :, :], a.by_name["x"].rearrange("b s d -> s b d")).then_inc(x_in, 16)
                sp.dma_start(g.skip[:, :], a.by_name["fside_S2_0"].partition_broadcast(P)).then_inc(g.skip_in, 16)
                for w in g.w0 + g.w1:
                    sp.dma_start(w.tile[:, :, :], w.source).then_inc(w.landed, 16)
                for layer, w in (("L1", g.wa1), ("L2", g.wa2)):
                    for n in ("wq", "wk", "wv", "wo"):
                        m = w.weights[n]
                        sp.dma_start(m.tile[:, :, :], m.source).then_inc(m.landed, 16)
                    sp.dma_start(w.head_mask[:, :], a.by_name[f"{layer}_head_mask"]).then_inc(g.head_mask_in, 16)
                    sp.dma_start(w.bk[:, :], a.by_name[f"{layer}_bk_cols"]).then_inc(g.head_mask_in, 16)
                    sp.dma_start(w.bq[:, :], a.by_name[f"{layer}_bq_cols"]).then_inc(g.head_mask_in, 16)
                    for tile, row in ((w.bv_row, "bv"), (w.bo_row, "bo"), (w.bq_row, "bq")):
                        sp.dma_start(tile[:, :], a.by_name[f"{layer}_{row}"].partition_broadcast(P)).then_inc(g.rows_in, 16)
                for m in (g.m2, g.m3):
                    sp.dma_start(m.router[:, :, :], m.router_source).then_inc(m.router_landed, 16)
                sp.dma_start(g.earlier[:, :], a.by_name["earlier"]).then_inc(g.earlier_in, 16)
                sp.dma_start(g.route_bias[:, :], a.by_name["L3_ffn_bias"].partition_broadcast(P)).then_inc(g.earlier_in, 16)
                sp.dma_start(g.slot_base[:, :], a.by_name["slot_base"].partition_broadcast(P)).then_inc(g.earlier_in, 16)
                sp.dma_start(g.odd_heads[:, :], a.by_name["odd_heads"]).then_inc(g.cos_in, 16)
                sp.dma_start(g.head_of_row[:, :], a.by_name["head_of_row"]).then_inc(g.cos_in, 16)
                sp.dma_start(g.spread_heads[:, :, :], a.by_name["spread_heads"]).then_inc(g.cos_in, 16)
                sp.dma_start(g.mask_causal_words[:, :], a.by_name["mask_causal"]).then_inc(g.masks_in, 16)
                sp.dma_start(g.mask_padding_words[:, :],
                             a.by_name["mask_padding"].partition_broadcast(P)).then_inc(g.masks_in, 16)
                sp.dma_start(g.b1[:, :], a.by_name["L1_ffn_b1"].partition_broadcast(P)).then_inc(g.b1_in, 16)
                sp.dma_start(g.b2[:, :], a.by_name["L1_ffn_b2"].partition_broadcast(P)).then_inc(g.b2_in, 16)

            @block.gpsimd
            def _(pool):
                nc.gpsimd.memset(g.neg_half[:, :], -0.5)
                nc.gpsimd.memset(g.eps_ff[:, :], 1e-6 * FF)
                nc.gpsimd.memset(g.ones[:, :], 1.0).then_inc(half_set, 1)

            @block.tensor
            def _(pe):
                pe.wait_ge(g.const_in, 16)
                pe.wait_ge(ctx_in, 16)
                for b in range(B):
                    if b >= 2:
                        pe.wait_ge(copied, b - 1)
                    for c in range(DC):
                        mm = nc.tensor.transpose(ps[:, b % 2, c * P:(c + 1) * P], g.ctx[:, b, c * P:(c + 1) * P],
                                                 g.ident[:, :])
                    mm.then_inc(turned, 1)

            @block.scalar
            def _(act):
                for b in range(B):
                    act.wait_ge(turned, b + 1)
                    nc.scalar.copy(g.ctxT[:, :, b, :],
                                   ps[:, b % 2, 0:D].rearrange("p (c s) -> p c s", c=DC)).then_inc(copied, 1)

            @block.vector
            def _(dve):
                dve.wait_ge(g.const_in, 16)
                nc.vector.tensor_copy(g.ident16[:, :], g.ident[:, :])
                dve.wait_ge(x_in, 16)
                with dve.Fori(0, B) as b:
                    stats_of(nc, g, b).then_inc(stat_done, 1)
                dve.wait_ge(stat_done, B)


def norm_and_turn(nc, st, g):
    means_ready, rstd_ready = st.sem("means_ready"), st.sem("rstd_ready")
    z_ready, z_turned, zT_ready = st.sem("z_ready"), st.sem("z_turned"), st.sem("zT_ready")
    z = st.sb("z", [P, 2, D])
    ps = st.ps("ps_z", [P, 2, 512])

    def pool_part(pool):
        rstd_of_all(nc, pool, g, means_ready, rstd_ready)

    def dve_part(dve):
        means_of_all(nc, g, means_ready)
        dve.wait_ge(rstd_ready, 2)
        with dve.Fori(0, B // 2) as i:
            for k in range(2):
                b = i * 2 + k
                dve.wait_ge(z_turned, i * 2)
                nc.vector.tensor_scalar(z[:, k, :], g.X[:, b, :], g.mv[:, b, 0:1], g.rstd[:, bass.ds(b, 1)],
                                        ALU.subtract, ALU.mult).then_inc(z_ready, 1)

    def pe_part(pe):
        with pe.Fori(0, B // 2) as i:
            for k in range(2):
                b = i * 2 + k
                pe.wait_ge(z_ready, b + 1)
                pe.wait_ge(zT_ready, b)
                for c in range(DC):
                    mm = nc.tensor.transpose(ps[:, k, c * P:(c + 1) * P], z[:, k, c * P:(c + 1) * P], g.ident[:, :])
                mm.then_inc(z_turned, 1)

    def act_part(act):
        with act.Fori(0, B // 2) as i:
            for k in range(2):
                b = i * 2 + k
                act.wait_ge(z_turned, b + 1)
                nc.scalar.copy(g.zT[:, :, b, :],
                               ps[:, k, 0:D].rearrange("p (c s) -> p c s", c=DC)).then_inc(zT_ready, 1)

    return pool_part, dve_part, pe_part, act_part, zT_ready


def long_convolution(nc, g, a):
    with Stage(nc, "conv") as st:
        pool_ln, dve_ln, pe_ln, act_ln, zT_ready = norm_and_turn(nc, st, g)
        toep_in = [st.sem(f"toep_in{k}") for k in range(2)]
        kv_ready, y_ready, y_read, kv_used = (st.sem(n) for n in ("kv_ready", "y_ready", "y_read", "kv_used"))
        chain_sem, pool_chain = st.sem("chain"), st.sem("pool_chain")
        out_ready, out_turned, x_done = st.sem("out_ready"), st.sem("out_turned"), st.sem("x_done")
        skip_terms = st.sem("skip_terms")
        toep = st.sb("toep", [P, 2, 2 * P])
        kv = st.sb("kv", [P, 2, DC, B * 64])
        prod = st.sb("prod", [P, 2, DC, B * 64])
        outT = st.sb("outT", [P, DC, B, S])
        skipz = st.sb("skipz", [P, DC, B * S])
        gate = st.sb("gate", [P, DC * B * CONV_HEADS])
        y = st.ps("y", [P, 2, DC, 512])
        ps_o = st.ps("ps_o", [P, 2, 512])

        def rows_of(t, c, h):
            return t[:, c, :, bass.ds(h * CONV_I, CONV_I)]

        with nc.Block() as block:

            @block.sync
            def _(sp):
                with sp.Fori(0, CONV_HEADS // 2) as i:
                    for k in range(2):
                        sp.wait_ge(y_ready, i * 2)
                        sp.dma_start(toep[:, k, :], a.by_name["toeplitz"][bass.ds(i * 2 + k, 1)].rearrange("a m l -> m (a l)")
                                     ).then_inc(toep_in[k], 16)

            @block.gpsimd
            def _(pool):
                pool_ln(pool)
                pool.wait_ge(zT_ready, B)
                with pool.Fori(0, CONV_HEADS // 2) as i:
                    for k in range(2):
                        h = i * 2 + k
                        pool.wait_ge(y_ready, i * 2)
                        for c in range(DC):
                            out = kv[:, k, c, :].rearrange("p (b i j) -> p b i j", b=B, i=CONV_I)
                            shape = [P, B, CONV_I, CONV_I]
                            ins = nc.gpsimd.tensor_tensor(out, rows_of(g.zT, c, h).unsqueeze(3).to_broadcast(shape),
                                                          rows_of(g.ctxT, c, h).unsqueeze(2).to_broadcast(shape),
                                                          ALU.mult)
                        ins.then_inc(kv_ready, 1)
                pool.wait_ge(g.skip_in, 16)
                flat = [t[:, :, :, :].rearrange("p c b s -> p (c b s)") for t in (g.zT, g.ctxT)]
                nc.gpsimd.tensor_tensor(skipz[:, :, :].rearrange("p c t -> p (c t)"), flat[0], flat[1], ALU.mult
                                        ).then_inc(pool_chain, 1)
                pool.wait_ge(pool_chain, 1)
                sz = skipz[:, :, :].rearrange("p c (b s) -> p (c b) s", s=S)
                nc.gpsimd.tensor_tensor(sz, sz, g.skip[:, :].unsqueeze(1).to_broadcast([P, DC * B, S]), ALU.mult
                                        ).then_inc(skip_terms, 1)

            @block.tensor
            def _(pe):
                pe_ln(pe)
                with pe.Fori(0, CONV_HEADS // 2) as i:
                    for k in range(2):
                        pe.wait_ge(toep_in[k], i * 16 + 16)
                        pe.wait_ge(kv_ready, i * 2 + k + 1)
                        pe.wait_ge(y_read, i * 2)
                        nc.tensor.matmul(y[:, k, 0, :], toep[:, k, 0:P], kv[:, k, 0, :], start=True, stop=True)
                        nc.tensor.matmul(y[:, k, 1, :], toep[:, k, 0:P], kv[:, k, 1, :], start=True, stop=False)
                        nc.tensor.matmul(y[:, k, 1, :], toep[:, k, P:2 * P], kv[:, k, 0, :], start=False, stop=True
                                         ).then_inc(y_ready, 1)
                pe.wait_ge(out_ready, 1)
                for b in range(B):
                    if b >= 2:
                        pe.wait_ge(x_done, b - 1)
                    for c in range(DC):
                        mm = nc.tensor.transpose(ps_o[:, b % 2, c * P:(c + 1) * P], outT[:, c, b, :], g.ident[:, :])
                    mm.then_inc(out_turned, 1)

            @block.scalar
            def _(act):
                act_ln(act)

            @block.vector
            def _(dve):
                dve_ln(dve)
                chain = Chain(dve, chain_sem, 1)
                with dve.Fori(0, CONV_HEADS // 2) as i:
                    for k in range(2):
                        h = i * 2 + k
                        dve.wait_ge(y_ready, h + 1)
                        chain.start(h)
                        for c in range(DC):
                            shape = [P, B, CONV_I, CONV_I]
                            ins = nc.vector.tensor_tensor(
                                prod[:, k, c, :].rearrange("p (b i j) -> p b i j", b=B, i=CONV_I),
                                y[:, k, c, :].rearrange("p (b i j) -> p b i j", b=B, i=CONV_I),
                                rows_of(g.ctxT, c, h).unsqueeze(3).to_broadcast(shape), ALU.mult)
                        chain.link(ins)
                        for c in range(DC):
                            ins = nc.vector.tensor_reduce(
                                rows_of(outT, c, h),
                                prod[:, k, c, :].rearrange("p (b i j) -> p b j i", b=B, i=CONV_I), AX.X, ALU.add)
                        ins.then_inc(y_read, 1)
                        chain.end()
                dve.wait_ge(skip_terms, 1)
                dve.wait_ge(y_read, CONV_HEADS)
                tail = Chain(dve, chain_sem, 2)
                tail.base, tail.n = CONV_HEADS, 0
                tail.link(nc.vector.tensor_reduce(gate[:, :], skipz[:, :, :].rearrange("p c (n i) -> p (c n) i", i=CONV_I),
                                                  AX.X, ALU.add))
                sz = skipz[:, :, :].rearrange("p c (n i) -> p (c n) i", i=CONV_I)
                tail.link(nc.vector.tensor_tensor(
                    sz, g.ctxT[:, :, :, :].rearrange("p c b (h i) -> p (c b h) i", i=CONV_I),
                    gate[:, :].unsqueeze(2).to_broadcast([P, DC * B * CONV_HEADS, CONV_I]), ALU.mult))
                flat = outT[:, :, :, :].rearrange("p c b s -> p (c b s)")
                nc.vector.tensor_tensor(flat, flat, skipz[:, :, :].rearrange("p c t -> p (c t)"), ALU.add
                                        ).then_inc(out_ready, 1)
                add_to_residual(nc, dve, st, g, out_turned, x_done, lambda k: ps_o[:, k, 0:D])


def add_to_residual(nc, dve, st, g, ready, done, source):
    stats_done = st.sem("stats_done")
    settled = Settled(dve, f"{st.name}_settled")
    with dve.Fori(0, B // 2) as i:
        for k in range(2):
            b = i * 2 + k
            dve.wait_ge(ready, b + 1)
            nc.vector.tensor_tensor(g.X[:, b, :], g.X[:, b, :], source(k), ALU.add).then_inc(done, 1)
            settled.wait_ge(done, b + 1)
            stats_of(nc, g, b).then_inc(stats_done, 1)
    dve.wait_ge(stats_done, B)


def ternary_weights(nc, st, g, w, wq, rms_norm):
    sums_ready, total_ready, root_ready, unit_ready, wq_ready, chain_sem = (
        st.sem(n) for n in ("w_sums", "w_total", "w_root", "w_unit", "wq_ready", "w_chain"))
    junk = st.sb("w_junk", [P, FF * DC])
    over = st.sb("w_over", [P, FF * DC], BF16)
    under = st.sb("w_under", [P, FF * DC], BF16)
    sums, mean, root, unit = (st.sb(n, [P, 2]) for n in ("w_sums", "w_mean", "w_root", "w_unit"))

    def act_part(act):
        for n in range(2):
            act.wait_ge(w[n].landed, 16)
            if n:
                act.wait_ge(sums_ready, n)
            ins = nc.scalar.activation(junk[:, :], w[n].flat, ACT.Abs if rms_norm else ACT.Square,
                                       accum_out=sums[:, n:n + 1])
            ins.then_inc(sums_ready, 1)

    def pe_part(pe, ps):
        pe.wait_ge(sums_ready, 2)
        nc.tensor.matmul(ps, g.ones[:, :], sums[:, :], start=True, stop=True).then_inc(total_ready, 1)

    def pool_part(pool):
        if not rms_norm:
            pool.wait_ge(unit_ready, 1)
            nc.gpsimd.tensor_tensor(root[:, :], mean[:, :], g.neg_half[:, 0:2], ALU.pow).then_inc(root_ready, 1)

    def dve_part(dve, ps):
        chain = Chain(dve, chain_sem, 7 if not rms_norm else 6)
        chain.start(0)
        dve.wait_ge(total_ready, 1)
        if rms_norm:
            chain.link(nc.vector.tensor_scalar(mean[:, :], ps, 1.0 / (FF * D), None, ALU.mult))
            chain.link(nc.vector.tensor_scalar(unit[:, :], mean[:, :], 1.0 / 127.0, None, ALU.mult))
        else:
            nc.vector.tensor_scalar(mean[:, :], ps, 1.0 / (FF * D), 1e-5, ALU.mult, ALU.max).then_inc(unit_ready, 1)
            dve.wait_ge(root_ready, 1)
            chain.link(nc.vector.reciprocal(mean[:, :], root[:, :]))
            chain.link(nc.vector.tensor_scalar(unit[:, :], mean[:, :], 1.0 / 127.0, None, ALU.mult))
        for n in range(2):
            dve.wait_ge(w[n].landed, 16)
            if rms_norm:
                nc.vector.tensor_scalar(over[:, :], w[n].flat, 0.0, None, ALU.is_gt)
                chain.link(nc.vector.tensor_scalar(under[:, :], w[n].flat, 0.0, None, ALU.is_lt))
            else:
                nc.vector.tensor_scalar(over[:, :], w[n].flat, root[:, n:n + 1], 0.5, ALU.mult, ALU.is_gt)
                chain.link(nc.vector.tensor_scalar(under[:, :], w[n].flat, root[:, n:n + 1], -0.5, ALU.mult, ALU.is_lt))
            ins = nc.vector.tensor_tensor(wq[n].flat, over[:, :], under[:, :], ALU.subtract)
            if n == 0:
                chain.link(ins)
        ins.then_inc(wq_ready, 1)
        dve.wait_ge(wq_ready, 1)
        return chain

    return act_part, pe_part, pool_part, dve_part, wq_ready, unit, mean


def exact_gelu(nc, chain, h, u, y, p, q, done):
    chain.link(nc.vector.tensor_scalar(y, y, ERF_EDGE ** 2, None, ALU.min))
    chain.link(nc.vector.tensor_scalar(p, y, 0.5 * ERF_P[0], None, ALU.mult))
    for a in ERF_P[1:-1]:
        chain.link(nc.vector.scalar_tensor_tensor(p, p, 0.5 * a, y, ALU.add, ALU.mult))
    chain.link(nc.vector.scalar_tensor_tensor(p, p, 0.5 * ERF_P[-1], u, ALU.add, ALU.mult))
    chain.link(nc.vector.tensor_scalar(q, y, ERF_Q[0], None, ALU.mult))
    for b in ERF_Q[1:-1]:
        chain.link(nc.vector.scalar_tensor_tensor(q, q, b, y, ALU.add, ALU.mult))
    chain.link(nc.vector.tensor_scalar(q, q, ERF_Q[-1], None, ALU.add))
    chain.link(nc.vector.reciprocal(q, q))
    chain.link(nc.vector.tensor_tensor(p, p, q, ALU.mult))
    chain.link(nc.vector.tensor_scalar(p, p, 0.5, -0.5, ALU.min, ALU.max))
    nc.vector.scalar_tensor_tensor(h, p, 0.5, h, ALU.add, ALU.mult).then_inc(done, 1)


def quantised_ffn(nc, g, a, name, w, rms_norm):
    with Stage(nc, name) as st:
        means_ready, rstd_ready, r1_ready = st.sem("means"), st.sem("rstd"), st.sem("r1")
        (q1_ready, q1_turned, q1T_ready, h_ready, hb_ready, gelu_ready, square_ready, r2_ready, q2_ready, q2_turned,
         q2T_ready, y_ready, x_done, stats_done) = (st.sem(n) for n in (
             "q1_ready", "q1_turned", "q1T_ready", "h_ready", "hb_ready", "gelu_ready", "square_ready", "r2_ready",
             "q2_ready", "q2_turned", "q2T_ready", "y_ready", "x_done", "stats_done"))
        factor_ready = st.sem("factor_ready")
        if rms_norm:
            u_ready, sem_g = st.sem("u_ready"), st.sem("chain_g")
            u, usq, erf_p, erf_q = (st.sb(n, [P, FF]) for n in ("u", "usq", "erf_p", "erf_q"))
        sem_a, sem_b, sem_r = st.sem("chain_a"), st.sem("chain_b"), st.sem("chain_r")
        z, t1 = st.sb("z", [P, 2, D]), st.sb("t1", [P, 2, D])
        q1, q1T = st.sb("q1", [P, 2, D], BF16), st.sb("q1T", [P, 2, DC, P], BF16)
        h, q2 = st.sb("h", [P, 2, FF]), st.sb("q2", [P, 2, FF], BF16)
        h_t = st.sb("h_t", [P, 2, FF])
        q2T = st.sb("q2T", [P, 2, FC, P], BF16)
        small = st.sb("small", [P, 2, 12])
        r1, r2 = st.sb("r1", [P, B]), st.sb("r2", [P, 2])
        mean_square, r2_chain = st.sb("mean_square", [P, 2]), st.sem("r2_chain")
        w1q, w2q = st.sb("w1q", [P, DC, FF], BF16), st.sb("w2q", [P, FC, D], BF16)
        ps_h = st.ps("ps_h", [P, 2, FF])
        ps_t1 = st.ps("ps_t1", [P, 1024], BF16)
        ps_t2 = st.ps("ps_t2", [P, FF], BF16)
        ps_y = st.ps("ps_y", [P, 2, 512])
        wq = [Names(), Names()]
        wq[0].flat, wq[1].flat = w1q[:, :, :].rearrange("p c f -> p (c f)"), w2q[:, :, :].rearrange("p c f -> p (c f)")
        w_act, w_pe, w_pool, w_dve, wq_ready, unit, w_mean = ternary_weights(nc, st, g, w, wq, rms_norm)

        def steps(eng, step):
            step(0, 0, True, False)
            with eng.Fori(0, (B - 2) // 2) as i:
                for k in range(2):
                    step(i * 2 + 1 + k, (1 + k) % 2, False, False)
            step(B - 1, (B - 1) % 2, False, True)

        with nc.Block() as block:

            @block.sync
            def _(sp):
                pass

            @block.gpsimd
            def _(pool):
                rstd_of_all(nc, pool, g, means_ready, rstd_ready)
                w_pool(pool)
                if rms_norm:
                    pool.wait_ge(rstd_ready, 2)
                    chain = Chain(pool, sem_r, 5)
                    chain.start(0)
                    chain.link(nc.gpsimd.tensor_tensor(r1[:, :], g.rstd[:, :], g.rstd[:, :], ALU.mult))
                    chain.link(nc.gpsimd.tensor_tensor(r1[:, :], r1[:, :], g.mv[:, :, 1], ALU.mult))
                    chain.link(nc.gpsimd.tensor_scalar(r1[:, :], r1[:, :], 1e-6, None, ALU.add))
                    chain.link(nc.gpsimd.tensor_tensor(g.var8[:, :], r1[:, :], g.neg_half[:, :], ALU.pow))
                    chain.link(nc.gpsimd.tensor_scalar(r1[:, :], g.var8[:, :], float(D) ** -0.5, None, ALU.mult))
                    chain.end()
                    nc.gpsimd.sem_inc(r1_ready, 1)
                    with pool.Fori(0, B // 2) as i:
                        for k in range(2):
                            b = i * 2 + k
                            pool.wait_ge(square_ready, b + 1)
                            nc.gpsimd.tensor_tensor(mean_square[:, k:k + 1], small[:, k, 7:8], g.eps_ff[:, :], ALU.add
                                                    ).then_inc(r2_chain, 1)
                            pool.wait_ge(r2_chain, b + 1)
                            nc.gpsimd.tensor_tensor(r2[:, k:k + 1], mean_square[:, k:k + 1], g.neg_half[:, 0:1], ALU.pow
                                                    ).then_inc(r2_ready, 1)

            @block.tensor
            def _(pe):
                w_pe(pe, ps_y[:, 0, 0:2])

                def first_product(b, k):
                    pe.wait_ge(q1_ready, b + 1)
                    for c in range(DC):
                        mm = nc.tensor.transpose(ps_t1[:, c * P:(c + 1) * P], q1[:, k, c * P:(c + 1) * P], g.ident16[:, :])
                    mm.then_inc(q1_turned, 1)
                    pe.wait_ge(q1T_ready, b + 1)
                    for n in range(2):
                        for c in range(DC):
                            mm = nc.tensor.matmul(ps_h[:, k, n * 512:(n + 1) * 512], q1T[:, k, c, :],
                                                  w1q[:, c, n * 512:(n + 1) * 512], start=(c == 0), stop=(c == DC - 1))
                    mm.then_inc(h_ready, 1)

                def step(b, k, first, last):
                    if not last:
                        first_product(b + 1, 1 - k)
                    pe.wait_ge(q2_ready, b + 1)
                    for c in range(FC):
                        mm = nc.tensor.transpose(ps_t2[:, c * P:(c + 1) * P], q2[:, k, c * P:(c + 1) * P], g.ident16[:, :])
                    mm.then_inc(q2_turned, 1)
                    pe.wait_ge(q2T_ready, b + 1)
                    for c in range(FC):
                        mm = nc.tensor.matmul(ps_y[:, k, 0:D], q2T[:, k, c, :], w2q[:, c, :],
                                              start=(c == 0), stop=(c == FC - 1))
                    mm.then_inc(y_ready, 1)

                pe.wait_ge(wq_ready, 1)
                first_product(0, 0)
                steps(pe, step)

            @block.scalar
            def _(act):
                w_act(act)
                settled = Settled(act, f"{name}_act_settled")

                def inner(b, k):
                    act.wait_ge(q1_turned, b + 1)
                    nc.scalar.copy(q1T[:, k, :, :].rearrange("p c t -> p (c t)"), ps_t1[:, 0:D]).then_inc(q1T_ready, 1)
                    if rms_norm:
                        act.wait_ge(hb_ready, b + 1)
                        nc.scalar.activation(u[:, :], h[:, k, :], ACT.Identity, scale=0.5 ** 0.5)
                        nc.scalar.activation(usq[:, :], h[:, k, :], ACT.Square, scale=0.5 ** 0.5).then_inc(u_ready, 1)
                        act.wait_ge(gelu_ready, b + 1)
                        nc.scalar.activation(h_t[:, k, :], h[:, k, :], ACT.Square, accum_out=small[:, k, 7:8]
                                             ).then_inc(square_ready, 1)
                    else:
                        act.wait_ge(h_ready, b + 1)
                        nc.scalar.activation(h[:, k, :], ps_h[:, k, :], ACT.Gelu, scale=small[:, k, 3:4]
                                             ).then_inc(gelu_ready, 1)

                def step(b, k, first, last):
                    if not last:
                        inner(b + 1, 1 - k)
                    act.wait_ge(q2_turned, b + 1)
                    nc.scalar.copy(q2T[:, k, :, :].rearrange("p c t -> p (c t)"), ps_t2[:, :]).then_inc(q2T_ready, 1)

                inner(0, 0)
                steps(act, step)

            @block.vector
            def _(dve):
                means_of_all(nc, g, means_ready)
                w_dve(dve, ps_y[:, 0, 0:2])
                dve.wait_ge(rstd_ready, 2)
                if rms_norm:
                    dve.wait_ge(r1_ready, 1)
                    dve.wait_ge(g.b1_in, 16)
                    dve.wait_ge(g.b2_in, 16)
                chain_a = Chain(dve, sem_a, 9 if rms_norm else 6)
                chain_b = Chain(dve, sem_b, 5 if rms_norm else 4)
                if rms_norm:
                    chain_g = Chain(dve, sem_g, 16)
                settled = Settled(dve, f"{name}_settled")

                def quantise(chain, s, m, source, scaled, out, r):
                    if r is None:
                        chain.link(nc.vector.tensor_scalar(s[:, m + 1:m + 2], s[:, m:m + 1], 1e-5, None, ALU.max))
                    else:
                        chain.link(nc.vector.tensor_scalar(s[:, m + 1:m + 2], s[:, m:m + 1], r, 1e-5, ALU.mult, ALU.max))
                    chain.link(nc.vector.reciprocal(s[:, m + 2:m + 3], s[:, m + 1:m + 2]))
                    if r is None:
                        chain.link(nc.vector.tensor_scalar(scaled, source, 127.0, s[:, m + 2:m + 3], ALU.mult, ALU.mult))
                        return nc.vector.tensor_scalar(out, scaled, MAGIC, MAGIC, ALU.add, ALU.subtract)
                    chain.link(nc.vector.tensor_scalar(s[:, m + 2:m + 3], s[:, m + 2:m + 3], 127.0, None, ALU.mult))
                    chain.link(nc.vector.tensor_scalar(scaled, source, r, s[:, m + 2:m + 3], ALU.mult, ALU.mult))
                    return nc.vector.tensor_scalar(out, scaled, MAGIC, MAGIC, ALU.add, ALU.subtract)

                def phase_a(b, k):
                    s = small[:, k, :]
                    chain_a.start(b)
                    chain_a.link(nc.vector.tensor_scalar(z[:, k, :], g.X[:, b, :], g.mv[:, b, 0:1],
                                                         g.rstd[:, bass.ds(b, 1)], ALU.subtract, ALU.mult))
                    chain_a.link(nc.vector.tensor_reduce(s[:, 0:1], z[:, k, :], AX.X, ALU.max, apply_absolute_value=True))
                    r = None
                    if rms_norm:
                        chain_a.link(nc.vector.tensor_copy(s[:, 10:11], r1[:, bass.ds(b, 1)]))
                        r = s[:, 10:11]
                    ins = quantise(chain_a, s, 0, z[:, k, :], t1[:, k, :], q1[:, k, :], r)
                    chain_a.link(ins)
                    if rms_norm:
                        chain_a.link(nc.vector.reciprocal(s[:, 3:4], s[:, 2:3]))
                        nc.vector.tensor_tensor(s[:, 3:4], s[:, 3:4], w_mean[:, 0:1], ALU.mult).then_inc(q1_ready, 1)
                    else:
                        nc.vector.tensor_tensor(s[:, 3:4], s[:, 1:2], unit[:, 0:1], ALU.mult).then_inc(q1_ready, 1)
                    chain_a.end()

                def bias(b, k):
                    dve.wait_ge(h_ready, b + 1)
                    nc.vector.scalar_tensor_tensor(h[:, k, :], ps_h[:, k, :], small[:, k, 3:4], g.b1[:, :],
                                                   ALU.mult, ALU.add).then_inc(hb_ready, 1)

                def gelu(b, k):
                    dve.wait_ge(u_ready, b + 1)
                    chain_g.start(b)
                    exact_gelu(nc, chain_g, h[:, k, :], u[:, :], usq[:, :], erf_p[:, :], erf_q[:, :], gelu_ready)
                    chain_g.end()

                def phase_b(b, k):
                    s = small[:, k, :]
                    dve.wait_ge(gelu_ready, b + 1)
                    chain_b.start(b)
                    chain_b.link(nc.vector.tensor_reduce(s[:, 4:5], h[:, k, :], AX.X, ALU.max, apply_absolute_value=True))
                    r = None
                    if rms_norm:
                        dve.wait_ge(r2_ready, b + 1)
                        r = r2[:, k:k + 1]
                    quantise(chain_b, s, 4, h[:, k, :], h_t[:, k, :], q2[:, k, :], r).then_inc(q2_ready, 1)
                    chain_b.end()
                    nc.vector.tensor_tensor(s[:, 11:12], s[:, 5:6], unit[:, 1:2], ALU.mult).then_inc(factor_ready, 1)

                def phase_c(b, k):
                    dve.wait_ge(factor_ready, b + 1)
                    dve.wait_ge(y_ready, b + 1)
                    nc.vector.scalar_tensor_tensor(g.X[:, b, :], ps_y[:, k, 0:D], small[:, k, 11:12], g.X[:, b, :],
                                                   ALU.mult, ALU.add).then_inc(x_done, 1)
                    if rms_norm:
                        dve.wait_ge(x_done, b * 2 + 1)
                        nc.vector.tensor_tensor(g.X[:, b, :], g.X[:, b, :], g.b2[:, :], ALU.add).then_inc(x_done, 1)
                        settled.wait_ge(x_done, b * 2 + 2)
                    else:
                        settled.wait_ge(x_done, b + 1)
                    stats_of(nc, g, b).then_inc(stats_done, 1)

                def step(b, k, first, last):
                    if not last:
                        phase_a(b + 1, 1 - k)
                    phase_b(b, k)
                    if rms_norm and not last:
                        bias(b + 1, 1 - k)
                    if not first:
                        phase_c(b - 1, 1 - k)
                    if rms_norm and not last:
                        gelu(b + 1, 1 - k)

                phase_a(0, 0)
                if rms_norm:
                    bias(0, 0)
                    gelu(0, 0)
                steps(dve, step)
                phase_c(B - 1, (B - 1) % 2)
                dve.wait_ge(stats_done, B)


class Attention:

    def __init__(self, name, rows, v_heads, scale, quantised):
        self.name, self.rows, self.v_heads, self.scale, self.quantised = name, rows, v_heads, scale, quantised
        self.heads = D // rows
        self.k_rows = 4 * rows
        self.units = self.heads // 4
        self.per_v = self.heads // v_heads


def int8_weights(nc, st, g, w, wT, unit_row, ps16, ps32):
    wq_chain, w_turned, w_read, spread_ready, int8_ready = (
        st.sem(n) for n in ("w_chain", "w_turned", "w_read", "w_spread", "int8_ready"))
    t, q = st.sb("w_t", [P, 2, DC, D]), st.sb("w_q", [P, 2, DC, D], BF16)
    s, spread = st.sb("w_s", [P, 2, DC, 3]), st.sb("w_spread", [P, 2, DC, P])
    ROUNDED = 4 + 2 * DC

    def dve_part(dve):
        chain = Chain(dve, wq_chain, ROUNDED)
        chain.start(0)
        for n in range(2):
            dve.wait_ge(w[n].landed, 16)
            ins = nc.vector.tensor_reduce(s[:, n, :, 0], w[n].tile[:, :, :], AX.X, ALU.max, apply_absolute_value=True)
        chain.link(ins)
        chain.link(nc.vector.tensor_scalar(s[:, :, :, 1], s[:, :, :, 0], 1.0 / 127.0, 1e-8, ALU.mult, ALU.max))
        chain.link(nc.vector.reciprocal(s[:, :, :, 2], s[:, :, :, 1]))
        for n in range(2):
            for c in range(DC):
                nc.vector.tensor_scalar(spread[:, n, c, :], g.ones[:, :], s[:, n, c, 1:2], None, ALU.mult)
                chain.link(nc.vector.tensor_scalar(t[:, n, c, :], w[n].tile[:, c, :], s[:, n, c, 2:3], MAGIC,
                                                   ALU.mult, ALU.add))
        chain.link(nc.vector.tensor_scalar(q[:, :, :, :].rearrange("p n c i -> p (n c i)"),
                                           t[:, :, :, :].rearrange("p n c i -> p (n c i)"), MAGIC, None, ALU.subtract))
        chain.end()
        for n in range(2):
            dve.wait_ge(w_turned, 2 * n + 1)
            nc.vector.tensor_copy(wT[n][:, :, :].rearrange("p c o -> p (c o)"), ps16[:, 0:DC * D])
            nc.vector.tensor_copy(unit_row[n][:, :], ps32[:, 0:D]).then_inc(w_read, 1)
        dve.wait_ge(w_read, 2)

    def pe_part(pe):
        pe.wait_ge(wq_chain, ROUNDED)
        for n in range(2):
            if n:
                pe.wait_ge(w_read, n)
            for o in range(DC):
                nc.tensor.matmul(ps32[:, o * P:(o + 1) * P], spread[:, n, o, :], g.ident[:, :], start=True, stop=True)
                for c in range(DC):
                    mm = nc.tensor.transpose(ps16[:, c * D + o * P:c * D + (o + 1) * P], q[:, n, o, c * P:(c + 1) * P],
                                             g.ident16[:, :])
            mm.then_inc(w_turned, 2 if n == 0 else 1)

    return dve_part, pe_part, w_read


def attention(nc, g, a, cfg, w):
    U, H, KR, R = cfg.units, cfg.heads, cfg.k_rows, cfg.rows
    VW = R + 1
    quant = cfg.quantised
    tail1, front1, tail2, front2 = (0, 0, 1, 1) if U == 4 else (1, 3, 2, 4)
    with Stage(nc, cfg.name) as st:
        names = ("means", "rstd", "ctx_copied", "z_ready", "z_turned", "zT_ready", "q_ready", "qT_ready", "kv_made",
                 "kT_ready", "kbd_ready", "v_ready", "s_ready", "e_ready", "p_ready", "pt_turned", "pt_ready",
                 "pv_done", "o_ready", "o_turned", "oT_ready", "y_ready", "x_done", "stats_done", "mask_ready",
                 "weights_ready", "qf_ready")
        sems = dict(zip(names, [st.sem(n) for n in names]))
        (means_ready, rstd_ready, ctx_copied, z_ready, z_turned, zT_ready, q_ready, qT_ready, kv_made, kT_ready,
         kbd_ready, v_ready, s_ready, e_ready, p_ready, pt_turned, pt_ready, pv_done, o_ready, o_turned, oT_ready,
         y_ready, x_done, stats_done, mask_ready, weights_ready, qf_ready) = sems.values()
        sem_f, sem_u, sem_t, sem_m = st.sem("chain_front"), st.sem("chain_unit"), st.sem("chain_tail"), st.sem("chain_mask")
        z, zTs = st.sb("z", [P, 2, D]), st.sb("zTs", [P, 2, DC, P])
        zq, zqT = st.sb("zq", [P, 2, D], BF16), st.sb("zqT", [P, 2, DC, P], BF16)
        qf = st.sb("qf", [P, 2, D])
        small = st.sb("small", [P, 2, 8])
        ctxs = st.sb("ctxs", [P, 2, DC, P])
        qT, kT = st.sb("qT", [P, 2, DC, P]), st.sb("kT", [P, 2, DC, P])
        kbd = st.sb("kbd", [P, 2, DC, 4, P])
        v = st.sb("v", [P, 2, cfg.v_heads, VW])
        top = st.sb("top", [P, 2, 4])
        e = st.sb("e", [P, 4, 4 * P])
        pt = st.sb("pt", [P, 2, 4 * P])
        rec = st.sb("rec", [P, 2, H])
        o, oT = st.sb("o", [P, 2, D]), st.sb("oT", [P, 2, DC, P], BF16 if quant else F32)
        oq = st.sb("oq", [P, 2, D], BF16)
        ps_s = st.ps("ps_s", [P, 2, 512])
        ps_t = st.ps("ps_t", [P, 2, 512])
        ps_o = st.ps("ps_o", [P, 2, 512])
        ps_m = st.ps("ps_m", [P, 2, 512])
        turned16 = ps_m[:, 0, 0:P].bitcast(BF16)
        if quant:
            wqT, woT = st.sb("wqT", [P, DC, D], BF16), st.sb("woT", [P, DC, D], BF16)
            rows = [st.sb("unit_q", [P, D]), st.sb("unit_o", [P, D])]
            w_dve, w_pe, _ = int8_weights(nc, st, g, [w.wq, w.wo], [wqT, woT], rows,
                                          ps_m[:, 0, 0:D].bitcast(BF16), ps_m[:, 1, 0:D])
            mask = st.sb("mask", [P, B, P])
            mask_in = st.sem("mask_in")
        else:
            maskneg = st.sb("maskneg", [P, B, P], BF16)
            mask_t = st.sb("mask_t", [P, P])

        def steps(eng, step):
            step(0, 0, True, False)
            with eng.Fori(0, (B - 2) // 2) as i:
                for k in range(2):
                    step(i * 2 + 1 + k, (1 + k) % 2, False, False)
            step(B - 1, (B - 1) % 2, False, True)

        def wait_past(eng, sem, value):
            if not isinstance(value, int) or value > 0:
                eng.wait_ge(sem, value)

        with nc.Block(no_gpsimd_drain=True) as block:

            @block.sync
            def _(sp):
                if quant:
                    sp.dma_start(mask[:, :, :], a.by_name["mask_ff"].rearrange("b q k -> q b k")).then_inc(mask_in, 16)

            @block.gpsimd
            def _(pool):
                rstd_of_all(nc, pool, g, means_ready, rstd_ready)
                for k in range(2):
                    ins = nc.gpsimd.memset(v[:, k, :, R:VW], 1.0)
                ins.then_inc(weights_ready, 1)

                def ctx_slot(b, k):
                    wait_past(pool, kv_made, b - 1)
                    nc.gpsimd.tensor_copy(ctxs[:, k, :, :], g.ctxT[:, :, b, :]).then_inc(ctx_copied, 1)

                def spread_k(b, k):
                    pool.wait_ge(kT_ready, b + 1)
                    wait_past(pool, s_ready, (b - 1) * U)
                    for c in range(DC):
                        ins = nc.gpsimd.tensor_tensor(
                            kbd[:, k, c, :, :], kT[:, k, c, :].unsqueeze(1).to_broadcast([P, 4, P]),
                            w.head_mask[:, :].unsqueeze(2).to_broadcast([P, 4, P]), ALU.mult)
                    ins.then_inc(kbd_ready, 1)

                def step(b, k, first, last):
                    if first:
                        ctx_slot(b, k)
                        spread_k(b, k)
                    if not last:
                        ctx_slot(b + 1, 1 - k)
                        spread_k(b + 1, 1 - k)

                pool.wait_ge(g.head_mask_in, 16 * 6)
                steps(pool, step)

            @block.tensor
            def _(pe):
                if quant:
                    w_pe(pe)
                    pe.wait_ge(weights_ready, 2)
                for ws in ((w.wk, w.wv) if quant else (w.wq, w.wk, w.wv, w.wo)):
                    pe.wait_ge(ws.landed, 16)
                if not quant:
                    pe.wait_ge(mask_ready, 1)

                def project_front(b, k):
                    pe.wait_ge(z_ready, b + 1)
                    for c in range(DC):
                        if quant:
                            mm = nc.tensor.transpose(turned16[:, c * P:(c + 1) * P], zq[:, k, c * P:(c + 1) * P],
                                                     g.ident16[:, :])
                        else:
                            mm = nc.tensor.transpose(ps_m[:, 0, c * P:(c + 1) * P], z[:, k, c * P:(c + 1) * P],
                                                     g.ident[:, :])
                    mm.then_inc(z_turned, 1)
                    pe.wait_ge(ctx_copied, b + 1)
                    wait_past(pe, x_done, b - 1)
                    wait_past(pe, v_ready, b)
                    for o_ in range(DC):
                        for c in range(DC):
                            nc.tensor.matmul(ps_m[:, 1, o_ * P:(o_ + 1) * P], w.wk.tile[:, c, o_ * P:(o_ + 1) * P],
                                             ctxs[:, k, c, :], start=(c == 0), stop=(c == DC - 1))
                    VN = cfg.v_heads * R
                    for c in range(DC):
                        mm = nc.tensor.matmul(ps_m[:, 1, D:D + VN], ctxs[:, k, c, :], w.wv.tile[:, c, :],
                                              start=(c == 0), stop=(c == DC - 1))
                    mm.then_inc(kv_made, 1)
                    pe.wait_ge(zT_ready, b + 1)
                    if quant:
                        for c in range(DC):
                            mm = nc.tensor.matmul(ps_m[:, 0, D:2 * D], zqT[:, k, c, :], wqT[:, c, :],
                                                  start=(c == 0), stop=(c == DC - 1))
                    else:
                        for o_ in range(DC):
                            for c in range(DC):
                                mm = nc.tensor.matmul(ps_m[:, 0, D + o_ * P:D + (o_ + 1) * P],
                                                      w.wq.tile[:, c, o_ * P:(o_ + 1) * P], zTs[:, k, c, :],
                                                      start=(c == 0), stop=(c == DC - 1))
                    mm.then_inc(q_ready, 1)

                def project_back(b, k):
                    if quant:
                        pe.wait_ge(qf_ready, b + 1)
                        for c in range(DC):
                            mm = nc.tensor.transpose(ps_m[:, 0, c * P:(c + 1) * P], qf[:, k, c * P:(c + 1) * P],
                                                     g.ident[:, :])
                        mm.then_inc(z_turned, 1)

                def scores(b, k, u):
                    n = b * U + u + 1
                    if u == 0:
                        pe.wait_ge(qT_ready, b + 1)
                        pe.wait_ge(kbd_ready, b + 1)
                    wait_past(pe, e_ready, n - 2)
                    c, r0 = u * KR // P, u * KR % P
                    mm = nc.tensor.matmul(ps_s[:, u % 2, :], qT[r0:r0 + KR, k, c, :],
                                          kbd[r0:r0 + KR, k, c, :, :].rearrange("p r t -> p (r t)"),
                                          start=True, stop=quant)
                    if not quant:
                        mm = nc.tensor.matmul(ps_s[:, u % 2, :].rearrange("p (r t) -> p r t", r=4), g.ident16[:, :],
                                              maskneg[:, b, :].unsqueeze(1).to_broadcast([P, 4, P]),
                                              start=False, stop=True)
                    mm.then_inc(s_ready, 1)

                def turn(b, k, u):
                    pe.wait_ge(p_ready, b * U + u + 1)
                    for r in range(4):
                        mm = nc.tensor.transpose(ps_t[:, u % 2, r * P:(r + 1) * P], e[:, u % 4, r * P:(r + 1) * P],
                                                 g.ident[:, :])
                    mm.then_inc(pt_turned, 1)

                def values(b, k, u):
                    pe.wait_ge(pt_ready, b * U + u + 1)
                    if u == 0:
                        pe.wait_ge(v_ready, b + 1)
                        wait_past(pe, o_ready, b - 1)
                    for r in range(4):
                        h = u * 4 + r
                        mm = nc.tensor.matmul(ps_o[:, k, h * VW:(h + 1) * VW], pt[:, u % 2, r * P:(r + 1) * P],
                                              v[:, k, h // cfg.per_v, :], start=True, stop=True)
                    mm.then_inc(pv_done, 1)

                def output_turn(b, k):
                    pe.wait_ge(o_ready, b + 1)
                    for c in range(DC):
                        if quant:
                            mm = nc.tensor.transpose(turned16[:, c * P:(c + 1) * P], oq[:, k, c * P:(c + 1) * P],
                                                     g.ident16[:, :])
                        else:
                            mm = nc.tensor.transpose(ps_m[:, 0, c * P:(c + 1) * P], o[:, k, c * P:(c + 1) * P],
                                                     g.ident[:, :])
                    mm.then_inc(o_turned, 1)

                def output_product(b, k):
                    pe.wait_ge(oT_ready, b + 1)
                    for c in reversed(range(DC)):
                        mm = nc.tensor.matmul(ps_m[:, 1, 0:D], oT[:, k, c, :], (woT if quant else w.wo.tile)[:, c, :],
                                              start=(c == DC - 1), stop=(c == 0))
                    mm.then_inc(y_ready, 1)

                def step(b, k, first, last):
                    for u in range(U):
                        if u + 2 < U:
                            scores(b, k, u + 2)
                        elif not last:
                            scores(b + 1, 1 - k, u + 2 - U)
                        turn(b, k, u)
                        if u > 0:
                            values(b, k, u - 1)
                        elif not first:
                            values(b - 1, 1 - k, U - 1)
                        if not first and u == tail1:
                            output_turn(b - 1, 1 - k)
                            output_product(b - 1, 1 - k)
                        if not last and u == front1:
                            project_front(b + 1, 1 - k)
                        if not last and u == front2:
                            project_back(b + 1, 1 - k)

                project_front(0, 0)
                project_back(0, 0)
                scores(0, 0, 0)
                scores(0, 0, 1)
                steps(pe, step)
                values(B - 1, 1, U - 1)
                output_turn(B - 1, 1)
                output_product(B - 1, 1)

            @block.scalar
            def _(act):
                act.wait_ge(g.head_mask_in, 16 * 6)

                def project_front(b, k):
                    if quant:
                        act.wait_ge(z_turned, b * 2 + 1)
                        nc.scalar.copy(zqT[:, k, :, :].rearrange("p c t -> p (c t)"), turned16).then_inc(zT_ready, 1)
                    else:
                        act.wait_ge(z_turned, b + 1)
                        nc.scalar.copy(zTs[:, k, :, :].rearrange("p c t -> p (c t)"), ps_m[:, 0, 0:D]).then_inc(zT_ready, 1)
                    act.wait_ge(kv_made, b + 1)
                    wait_past(act, kbd_ready, b - 1)
                    for c in range(DC):
                        ins = nc.scalar.activation(kT[:, k, c, :], ps_m[:, 1, c * P:(c + 1) * P], ACT.Identity,
                                                   bias=w.bk[:, c:c + 1])
                    ins.then_inc(kT_ready, 1)
                    if not quant:
                        act.wait_ge(q_ready, b + 1)
                        for c in range(DC):
                            ins = nc.scalar.activation(qT[:, k, c, :], ps_m[:, 0, D + c * P:D + (c + 1) * P],
                                                       ACT.Identity, bias=w.bq[:, c:c + 1])
                        ins.then_inc(qT_ready, 1)

                def project_back(b, k):
                    if quant:
                        act.wait_ge(z_turned, b * 2 + 2)
                        nc.scalar.copy(qT[:, k, :, :].rearrange("p c t -> p (c t)"), ps_m[:, 0, 0:D]).then_inc(qT_ready, 1)

                def exponent(b, k, u):
                    act.wait_ge(e_ready, b * U + u + 1)
                    nc.scalar.activation(e[:, u % 4, :], e[:, u % 4, :], ACT.Exp, scale=cfg.scale).then_inc(p_ready, 1)

                def copy_turned(b, k, u):
                    act.wait_ge(pt_turned, b * U + u + 1)
                    nc.scalar.copy(pt[:, u % 2, :], ps_t[:, u % 2, :]).then_inc(pt_ready, 1)

                def output_copy(b, k):
                    act.wait_ge(o_turned, b + 1)
                    nc.scalar.copy(oT[:, k, :, :].rearrange("p c t -> p (c t)"), turned16 if quant else ps_m[:, 0, 0:D]
                                   ).then_inc(oT_ready, 1)

                def step(b, k, first, last):
                    for u in range(U):
                        exponent(b, k, u)
                        if u > 0:
                            copy_turned(b, k, u - 1)
                        elif not first:
                            copy_turned(b - 1, 1 - k, U - 1)
                        if not first and u == tail1:
                            output_copy(b - 1, 1 - k)
                        if not last and u == front1:
                            project_front(b + 1, 1 - k)
                        if not last and u == front2:
                            project_back(b + 1, 1 - k)

                project_front(0, 0)
                project_back(0, 0)
                steps(act, step)
                copy_turned(B - 1, 1, U - 1)
                output_copy(B - 1, 1)

            @block.vector
            def _(dve):
                means_of_all(nc, g, means_ready)
                if quant:
                    w_dve(dve)
                    nc.vector.engine_nop().then_inc(weights_ready, 1)
                    dve.wait_ge(mask_in, 16)
                    dve.wait_ge(g.rows_in, 16 * 6)
                else:
                    dve.wait_ge(g.masks_in, 32)
                    dve.wait_ge(g.rows_in, 16 * 6)
                    masks = Chain(dve, sem_m, 2)
                    for b in range(B):
                        masks.start(b)
                        masks.link(nc.vector.tensor_tensor(mask_t[:, :], g.mask_causal, g.mask_padding[:, b, :],
                                                           ALU.max))
                        masks.link(nc.vector.tensor_scalar(maskneg[:, b, :], mask_t[:, :], -1e30, None, ALU.mult))
                        masks.end()
                    nc.vector.engine_nop().then_inc(mask_ready, 1)
                dve.wait_ge(rstd_ready, 2)
                dve.wait_ge(weights_ready, 2 if quant else 1)
                front = Chain(dve, sem_f, 6)
                units = Chain(dve, sem_u, 2 * U if quant else U)
                tail = Chain(dve, sem_t, 7 if quant else 1)
                settled = Settled(dve, f"{cfg.name}_settled")

                def project_front(b, k):
                    s = small[:, k, :]
                    if not quant:
                        nc.vector.tensor_scalar(z[:, k, :], g.X[:, b, :], g.mv[:, b, 0:1], g.rstd[:, bass.ds(b, 1)],
                                                ALU.subtract, ALU.mult).then_inc(z_ready, 1)
                        return
                    front.start(b)
                    front.link(nc.vector.tensor_scalar(z[:, k, :], g.X[:, b, :], g.mv[:, b, 0:1],
                                                       g.rstd[:, bass.ds(b, 1)], ALU.subtract, ALU.mult))
                    front.link(nc.vector.tensor_reduce(s[:, 0:1], z[:, k, :], AX.X, ALU.max, apply_absolute_value=True))
                    front.link(nc.vector.tensor_scalar(s[:, 1:2], s[:, 0:1], 1.0 / 127.0, 1e-8, ALU.mult, ALU.max))
                    front.link(nc.vector.reciprocal(s[:, 2:3], s[:, 1:2]))
                    front.link(nc.vector.tensor_scalar(qf[:, k, :], z[:, k, :], s[:, 2:3], MAGIC, ALU.mult, ALU.add))
                    nc.vector.tensor_scalar(zq[:, k, :], qf[:, k, :], MAGIC, None, ALU.subtract).then_inc(z_ready, 1)

                def project_mid(b, k):
                    if not quant:
                        return
                    dve.wait_ge(q_ready, b + 1)
                    front.link(nc.vector.scalar_tensor_tensor(qf[:, k, :], ps_m[:, 0, D:2 * D], small[:, k, 1:2],
                                                              rows[0][:, :], ALU.mult, ALU.mult))
                    nc.vector.tensor_tensor(qf[:, k, :], qf[:, k, :], w.bq_row[:, :], ALU.add).then_inc(qf_ready, 1)
                    dve.wait_ge(qf_ready, b + 1)

                def project_back(b, k):
                    dve.wait_ge(kT_ready, b + 1)
                    VN = cfg.v_heads * R
                    nc.vector.tensor_tensor(v[:, k, :, 0:R], ps_m[:, 1, D:D + VN].rearrange("p (h r) -> p h r", r=R),
                                            w.bv_row[:, :].rearrange("p (h r) -> p h r", r=R), ALU.add
                                            ).then_inc(v_ready, 1)

                def softmax_shift(b, k, u):
                    dve.wait_ge(s_ready, b * U + u + 1)
                    source = ps_s[:, u % 2, :].rearrange("p (r t) -> p r t", r=4)
                    room = e[:, u % 4, :].rearrange("p (r t) -> p r t", r=4)
                    if quant:
                        wait_past(dve, pt_turned, b * U + u - 3)
                        units.link(nc.vector.scalar_tensor_tensor(
                            room, source, 1.0 / 4.0, mask[:, b, :].unsqueeze(1).to_broadcast([P, 4, P]),
                            ALU.mult, ALU.add))
                        source = room
                    units.link(nc.vector.tensor_reduce(top[:, u % 2, :], source, AX.X, ALU.max))
                    if not quant:
                        wait_past(dve, pt_turned, b * U + u - 3)
                    nc.vector.tensor_tensor(room, source, top[:, u % 2, :].unsqueeze(2).to_broadcast([P, 4, P]),
                                            ALU.subtract).then_inc(e_ready, 1)

                def normalise(b, k):
                    s = small[:, k, :]
                    tail.start(b)
                    dve.wait_ge(pv_done, b * U + U)
                    heads = ps_o[:, k, 0:H * VW].rearrange("p (h w) -> p h w", w=VW)
                    tail.link(nc.vector.reciprocal(rec[:, k, :], heads[:, :, R]))
                    ins = nc.vector.tensor_tensor(o[:, k, :].rearrange("p (h r) -> p h r", r=R), heads[:, :, 0:R],
                                                  rec[:, k, :].unsqueeze(2).to_broadcast([P, H, R]), ALU.mult)
                    if not quant:
                        ins.then_inc(o_ready, 1)
                        return
                    tail.link(ins)
                    tail.link(nc.vector.tensor_reduce(s[:, 4:5], o[:, k, :], AX.X, ALU.max, apply_absolute_value=True))
                    tail.link(nc.vector.tensor_scalar(s[:, 5:6], s[:, 4:5], 1.0 / 127.0, 1e-8, ALU.mult, ALU.max))
                    tail.link(nc.vector.reciprocal(s[:, 6:7], s[:, 5:6]))
                    tail.link(nc.vector.tensor_scalar(o[:, k, :], o[:, k, :], s[:, 6:7], MAGIC, ALU.mult, ALU.add))
                    nc.vector.tensor_scalar(oq[:, k, :], o[:, k, :], MAGIC, None, ALU.subtract).then_inc(o_ready, 1)

                def add_output(b, k):
                    dve.wait_ge(y_ready, b + 1)
                    if quant:
                        dve.wait_ge(o_ready, b + 1)
                        tail.link(nc.vector.scalar_tensor_tensor(o[:, k, :], ps_m[:, 1, 0:D], small[:, k, 5:6],
                                                                 rows[1][:, :], ALU.mult, ALU.mult))
                        nc.vector.tensor_tensor(o[:, k, :], o[:, k, :], w.bo_row[:, :], ALU.add).then_inc(x_done, 1)
                    else:
                        nc.vector.tensor_tensor(o[:, k, :], ps_m[:, 1, 0:D], w.bo_row[:, :], ALU.add).then_inc(x_done, 1)
                    dve.wait_ge(x_done, b + 1)
                    nc.vector.tensor_tensor(g.X[:, b, :], g.X[:, b, :], o[:, k, :], ALU.add).then_inc(stats_done, 1)
                    settled.wait_ge(stats_done, b * 2 + 1)
                    stats_of(nc, g, b).then_inc(stats_done, 1)
                    tail.end()

                def step(b, k, first, last):
                    for u in range(U):
                        softmax_shift(b, k, u)
                        if not first and u == tail1:
                            normalise(b - 1, 1 - k)
                        if not last and u == front1:
                            project_front(b + 1, 1 - k)
                        if not first and u == tail2:
                            add_output(b - 1, 1 - k)
                        if not last and u == front2:
                            project_mid(b + 1, 1 - k)
                            project_back(b + 1, 1 - k)
                    units.end()

                project_front(0, 0)
                project_mid(0, 0)
                project_back(0, 0)
                def step_of(b, k, first, last):
                    units.start(b)
                    step(b, k, first, last)
                steps(dve, step_of)
                normalise(B - 1, 1)
                add_output(B - 1, 1)
                dve.wait_ge(stats_done, 2 * B)


class Experts:

    def __init__(self, name, routed, top, inner):
        self.name, self.routed, self.top, self.inner = name, routed, top, inner
        self.chunks = inner // P


def choose_top(nc, dve, st, g, cfg, value, sel, chain_sem):
    E, K = cfg.routed, cfg.top
    best, over, same = st.sb("best", [P, B, 8]), st.sb("over", [P, B, E]), st.sb("same", [P, B, E])
    rank, room = st.sb("rank", [P, B, E]), st.sb("room", [P, B])
    chain = Chain(dve, chain_sem, 6)
    chain.start(0)
    for b in range(B):
        ins = nc.vector.max(best[:, b, :], value[:, b, :])
    chain.link(ins)
    last = best[:, :, K - 1:K].to_broadcast([P, B, E])
    nc.vector.tensor_tensor(over[:, :, :], value, last, ALU.is_gt)
    chain.link(nc.vector.tensor_tensor(same[:, :, :], value, last, ALU.is_equal))
    nc.vector.tensor_reduce(room[:, :], over[:, :, :], AX.X, ALU.add)
    for b in range(B):
        ins = nc.vector.tensor_tensor_scan(rank[:, b, :], same[:, b, :], same[:, b, :], 0.0, ALU.add, ALU.bypass)
    chain.link(ins)
    chain.link(nc.vector.tensor_scalar(room[:, :], room[:, :], -1.0, float(K), ALU.mult, ALU.add))
    chain.link(nc.vector.tensor_tensor(rank[:, :, :], rank[:, :, :], room[:, :].unsqueeze(2).to_broadcast([P, B, E]),
                                       ALU.is_le))
    chain.link(nc.vector.tensor_tensor(same[:, :, :], same[:, :, :], rank[:, :, :], ALU.mult))
    chain.end()
    return nc.vector.tensor_tensor(sel, over[:, :, :], same[:, :, :], ALU.add)


def route_by_softmax(nc, st, g, cfg, comb, chosen):
    E = cfg.routed
    shifted, shares = st.sem("r_shifted"), st.sem("r_shares")
    chain_sem, top_sem = st.sem("r_chain"), st.sem("r_top")
    value, sel = st.sb("r_value", [P, B, E]), st.sb("r_sel", [P, B, E])
    one, total = st.sb("r_one", [P, B]), st.sb("r_total", [P, B])

    def act_part(act):
        act.wait_ge(shifted, 1)
        nc.scalar.activation(value[:, :, :], value[:, :, :], ACT.Exp).then_inc(shares, 1)

    def dve_part(dve, logits):
        chain = Chain(dve, chain_sem, 6)
        chain.start(0)
        chain.link(nc.vector.tensor_reduce(one[:, :], logits, AX.X, ALU.max))
        nc.vector.tensor_tensor(value[:, :, :], logits, one[:, :].unsqueeze(2).to_broadcast([P, B, E]), ALU.subtract
                                ).then_inc(shifted, 1)
        dve.wait_ge(shares, 1)
        chain.link(choose_top(nc, dve, st, g, cfg, value[:, :, :], sel[:, :, :], top_sem))
        chain.link(nc.vector.tensor_tensor(sel[:, :, :], sel[:, :, :], value[:, :, :], ALU.mult))
        chain.link(nc.vector.tensor_reduce(total[:, :], sel[:, :, :], AX.X, ALU.add))
        chain.link(nc.vector.reciprocal(one[:, :], total[:, :]))
        chain.link(nc.vector.tensor_tensor(comb[:, 0:E, :].rearrange("p e b -> p b e"), sel[:, :, :],
                                           one[:, :].unsqueeze(2).to_broadcast([P, B, E]), ALU.mult))
        chain.end()
        nc.vector.memset(comb[:, E, :], 1.0).then_inc(chosen, 1)
        dve.wait_ge(chosen, 1)

    return act_part, None, dve_part


def route_with_capacity(nc, st, g, cfg, pos, slots, slot, weight, total_scale):
    E, K = cfg.routed, cfg.top
    e_wanted, e_ready, l_wanted, l_ready, s_wanted, s_ready, sel_ready, pos_ready = (
        st.sem(f"r_{n}") for n in ("e_wanted", "e_ready", "l_wanted", "l_ready", "s_wanted", "s_ready", "sel_ready", "pos"))
    chain_sem, top_sem = st.sem("r_chain"), st.sem("r_top")
    mag, ex, w, lg, soft, score = (st.sb(f"r_{n}", [P, B, E]) for n in ("mag", "ex", "w", "lg", "soft", "score"))
    value, sel = st.sb("r_value", [P, B, E]), st.sb("r_sel", [P, B, E])
    before, sel16 = st.sb("r_before", [P, B, E], BF16), st.sb("r_sel16", [P, B, E], BF16)
    total, one = st.sb("r_total", [P, B]), st.sb("r_one", [P, B])
    pick, place = st.sb("r_pick", [P, B, E]), st.sb("r_place", [P, B, E])
    of_pick, slot_f = st.sb("r_of_pick", [P, K, B, E]), st.sb("r_slot", [P, K * B])

    def act_part(act):
        act.wait_ge(e_wanted, 1)
        nc.scalar.activation(ex[:, :, :], mag[:, :, :], ACT.Exp, scale=-1.0).then_inc(e_ready, 1)
        act.wait_ge(l_wanted, 1)
        nc.scalar.activation(lg[:, :, :], w[:, :, :], ACT.Ln).then_inc(l_ready, 1)
        act.wait_ge(s_wanted, 1)
        nc.scalar.activation(score[:, :, :], soft[:, :, :], ACT.Sqrt).then_inc(s_ready, 1)

    def pe_part(pe):
        pe.wait_ge(sel_ready, 1)
        pe.wait_ge(g.earlier_in, 48)
        nc.tensor.matmul(pos, g.earlier16[:, :], sel16[:, :, :].rearrange("p b e -> p (b e)"), start=True, stop=False)
        nc.tensor.matmul(pos, g.ones16[:, :], before[:, :, :].rearrange("p b e -> p (b e)"), start=False, stop=True
                         ).then_inc(pos_ready, 1)

    def dve_part(dve, logits, picked):
        chain = Chain(dve, chain_sem, 0)
        chain.start(0)
        nc.vector.tensor_copy(g.earlier16[:, :], g.earlier[:, :])
        nc.vector.tensor_copy(g.ones16[:, :], g.ones[:, :])
        chain.link(nc.vector.tensor_copy(soft[:, :, :], logits))
        nc.vector.scalar_tensor_tensor(mag[:, :, :], soft[:, :, :], -1.0, soft[:, :, :], ALU.mult, ALU.max
                                       ).then_inc(e_wanted, 1)
        dve.wait_ge(e_ready, 1)
        nc.vector.tensor_scalar(w[:, :, :], ex[:, :, :], 1.0, None, ALU.add).then_inc(l_wanted, 1)
        chain.link(nc.vector.tensor_scalar(sel[:, :, :], ex[:, :, :], 1.0 / 5.0, None, ALU.mult))
        for c in (-1.0 / 4.0, 1.0 / 3.0, -1.0 / 2.0, 1.0):
            chain.link(nc.vector.scalar_tensor_tensor(sel[:, :, :], sel[:, :, :], c, ex[:, :, :], ALU.add, ALU.mult))
        chain.link(nc.vector.scalar_tensor_tensor(sel[:, :, :], ex[:, :, :], SERIES_BELOW, sel[:, :, :],
                                                  ALU.is_lt, ALU.mult))
        dve.wait_ge(l_ready, 1)
        chain.link(nc.vector.scalar_tensor_tensor(value[:, :, :], ex[:, :, :], SERIES_BELOW, lg[:, :, :],
                                                  ALU.is_ge, ALU.mult))
        chain.link(nc.vector.tensor_tensor(sel[:, :, :], sel[:, :, :], value[:, :, :], ALU.add))
        chain.link(nc.vector.tensor_scalar(soft[:, :, :], soft[:, :, :], 0.0, None, ALU.max))
        nc.vector.tensor_tensor(soft[:, :, :], soft[:, :, :], sel[:, :, :], ALU.add).then_inc(s_wanted, 1)
        dve.wait_ge(s_ready, 1)
        chain.link(nc.vector.tensor_tensor(value[:, :, :], score[:, :, :], g.route_bias[:, :].unsqueeze(1)
                                           .to_broadcast([P, B, E]), ALU.add))
        chain.link(choose_top(nc, dve, st, g, cfg, value[:, :, :], sel[:, :, :], top_sem))
        nc.vector.tensor_copy(sel16[:, :, :], sel[:, :, :])
        chain.link(nc.vector.memset(before[:, 0, :], 0.0))
        for b in range(1, B):
            chain.link(nc.vector.tensor_tensor(before[:, b, :], before[:, b - 1, :], sel16[:, b - 1, :], ALU.add))
        nc.vector.engine_nop().then_inc(sel_ready, 1)
        chain.link(nc.vector.tensor_tensor(score[:, :, :], score[:, :, :], sel[:, :, :], ALU.mult))
        chain.link(nc.vector.tensor_reduce(total[:, :], score[:, :, :], AX.X, ALU.add))
        chain.link(nc.vector.reciprocal(one[:, :], total[:, :]))
        chain.link(nc.vector.tensor_tensor(score[:, :, :], score[:, :, :], one[:, :].unsqueeze(2)
                                           .to_broadcast([P, B, E]), ALU.mult))
        for b in range(B):
            ins = nc.vector.tensor_tensor_scan(pick[:, b, :], sel[:, b, :], sel[:, b, :], 0.0, ALU.add, ALU.bypass)
        chain.link(ins)
        chain.link(nc.vector.tensor_tensor(pick[:, :, :], pick[:, :, :], sel[:, :, :], ALU.mult))
        dve.wait_ge(pos_ready, 1)
        pos3 = pos.rearrange("p (b e) -> p b e", e=E)
        nc.vector.tensor_tensor(place[:, :, :], pos3, g.slot_base[:, :].unsqueeze(1).to_broadcast([P, B, E]), ALU.add)
        chain.link(nc.vector.tensor_scalar(value[:, :, :], pos3, float(slots.capacity), None, ALU.is_lt))
        chain.link(nc.vector.scalar_tensor_tensor(place[:, :, :], place[:, :, :], -float(slots.zero_row),
                                                  value[:, :, :], ALU.add, ALU.mult))
        chain.link(nc.vector.scalar_tensor_tensor(score[:, :, :], score[:, :, :], total_scale, value[:, :, :],
                                                  ALU.mult, ALU.mult))
        for source, out in ((place, slot_f[:, :]), (score, weight[:, :, :].rearrange("p k b -> p (k b)"))):
            for k in range(K):
                ins = nc.vector.scalar_tensor_tensor(of_pick[:, k, :, :], pick[:, :, :], float(k + 1), source[:, :, :],
                                                     ALU.is_equal, ALU.mult)
            chain.link(ins)
            chain.link(nc.vector.tensor_reduce(out, of_pick[:, :, :, :].rearrange("p k b e -> p (k b) e"), AX.X, ALU.add))
        nc.vector.tensor_scalar(slot[:, :, :].rearrange("p k b -> p (k b)"), slot_f[:, :], float(slots.zero_row), None,
                                ALU.add).then_inc(picked, 1)

    return act_part, pe_part, dve_part


def mixture(nc, g, a, cfg, w, clip=None, capacity=None, total_scale=None):
    E, M = cfg.routed, cfg.chunks
    UN = 2 * M
    with Stage(nc, cfg.name) as st:
        pool_ln, dve_ln, pe_ln, act_ln, zT_ready = norm_and_turn(nc, st, g)
        logits_ready, chosen = st.sem("logits_ready"), st.sem("chosen")
        gu_ready, silu_ready, h_ready, y_ready, y_read = (
            st.sem(n) for n in ("gu_ready", "silu_ready", "h_ready", "y_ready", "y_read"))
        clip_sem, stats_done = st.sem("clip"), st.sem("stats_done")
        landed = [st.sem(f"landed{k}") for k in range(2)]
        gate_up = st.sb("gate_up", [P, 2, DC, 2, cfg.inner])
        down = st.sb("down", [P, 2, M, D])
        silu, h = st.sb("silu", [P, 2, 512]), st.sb("h", [P, 2, M, 512])
        comb = st.sb("comb", [P, E + 1, B])
        ps_gu = st.ps("ps_gu", [P, 2, 2, 512])
        ps_y = st.ps("ps_y", [P, 2, 512])
        ps_y4 = [ps_y[:, 0, 0:D], ps_y[:, 1, 0:D]]
        logits = ps_y[:, 0, 0:B * E]
        st.pos = ps_y[:, 1, 0:B * E]
        logits3 = logits.rearrange("p (b e) -> p b e", e=E)
        if capacity is None:
            r_act, r_pe, r_dve = route_by_softmax(nc, st, g, cfg, comb, chosen)
        else:
            r_act, r_pe, r_dve = route_with_capacity(nc, st, g, cfg, comb, chosen, capacity, total_scale)

        def experts(eng, one_expert, first=0):
            with eng.Fori(first, E // 2) as i:
                for k in range(2):
                    one_expert(i * 2 + k, k, False)
            one_expert(E, E % 2, True)

        with nc.Block(no_gpsimd_drain=True) as block:

            @block.sync
            def _(sp):
                def load(e, k, last):
                    at = e if isinstance(e, int) else bass.ds(e, 1)
                    if not isinstance(e, int):
                        sp.wait_ge(y_ready, (e - 1) * B)
                        src = w.gate_up[at].rearrange("z (c p) g i -> p (z c) g i", p=P)
                        src_d = w.down[at].rearrange("z (m p) d -> p (z m) d", p=P)
                    else:
                        if e >= 2:
                            sp.wait_ge(y_ready, (e - 1) * B)
                        src = w.gate_up[at].rearrange("(c p) g i -> p c g i", p=P)
                        src_d = w.down[at].rearrange("(m p) d -> p m d", p=P)
                    sp.dma_start(gate_up[:, k, :, :, :], src).then_inc(landed[k], 16)
                    sp.dma_start(down[:, k, :, :], src_d).then_inc(landed[k], 16)

                load(0, 0, False)
                load(1, 1, False)
                experts(sp, load, first=1)

            @block.gpsimd
            def _(pool):
                pool_ln(pool)

            @block.tensor
            def _(pe):
                pe_ln(pe)
                pe.wait_ge(zT_ready, B)
                pe.wait_ge(w.router_landed, 16)
                for b in range(B):
                    for c in range(DC):
                        mm = nc.tensor.matmul(logits[:, b * E:(b + 1) * E], g.zT[:, c, b, :], w.router[:, c, :],
                                              start=(c == 0), stop=(c == DC - 1))
                mm.then_inc(logits_ready, 1)
                if r_pe:
                    r_pe(pe, st.pos)
                pe.wait_ge(chosen, 1)

                def one_expert(e, k, last):
                    pe.wait_ge(landed[k], (e - k) * 16 + 32)
                    for half in range(2):
                        tokens = g.zT[:, :, half * 4:half * 4 + 4, :]
                        for m in range(M):
                            j = half * M + m
                            pe.wait_ge(h_ready, e * UN + j + 1)
                            for which in range(2):
                                for c in range(DC):
                                    mm = nc.tensor.matmul(ps_gu[:, j % 2, which, :],
                                                          gate_up[:, k, c, which, m * P:(m + 1) * P],
                                                          tokens[:, c, :, :].rearrange("p b s -> p (b s)"),
                                                          start=(c == 0), stop=(c == DC - 1))
                            mm.then_inc(gu_ready, 1)
                    for t in range(B):
                        half = t // 4
                        pe.wait_ge(h_ready, e * UN + (half + 1) * M + 2)
                        pe.wait_ge(y_read, e * B + t + 1)
                        for m in range(M):
                            mm = nc.tensor.matmul(ps_y4[t % 2], h[:, half, m, (t % 4) * P:(t % 4 + 1) * P],
                                                  down[:, k, m, :], start=(m == 0), stop=(m == M - 1))
                        mm.then_inc(y_ready, 1)

                experts(pe, one_expert)

            @block.scalar
            def _(act):
                act_ln(act)
                r_act(act)

                def one_expert(e, k, last):
                    for j in range(UN):
                        act.wait_ge(gu_ready, e * UN + j + 1)
                        nc.scalar.activation(silu[:, j % 2, :], ps_gu[:, j % 2, 0, :], ACT.Silu).then_inc(silu_ready, 1)

                experts(act, one_expert)

            @block.vector
            def _(dve):
                dve_ln(dve)
                if capacity is not None:
                    dve.wait_ge(g.earlier_in, 48)
                dve.wait_ge(logits_ready, 1)
                r_dve(dve, logits3)
                dve.sem_inc(h_ready, 2)
                dve.sem_inc(y_read, 2)
                settled = Settled(dve, f"{cfg.name}_settled")

                def one_expert(e, k, last):
                    for j in range(UN):
                        half, m = j // M, j % M
                        dve.wait_ge(silu_ready, e * UN + j + 1)
                        out = h[:, half, m, :]
                        if last and clip:
                            nc.vector.tensor_tensor(out, silu[:, j % 2, :], ps_gu[:, j % 2, 1, :], ALU.mult
                                                    ).then_inc(clip_sem, 1)
                            dve.wait_ge(clip_sem, j + 1)
                            nc.vector.tensor_scalar(out, out, -clip, clip, ALU.max, ALU.min).then_inc(h_ready, 1)
                        else:
                            nc.vector.tensor_tensor(out, silu[:, j % 2, :], ps_gu[:, j % 2, 1, :], ALU.mult
                                                    ).then_inc(h_ready, 1)
                    for t in range(B):
                        dve.wait_ge(y_ready, e * B + t + 1)
                        dve.wait_ge(y_read, e * B + 2)
                        weight = comb[:, e, t:t + 1] if isinstance(e, int) else comb[:, bass.ds(e, 1), t]
                        nc.vector.scalar_tensor_tensor(g.X[:, t, :], ps_y4[t % 2], weight, g.X[:, t, :],
                                                       ALU.mult, ALU.add).then_inc(y_read, 1)

                experts(dve, one_expert)
                dve.wait_ge(y_read, (E + 1) * B + 2)
                for b in range(B):
                    ins = stats_of(nc, g, b)
                ins.then_inc(stats_done, 1)
                dve.wait_ge(stats_done, 1)


class Slots:

    def __init__(self, experts, capacity, top):
        self.experts, self.capacity, self.top = experts, capacity, top
        self.rows = experts * capacity
        self.zero_row = self.rows


def capacity_mixture(nc, g, a, cfg, w, clip, capacity, total_scale):
    E, K, GROUP, WSLOTS = cfg.routed, cfg.top, 4, 3
    G, slots = E // GROUP, Slots(E, capacity, K)
    C = capacity
    z_slots = nc.dram_tensor(f"{cfg.name}_z_slots", (slots.rows, D), F32, kind="Internal").ap()
    y_slots = nc.dram_tensor(f"{cfg.name}_y_slots", (slots.rows + P, D), F32, kind="Internal").ap()
    with Stage(nc, cfg.name) as st:
        means_ready, rstd_ready = st.sem("means_ready"), st.sem("rstd_ready")
        z_ready, z_turned, zT_ready = st.sem("z_ready"), st.sem("z_turned"), st.sem("zT_ready")
        logits_ready, picked = st.sem("logits_ready"), st.sem("picked")
        zeros_set, zeroed, scattered = st.sem("zeros_set"), st.sem("zeroed"), st.sem("scattered")
        rows_in = [st.sem(f"rows_in{k}") for k in range(2)]
        w_in = [st.sem(f"w_in{k}") for k in range(WSLOTS)]
        shared_in = st.sem("shared_in")
        gathered = [st.sem(f"gathered{k}") for k in range(GATHERS)]
        s_gu_ready, s_silu_ready, s_clip, s_h_ready, s_y_ready, s_y_read = (
            st.sem(f"shared_{n}") for n in ("gu_ready", "silu_ready", "clip", "h_ready", "y_ready", "y_read"))
        turned, rowsT_ready, gu_ready, silu_ready, h_ready, y_ready, y_copied = (
            st.sem(n) for n in ("turned", "rowsT_ready", "gu_ready", "silu_ready", "h_ready", "y_ready", "y_copied"))
        y_stored = [st.sem(f"y_stored{k}") for k in range(2)]
        added, stats_done = st.sem("added"), st.sem("stats_done")
        Z = st.sb("Z", [P, B, D])
        zeros = st.sb("zeros", [P, 4 * D])
        gate_up = st.sb("gate_up", [P, WSLOTS, GROUP, DC, 2 * P])
        down = st.sb("down", [P, WSLOTS, GROUP, D])
        s_gate_up, s_down = st.sb("shared_gate_up", [P, DC, 2, P]), st.sb("shared_down", [P, D])
        s_silu, s_h = st.sb("shared_silu", [P, 2, 512]), st.sb("shared_h", [P, 2, 512])
        rows = st.sb("rows", [C, 2, GROUP, D])
        rowsT = st.sb("rowsT", [P, 2, DC, GROUP * C])
        silu, h = st.sb("silu", [P, 2, GROUP * C]), st.sb("h", [P, 2, GROUP * C])
        y = st.sb("y", [C, 2, GROUP, D])
        got = gate_up[:, :, :, :, :].rearrange("p w e c i -> p (w e c i)")[:, 0:GATHERS * K * D].rearrange(
            "p (n k d) -> p n k d", n=GATHERS, k=K)
        slot, weight = st.sb("slot", [P, K, B], U32), st.sb("weight", [P, K, B])
        ps_t = st.ps("ps_t", [P, 2, 512])
        ps_gu = st.ps("ps_gu", [P, 2, 2, 512])
        ps_y = st.ps("ps_y", [P, 2, 512])
        logits, pos = ps_y[:, 0, 0:B * E], ps_y[:, 1, 0:B * E]
        r_act, r_pe, r_dve = route_with_capacity(nc, st, g, cfg, pos, slots, slot, weight, total_scale)

        with nc.Block(no_gpsimd_drain=True) as block:

            @block.sync
            def _(sp):
                sp.dma_start(s_gate_up[:, :, :, :], w.gate_up[E].rearrange("(c p) g i -> p c g i", p=P)
                             ).then_inc(shared_in, 16)
                sp.dma_start(s_down[:, :], w.down[E]).then_inc(shared_in, 16)
                sp.wait_ge(zeros_set, 1)
                for n in range(slots.rows // (4 * P)):
                    sp.dma_start(z_slots[n * 4 * P:(n + 1) * 4 * P, :].rearrange("(p r) d -> p (r d)", p=P), zeros[:, :]
                                 ).then_inc(zeroed, 16)
                sp.dma_start(y_slots[slots.rows:slots.rows + P, :], zeros[:, 0:D]).then_inc(zeroed, 16)

                def load_weights(n):
                    if n >= WSLOTS:
                        sp.wait_ge(y_ready, n - WSLOTS + 1)
                    k, at = n % WSLOTS, slice(n * GROUP, (n + 1) * GROUP)
                    for c in range(DC):
                        sp.dma_start(gate_up[:, k, :, c, :],
                                     w.gate_up[at, c * P:(c + 1) * P].rearrange("e p g i -> p e (g i)")
                                     ).then_inc(w_in[k], 16)
                    sp.dma_start(down[:, k, :, :], w.down[at].rearrange("e p d -> p e d")).then_inc(w_in[k], 16)

                def load_rows(n):
                    if n >= 2:
                        sp.wait_ge(turned, n - 1)
                    sp.dma_start(rows[:, n % 2, :, :], z_slots[n * GROUP * C:(n + 1) * GROUP * C, :]
                                 .rearrange("(e s) d -> s e d", s=C)).then_inc(rows_in[n % 2], 16)

                for n in range(WSLOTS):
                    load_weights(n)
                sp.wait_ge(scattered, 16 * K * B)
                load_rows(0)
                load_rows(1)
                for n in range(G):
                    if n + 2 < G:
                        load_rows(n + 2)
                    if n + WSLOTS < G:
                        load_weights(n + WSLOTS)

            @block.gpsimd
            def _(pool):
                nc.gpsimd.memset(zeros[:, :], 0.0).then_inc(zeros_set, 1)
                rstd_of_all(nc, pool, g, means_ready, rstd_ready)
                pool.wait_ge(z_ready, B)
                pool.wait_ge(zeroed, 16 * (slots.rows // (4 * P) + 1))
                pool.wait_ge(picked, 1)
                for b in range(B):
                    for k in range(K):
                        pool.indirect_dma_start(z_slots, bass.IndirectOffsetOnAxis(slot[:, k, b:b + 1], 0), Z[:, b, :],
                                                None, bounds_check=slots.rows - 1, oob_is_err=False
                                                ).then_inc(scattered, 16)
                for k in range(2):
                    pool.wait_ge(y_stored[k], 16 * (G // 2))
                for b in range(B):
                    if b >= GATHERS:
                        pool.wait_ge(added, (b - GATHERS + 1) * K)
                    for k in range(K):
                        pool.indirect_dma_start(got[:, b % GATHERS, k, :], None, y_slots,
                                                bass.IndirectOffsetOnAxis(slot[:, k, b:b + 1], 0),
                                                ).then_inc(gathered[b % GATHERS], 16)

            @block.tensor
            def _(pe):
                for b in range(B):
                    pe.wait_ge(z_ready, b + 1)
                    if b >= 2:
                        pe.wait_ge(zT_ready, b - 1)
                    for c in range(DC):
                        mm = nc.tensor.transpose(ps_t[:, b % 2, c * P:(c + 1) * P], Z[:, b, c * P:(c + 1) * P],
                                                 g.ident[:, :])
                    mm.then_inc(z_turned, 1)
                pe.wait_ge(zT_ready, B)
                pe.wait_ge(w.router_landed, 16)
                for b in range(B):
                    for c in range(DC):
                        mm = nc.tensor.matmul(logits[:, b * E:(b + 1) * E], g.zT[:, c, b, :], w.router[:, c, :],
                                              start=(c == 0), stop=(c == DC - 1))
                mm.then_inc(logits_ready, 1)
                pe.wait_ge(shared_in, 32)
                for half in range(2):
                    for which in range(2):
                        for c in range(DC):
                            mm = nc.tensor.matmul(ps_gu[:, half, which, :], s_gate_up[:, c, which, :],
                                                  g.zT[:, c, half * 4:half * 4 + 4, :].rearrange("p b s -> p (b s)"),
                                                  start=(c == 0), stop=(c == DC - 1))
                    mm.then_inc(s_gu_ready, 1)
                r_pe(pe)
                pe.wait_ge(picked, 1)
                for t in range(B):
                    pe.wait_ge(s_h_ready, t // 4 + 1)
                    if t >= 2:
                        pe.wait_ge(s_y_read, t - 1)
                    nc.tensor.matmul(ps_y[:, t % 2, 0:D], s_h[:, t // 4, (t % 4) * P:(t % 4 + 1) * P], s_down[:, :],
                                     start=True, stop=True).then_inc(s_y_ready, 1)

                def turn(n):
                    pe.wait_ge(rows_in[n % 2], 16 * (n // 2 + 1))
                    if n >= 1:
                        pe.wait_ge(rowsT_ready, n)
                    for c in range(DC):
                        for j in range(GROUP):
                            mm = nc.tensor.transpose(ps_t[:, c, j * C:(j + 1) * C],
                                                     rows[:, n % 2, j, c * P:(c + 1) * P], g.ident[0:C, 0:C])
                    mm.then_inc(turned, 1)

                def inner(n):
                    pe.wait_ge(w_in[n % WSLOTS], 48 * (n // WSLOTS + 1))
                    pe.wait_ge(rowsT_ready, n + 1)
                    if n >= 2:
                        pe.wait_ge(h_ready, n - 1)
                    else:
                        pe.wait_ge(s_h_ready, 2)
                    for j in range(GROUP):
                        for which in range(2):
                            for c in range(DC):
                                mm = nc.tensor.matmul(ps_gu[:, n % 2, which, j * C:(j + 1) * C],
                                                      gate_up[:, n % WSLOTS, j, c, which * P:(which + 1) * P],
                                                      rowsT[:, n % 2, c, j * C:(j + 1) * C],
                                                      start=(c == 0), stop=(c == DC - 1))
                    mm.then_inc(gu_ready, 1)

                def outer(n):
                    pe.wait_ge(h_ready, n + 1)
                    if n >= 1:
                        pe.wait_ge(y_copied, n)
                    else:
                        pe.wait_ge(s_y_read, B)
                    for j in range(GROUP):
                        mm = nc.tensor.matmul(ps_y[0:C, j // 2, (j % 2) * D:(j % 2 + 1) * D],
                                              h[:, n % 2, j * C:(j + 1) * C], down[:, n % WSLOTS, j, :],
                                              start=True, stop=True)
                    mm.then_inc(y_ready, 1)

                turn(0)
                for n in range(G):
                    inner(n)
                    if n + 1 < G:
                        turn(n + 1)
                    outer(n)

            @block.scalar
            def _(act):
                for b in range(B):
                    act.wait_ge(z_turned, b + 1)
                    nc.scalar.copy(g.zT[:, :, b, :], ps_t[:, b % 2, 0:D].rearrange("p (c s) -> p c s", c=DC)
                                   ).then_inc(zT_ready, 1)
                def store_rows(n):
                    act.wait_ge(y_copied, n + 1)
                    act.dma_start(y_slots[n * GROUP * C:(n + 1) * GROUP * C, :].rearrange("(e s) d -> s e d", s=C),
                                  y[:, n % 2, :, :]).then_inc(y_stored[n % 2], 16)

                r_act(act)
                for half in range(2):
                    act.wait_ge(s_gu_ready, half + 1)
                    nc.scalar.activation(s_silu[:, half, :], ps_gu[:, half, 0, :], ACT.Silu).then_inc(s_silu_ready, 1)
                for n in range(G):
                    act.wait_ge(turned, n + 1)
                    if n >= 2:
                        act.wait_ge(gu_ready, n - 1)
                    nc.scalar.copy(rowsT[:, n % 2, :, :], ps_t[:, :, 0:GROUP * C]).then_inc(rowsT_ready, 1)
                    act.wait_ge(gu_ready, n + 1)
                    if n >= 2:
                        act.wait_ge(h_ready, n - 1)
                    nc.scalar.activation(silu[:, n % 2, :], ps_gu[:, n % 2, 0, 0:GROUP * C], ACT.Silu
                                         ).then_inc(silu_ready, 1)
                    if n:
                        store_rows(n - 1)
                store_rows(G - 1)

            @block.vector
            def _(dve):
                means_of_all(nc, g, means_ready)
                dve.wait_ge(rstd_ready, 2)
                for b in range(B):
                    nc.vector.tensor_scalar(Z[:, b, :], g.X[:, b, :], g.mv[:, b, 0:1], g.rstd[:, b:b + 1],
                                            ALU.subtract, ALU.mult).then_inc(z_ready, 1)
                dve.wait_ge(g.earlier_in, 48)
                dve.wait_ge(logits_ready, 1)
                r_dve(dve, logits.rearrange("p (b e) -> p b e", e=E), picked)
                for half in range(2):
                    dve.wait_ge(s_silu_ready, half + 1)
                    nc.vector.tensor_tensor(s_h[:, half, :], s_silu[:, half, :], ps_gu[:, half, 1, :], ALU.mult
                                            ).then_inc(s_clip, 1)
                    dve.wait_ge(s_clip, half + 1)
                    nc.vector.tensor_scalar(s_h[:, half, :], s_h[:, half, :], -clip, clip, ALU.max, ALU.min
                                            ).then_inc(s_h_ready, 1)
                for t in range(B):
                    dve.wait_ge(s_y_ready, t + 1)
                    nc.vector.tensor_tensor(g.X[:, t, :], g.X[:, t, :], ps_y[:, t % 2, 0:D], ALU.add
                                            ).then_inc(s_y_read, 1)
                for n in range(G):
                    dve.wait_ge(silu_ready, n + 1)
                    if n >= 2:
                        dve.wait_ge(y_ready, n - 1)
                    nc.vector.tensor_tensor(h[:, n % 2, :], silu[:, n % 2, :], ps_gu[:, n % 2, 1, 0:GROUP * C], ALU.mult
                                            ).then_inc(h_ready, 1)
                    dve.wait_ge(y_ready, n + 1)
                    if n >= 2:
                        dve.wait_ge(y_stored[n % 2], 16 * (n // 2))
                    nc.vector.tensor_copy(y[:, n % 2, :, :].rearrange("p (u v) d -> p u (v d)", u=2),
                                          ps_y[0:C, :, :]).then_inc(y_copied, 1)
                dve.wait_ge(s_y_read, B)
                for b in range(B):
                    dve.wait_ge(gathered[b % GATHERS], 16 * K * (b // GATHERS + 1))
                    for k in range(K):
                        if k:
                            dve.wait_ge(added, b * K + k)
                        nc.vector.scalar_tensor_tensor(g.X[:, b, :], got[:, b % GATHERS, k, :], weight[:, k, b:b + 1],
                                                       g.X[:, b, :], ALU.mult, ALU.add).then_inc(added, 1)
                    dve.wait_ge(added, (b + 1) * K)
                    ins = stats_of(nc, g, b)
                ins.then_inc(stats_done, 1)
                dve.wait_ge(stats_done, 1)

def cosine_attention(nc, g, a):
    HEADS, R, ALPHA, EPS = 8, S // 8, 5.0, 1e-12
    VW = R + 1
    with Stage(nc, "cos") as st:
        means_ready, rstd_ready, z_ready, squares_ready, norms_ready, roots_ready, rq_ready, rq_turned, rqT_ready = (
            st.sem(n) for n in ("means", "rstd", "z_ready", "squares", "norms", "roots", "rq_ready", "rq_turned", "rqT"))
        spread_ready, qn_ready, slots_ready, s_ready, p_ready, o_ready, on_ready, o_turned, x_done, stats_done = (
            st.sem(n) for n in ("spread", "qn_ready", "slots", "s_ready", "p_ready", "o_ready", "on_ready", "o_turned",
                                "x_done", "stats_done"))
        sem_c, sem_t, ones_set, pool_sem = st.sem("chain"), st.sem("chain_tail"), st.sem("ones_set"), st.sem("pool_chain")
        Z = st.sb("Z", [P, B, D])
        zz, cc = st.sb("zz", [P, B, D]), st.sb("cc", [P, B, D])
        root = st.sb("root", [P, 2, DC * B * HEADS])
        rk, rq = st.sb("rk", [P, DC, B, HEADS]), st.sb("rq", [P, DC, B * HEADS])
        rqT = st.sb("rqT", [B * HEADS, D])
        ks, qs = st.sb("ks", [P, 2, 2, D]), st.sb("qs", [P, 2, D])
        vs = st.sb("vs", [P, 2, DC, HEADS, VW])
        e = st.sb("e", [P, 4, DC, D])
        rec = st.sb("rec", [P, 2, DC * HEADS])
        on = st.sb("on", [P, 2, DC, S])
        ps_s = st.ps("ps_s", [P, 4, 512])
        ps_o = st.ps("ps_o", [P, 2, 512])
        ps_t = st.ps("ps_t", [P, 2, 512])
        N = DC * B * HEADS

        def steps(eng, step):
            step(0, 0, True, False)
            with eng.Fori(0, (B - 2) // 2) as i:
                for k in range(2):
                    step(i * 2 + 1 + k, (1 + k) % 2, False, False)
            step(B - 1, (B - 1) % 2, False, True)

        def wait_past(eng, sem, value):
            if not isinstance(value, int) or value > 0:
                eng.wait_ge(sem, value)

        with nc.Block(no_gpsimd_drain=True) as block:

            @block.gpsimd
            def _(pool):
                rstd_of_all(nc, pool, g, means_ready, rstd_ready)
                for k in range(2):
                    ins = nc.gpsimd.memset(vs[:, k, :, :, R:VW], 1.0)
                ins.then_inc(ones_set, 1)
                pool.wait_ge(ones_set, 1)
                pool.wait_ge(g.cos_in, 48)

                def slots(b, k):
                    wait_past(pool, o_ready, b - 1)
                    for c in range(DC):
                        nc.gpsimd.tensor_copy(vs[:, k, c, :, 0:R],
                                              g.ctxT[:, c, b, :].rearrange("p (h r) -> p h r", r=R))
                    for odd in range(2):
                        nc.gpsimd.tensor_tensor(ks[:, k, odd, :], g.ctx[:, b, :],
                                                g.odd_heads[:, odd:odd + 1].to_broadcast([P, D]), ALU.mult)
                    if isinstance(b, int) and b == 0:
                        pool.wait_ge(qn_ready, B)
                    nc.gpsimd.tensor_copy(qs[:, k, :], Z[:, b, :]).then_inc(slots_ready, 1)

                def step(b, k, first, last):
                    if first:
                        slots(b, k)
                    if not last:
                        slots(b + 1, 1 - k)

                steps(pool, step)

            @block.tensor
            def _(pe):
                pe.wait_ge(g.cos_in, 48)
                pe.wait_ge(squares_ready, 2)
                for which, sq in ((0, cc), (1, zz)):
                    for c in range(DC):
                        for b in range(B):
                            col = which * N + (c * B + b) * HEADS
                            mm = nc.tensor.matmul(ps_t[:, 0, col:col + HEADS], sq[:, b, c * P:(c + 1) * P],
                                                  g.head_of_row[:, :], start=True, stop=True)
                mm.then_inc(norms_ready, 1)
                pe.wait_ge(rq_ready, 1)
                for c in range(DC):
                    mm = nc.tensor.transpose(ps_t[0:B * HEADS, 1, c * P:(c + 1) * P], rq[:, c, :], g.ident[:, :])
                mm.then_inc(rq_turned, 1)
                pe.wait_ge(rqT_ready, 1)
                for b in range(B):
                    if b >= 4:
                        pe.wait_ge(qn_ready, b - 3)
                    nc.tensor.matmul(ps_s[:, b % 4, 0:D], g.spread_heads[:, b, :], rqT[:, :], start=True, stop=True
                                     ).then_inc(spread_ready, 1)
                pe.wait_ge(qn_ready, B)

                def scores(b, k, u):
                    n = b * HEADS + u + 1
                    if u == 0:
                        pe.wait_ge(slots_ready, b + 1)
                    wait_past(pe, p_ready, n - 4)
                    r0 = u // 2 * 2 * R
                    for c in range(DC):
                        mm = nc.tensor.matmul(ps_s[:, u % 4, c * D:(c + 1) * D], ks[r0:r0 + 2 * R, k, u % 2, c * P:(c + 1) * P],
                                              qs[r0:r0 + 2 * R, k, :], start=True, stop=True)
                    mm.then_inc(s_ready, 1)

                def values(b, k, u):
                    pe.wait_ge(p_ready, b * HEADS + u + 1)
                    if u == 0:
                        wait_past(pe, on_ready, b - 1)
                    for qc in range(DC):
                        for c in range(DC):
                            col = (qc * HEADS + u) * VW
                            mm = nc.tensor.matmul(ps_o[:, k, col:col + VW], e[:, u % 4, c, qc * P:(qc + 1) * P],
                                                  vs[:, k, c, u, :], start=(c == 0), stop=(c == DC - 1))
                    if u == HEADS - 1:
                        mm.then_inc(o_ready, 1)

                def turn_output(b, k):
                    pe.wait_ge(on_ready, b + 1)
                    for c in range(DC):
                        mm = nc.tensor.transpose(ps_t[:, k, c * P:(c + 1) * P], on[:, k, c, :], g.ident[:, :])
                    mm.then_inc(o_turned, 1)

                def step(b, k, first, last):
                    for u in range(HEADS):
                        if u + 2 < HEADS:
                            scores(b, k, u + 2)
                        elif not last:
                            scores(b + 1, 1 - k, u + 2 - HEADS)
                        values(b, k, u)
                        if not first and u == 2:
                            turn_output(b - 1, 1 - k)

                scores(0, 0, 0)
                scores(0, 0, 1)
                steps(pe, step)
                turn_output(B - 1, 1)

            @block.scalar
            def _(act):
                act.wait_ge(z_ready, B)
                nc.scalar.activation(cc[:, :, :], g.ctx[:, :, :], ACT.Square).then_inc(squares_ready, 1)
                nc.scalar.activation(zz[:, :, :], Z[:, :, :], ACT.Square).then_inc(squares_ready, 1)
                act.wait_ge(norms_ready, 1)
                nc.scalar.activation(root[:, :, :].rearrange("p w n -> p (w n)"), ps_t[:, 0, 0:2 * N], ACT.Sqrt
                                     ).then_inc(roots_ready, 1)
                act.wait_ge(rq_turned, 1)
                nc.scalar.copy(rqT[:, :], ps_t[0:B * HEADS, 1, 0:D]).then_inc(rqT_ready, 1)
                settled = Settled(act, "cos_act_settled")

                def step(b, k, first, last):
                    for u in range(HEADS):
                        settled.wait_ge(s_ready, b * HEADS + u + 1)
                        for c in range(DC):
                            ins = nc.scalar.activation(e[:, u % 4, c, :], ps_s[:, u % 4, c * D:(c + 1) * D], ACT.Exp,
                                                       scale=rk[:, c, b, u:u + 1])
                        ins.then_inc(p_ready, 1)

                steps(act, step)

            @block.vector
            def _(dve):
                means_of_all(nc, g, means_ready)
                dve.wait_ge(rstd_ready, 2)
                with dve.Fori(0, B) as b:
                    nc.vector.tensor_scalar(Z[:, b, :], g.X[:, b, :], g.mv[:, b, 0:1], g.rstd[:, bass.ds(b, 1)],
                                            ALU.subtract, ALU.mult).then_inc(z_ready, 1)
                chain = Chain(dve, sem_c, 2)
                chain.start(0)
                dve.wait_ge(roots_ready, 1)
                chain.link(nc.vector.tensor_scalar(root[:, :, :], root[:, :, :], EPS, None, ALU.max))
                chain.link(nc.vector.reciprocal(root[:, :, :], root[:, :, :]))
                chain.end()
                nc.vector.tensor_copy(rq[:, :, :].rearrange("p c n -> p (c n)"), root[:, 1, :]).then_inc(rq_ready, 1)
                nc.vector.tensor_scalar(rk[:, :, :, :].rearrange("p c b h -> p (c b h)"), root[:, 0, :], ALPHA, None,
                                        ALU.mult).then_inc(rq_ready, 1)
                for b in range(B):
                    dve.wait_ge(spread_ready, b + 1)
                    nc.vector.tensor_tensor(Z[:, b, :], Z[:, b, :], ps_s[:, b % 4, 0:D], ALU.mult).then_inc(qn_ready, 1)
                tail = Chain(dve, sem_t, 1)
                settled = Settled(dve, "cos_settled")

                def normalise(b, k):
                    dve.wait_ge(o_ready, b + 1)
                    tail.start(b)
                    heads = ps_o[:, k, 0:DC * HEADS * VW].rearrange("p (n w) -> p n w", w=VW)
                    tail.link(nc.vector.reciprocal(rec[:, k, :], heads[:, :, R]))
                    nc.vector.tensor_tensor(on[:, k, :, :].rearrange("p c (h r) -> p (c h) r", r=R), heads[:, :, 0:R],
                                            rec[:, k, :].unsqueeze(2).to_broadcast([P, DC * HEADS, R]), ALU.mult
                                            ).then_inc(on_ready, 1)
                    tail.end()

                def add_output(b, k):
                    dve.wait_ge(o_turned, b + 1)
                    nc.vector.tensor_tensor(g.X[:, b, :], g.X[:, b, :], ps_t[:, k, 0:D], ALU.add).then_inc(x_done, 1)
                    settled.wait_ge(x_done, b + 1)
                    stats_of(nc, g, b).then_inc(stats_done, 1)

                def step(b, k, first, last):
                    normalise(b, k)
                    add_output(b, k)

                steps(dve, step)
                dve.wait_ge(stats_done, B)


def store(nc, g, a):
    with Stage(nc, "store") as st:
        out_done = st.sem("out_done")
        with nc.Block() as block:

            @block.sync
            def _(sp):
                sp.dma_start(a.out.rearrange("b s d -> s b d"), g.X[:, :, :]).then_inc(out_done, 16)
                sp.wait_ge(out_done, 16)


class Names:
    pass


def a_len(a, name):
    return a.by_name[name].shape[0]


def program(nc, a):
    with ExitStack() as ctx:
        g = Names()

        def sb(name, shape, dt=F32):
            return ctx.enter_context(nc.sbuf_tensor(name, shape, dt))

        g.X = sb("X", [P, B, D])
        g.ctx = sb("ctx", [P, B, D])
        g.ctxT = sb("ctxT", [P, DC, B, S])
        g.zT = sb("zT", [P, DC, B, S])
        g.ident = sb("ident", [P, P])
        g.skip = sb("skip", [P, S])
        g.stats = sb("stats", [P, B, 6])
        g.mv = sb("mv", [P, B, 2])
        g.var8 = sb("var8", [P, B])
        g.rstd = sb("rstd", [P, B])
        g.neg_half = sb("neg_half", [P, B])
        g.eps_ff = sb("eps_ff", [P, 1])
        g.ident16 = sb("ident16", [P, P], BF16)
        g.ones = sb("ones", [P, P])
        g.b1, g.b2 = sb("b1", [P, FF]), sb("b2", [P, D])
        g.w0, g.w1 = [Names(), Names()], [Names(), Names()]
        for layer, w in (("L0", g.w0), ("L1", g.w1)):
            for n, (chunks, width) in enumerate(((DC, FF), (FC, D))):
                w[n].tile = sb(f"{layer}_ffn_w{n + 1}", [P, chunks, width])
                w[n].flat = w[n].tile[:, :, :].rearrange("p c f -> p (c f)")
                w[n].landed = nc.alloc_semaphore(f"{layer}_ffn_w{n + 1}_in")
                w[n].source = a.by_name[f"{layer}_ffn_w{n + 1}T"].rearrange("(c p) f -> p c f", p=P)
        g.wa1, g.wa2 = Names(), Names()
        for layer, w, ones in (("L1", g.wa1, ("wq", "wk", "wv", "wo")), ("L2", g.wa2, ("wq", "wk", "wv", "wo"))):
            w.weights = {}
            for n in ones:
                src = a.by_name[f"{layer}_{n}"]
                m = w.weights[n] = Names()
                m.tile = sb(f"{layer}_{n}", [P, DC, src.shape[1]])
                m.landed = nc.alloc_semaphore(f"{layer}_{n}_in")
                m.source = src.rearrange("(c p) f -> p c f", p=P)
            w.wq, w.wk, w.wv, w.wo = (w.weights[n] for n in ones)
            w.head_mask = sb(f"{layer}_head_mask", [P, 4])
            w.bq, w.bk = sb(f"{layer}_bq", [P, DC]), sb(f"{layer}_bk", [P, DC])
            w.bv_row, w.bo_row = sb(f"{layer}_bv", [P, a_len(a, f"{layer}_bv")]), sb(f"{layer}_bo", [P, D])
            w.bq_row = sb(f"{layer}_bq_row", [P, D])
        g.mask_causal_words = sb("mask_causal", [P, P // 4], mybir.dt.int32)
        g.mask_padding_words = sb("mask_padding", [P, B * P // 4], mybir.dt.int32)
        g.mask_causal = g.mask_causal_words[:, :].bitcast(U8)
        g.mask_padding = g.mask_padding_words[:, :].bitcast(U8).rearrange("p (b k) -> p b k", b=B)
        g.m2, g.m3 = Names(), Names()
        for layer, m, e in (("L2", g.m2, 8), ("L3", g.m3, 32)):
            m.gate_up, m.down = a.by_name[f"{layer}_gate_up"], a.by_name[f"{layer}_down"]
            m.router = sb(f"{layer}_router", [P, DC, e])
            m.router_source = a.by_name[f"{layer}_router"].rearrange("(c p) e -> p c e", p=P)
            m.router_landed = nc.alloc_semaphore(f"{layer}_router_in")
        g.earlier, g.earlier16, g.ones16 = sb("earlier", [P, P]), sb("earlier16", [P, P], BF16), sb("ones16", [P, P], BF16)
        g.route_bias, g.slot_base = sb("route_bias", [P, 32]), sb("slot_base", [P, 32])
        g.earlier_in = nc.alloc_semaphore("earlier_in")
        g.odd_heads, g.head_of_row = sb("odd_heads", [P, 2]), sb("head_of_row", [P, 8])
        g.spread_heads = sb("spread_heads", [B * 8, B, P])
        g.cos_in = nc.alloc_semaphore("cos_in")
        g.masks_in, g.rows_in, g.head_mask_in = (nc.alloc_semaphore(n) for n in ("masks_in", "rows_in", "head_mask_in"))
        g.b1_in, g.b2_in = nc.alloc_semaphore("b1_in"), nc.alloc_semaphore("b2_in")
        g.const_in = nc.alloc_semaphore("const_in")
        g.skip_in = nc.alloc_semaphore("skip_in")

        load_and_prepare(nc, g, a)
        long_convolution(nc, g, a)
        quantised_ffn(nc, g, a, "ffn0", g.w0, False)
        attention(nc, g, a, Attention("att1", 8, 8, 8 ** -0.5, False), g.wa1)
        quantised_ffn(nc, g, a, "ffn1", g.w1, True)
        attention(nc, g, a, Attention("att2", 16, 16, 1.0, True), g.wa2)
        mixture(nc, g, a, Experts("moe2", 8, 2, 512), g.m2)
        cosine_attention(nc, g, a)
        capacity_mixture(nc, g, a, Experts("moe3", 32, 6, 128), g.m3, 10.0, L3_CAPACITY, 1.5)
        store(nc, g, a)


def kernel(**inputs):
    import concourse.bacc as _bacc
    from concourse.bass_utils import run_bass_kernel_spmd as _run

    nc = _bacc.Bacc("TRN2", target_bir_lowering=False, num_devices=1)
    f = {k: np.asarray(v) for k, v in inputs.items()}
    k = f["L0_xattn_k"]
    padded = np.concatenate([np.zeros((CONV_HEADS, P - 1), k.dtype), k], axis=1)
    at = (P - 1) + np.arange(2 * P)[None, :] - np.arange(P)[:, None]
    shared = (np.arange(D) // 8 // 4) * 8 + np.arange(D) % 8
    cols = lambda v: v.reshape(DC, P).T
    head_mask = lambda rows: (np.arange(P)[:, None] // rows % 4 == np.arange(4)[None, :]).astype(np.float32)
    split = lambda gu: gu.reshape(*gu.shape[:-1], 2, gu.shape[-1] // 2)
    both = lambda gate, up: np.stack([np.swapaxes(gate, -1, -2), np.swapaxes(up, -1, -2)], axis=-2)
    joined = lambda routed, shared: np.concatenate([routed, shared[None]], axis=0)
    laid = {
        "L2_gate_up": split(joined(f["L2_ffn_expert_gate_up"], f["L2_ffn_base_gate_up"])),
        "L2_down": joined(f["L2_ffn_expert_down"], f["L2_ffn_base_down"]),
        "L2_router": f["L2_ffn_gate_w"],
        "L3_gate_up": both(joined(f["L3_ffn_w_gate"], f["L3_ffn_sg"]), joined(f["L3_ffn_w_up"], f["L3_ffn_su"])),
        "L3_down": np.swapaxes(joined(f["L3_ffn_w_down"], f["L3_ffn_sd"]), 1, 2),
        "L3_router": f["L3_ffn_gate_w"].T, "L3_ffn_bias": f["L3_ffn_bias"],
        "odd_heads": (np.arange(P)[:, None] // 16 % 2 == np.arange(2)[None, :]).astype(np.float32),
        "head_of_row": (np.arange(P)[:, None] // 16 == np.arange(8)[None, :]).astype(np.float32),
        "spread_heads": (np.eye(B)[:, None, :, None] * (np.arange(8)[:, None] == np.arange(P)[None, :] // 16)[None, :, None, :]
                         ).reshape(B * 8, B, P).astype(np.float32),
        "slot_base": (np.arange(32) * L3_CAPACITY).astype(np.float32),
        "earlier": np.triu(np.ones((P, P), np.float32), 1),
        "L1_wq": f["L1_xattn_Wq"].T, "L1_wk": f["L1_xattn_Wk"][shared].T, "L1_wv": f["L1_xattn_Wv"].T,
        "L1_wo": f["L1_xattn_Wo"].T,
        "L1_bq": f["L1_xattn_bq"], "L1_bv": f["L1_xattn_bv"], "L1_bo": f["L1_xattn_bo"],
        "L1_bq_cols": cols(f["L1_xattn_bq"]), "L1_bk_cols": cols(f["L1_xattn_bk"][shared]), "L1_head_mask": head_mask(8),
        "L2_wq": f["L2_xattn_wq"], "L2_wk": f["L2_xattn_wk"].T, "L2_wv": f["L2_xattn_wv"].T, "L2_wo": f["L2_xattn_wo"],
        "L2_bq": f["L2_xattn_bq"], "L2_bv": f["L2_xattn_bv"], "L2_bo": f["L2_xattn_bo"],
        "L2_bq_cols": cols(f["L2_xattn_bq"]), "L2_bk_cols": cols(f["L2_xattn_bk"]), "L2_head_mask": head_mask(16),
        "mask_causal": f["mask_SxS2_bc0"].view(np.int32), "mask_padding": f["mask_BxS2_bk0"].view(np.int32).reshape(-1),
        "mask_ff": f["mask_BxSxS2_ff0"],
        "x": f["x"], "ctx_2048": f["ctx_2048"], "fside_S2_0": f["fside_S2_0"],
        "toeplitz": padded[:, at],
        "L0_ffn_w1T": f["L0_ffn_w1"].T, "L0_ffn_w2T": f["L0_ffn_w2"].T,
        "L1_ffn_w1T": f["L1_ffn_w1"].T, "L1_ffn_w2T": f["L1_ffn_w2"].T,
        "L1_ffn_b1": f["L1_ffn_b1"], "L1_ffn_b2": f["L1_ffn_b2"],
        "ident": np.eye(P, dtype=np.float32),
    }
    a, arrays = Names(), {}
    a.by_name = {}
    for name, v in laid.items():
        v = np.ascontiguousarray(v)
        arrays[f"in_{name}_dram"] = v
        a.by_name[name] = nc.dram_tensor(f"in_{name}_dram", v.shape, mybir.dt.from_np(v.dtype), kind="ExternalInput").ap()
    a.out = nc.dram_tensor("out_0_dram", (B, S, D), F32, kind="ExternalOutput").ap()
    program(nc, a)
    r = _run(nc, [arrays], core_ids=[0])
    return r.results[0]["out_0_dram"]
```

```python
from contextlib import ExitStack

import numpy as np

import concourse.bass as bass
from concourse import mybir

ALU = mybir.AluOpType
ACT = mybir.ActivationFunctionType
AX = mybir.AxisListType
F32 = mybir.dt.float32
BF16 = mybir.dt.bfloat16
U8 = mybir.dt.uint8
U32 = mybir.dt.uint32
I32 = mybir.dt.int32
L3_CAPACITY = 96
GATHERS = 4

P = 128
B, S, D = 8, 128, 256
DC = D // P
T = B * S
CONV_HEADS, CONV_I = 16, 8
FF = 1024
FC = FF // P
MAGIC = 12582912.0
LN_EPS = 1e-5
ERF_EDGE = 5.38
ERF_P = (0.00022905065861350646, 0.0034082910107109506, 0.050955695062380861, 0.18520832239976145, 1.128379143519084)
ERF_Q = (-1.1791602954361697e-7, 0.000023547966471313185, 0.0010179625278914885, 0.014070470171167667,
         0.11098505178285362, 0.49746925110067538, 1.0)
ERF_SQUARES = [(-r.real, r.imag ** 2) for r in np.roots(ERF_P) if r.imag > 0]
EXP_AND_LN = 6
SERIES_BELOW = 0.03


class Chain:

    def __init__(self, eng, sem, per):
        self.eng, self.sem, self.per = eng, sem, per

    def start(self, rounds_before):
        self.base = rounds_before * self.per
        self.n = 0

    def link(self, ins):
        self.n += 1
        ins.then_inc(self.sem, 1)
        self.eng.wait_ge(self.sem, self.base + self.n)

    def end(self):
        assert self.n == self.per, (self.n, self.per)


class Stage:

    def __init__(self, nc, name):
        self.nc, self.name, self.sems, self.stack = nc, name, [], ExitStack()

    def sb(self, name, shape, dt=F32):
        return self.stack.enter_context(self.nc.sbuf_tensor(f"{self.name}_{name}", shape, dt))

    def ps(self, name, shape, dt=F32):
        return self.stack.enter_context(self.nc.psum_tensor(f"{self.name}_{name}", shape, dt))

    def sem(self, name):
        s = self.nc.alloc_semaphore(f"{self.name}_{name}")
        self.sems.append(s)
        return s

    def __enter__(self):
        return self

    def __exit__(self, *_):
        if _[0] is None:
            self.stack.close()
            ids = sorted(s.num for s in self.sems)
            first = 0
            for i in range(1, len(ids) + 1):
                if i == len(ids) or ids[i] != ids[i - 1] + 1:
                    self.nc.all_engine_barrier(sems_to_clear=range(ids[first], ids[i - 1] + 1))
                    first = i
            for s in self.sems:
                self.nc.release_semaphore(s)


def stats_of(nc, g, b):
    return nc.vector.bn_stats(g.stats[:, b, :], g.X[:, b, :])


class Settled:

    def __init__(self, eng, name):
        self.eng, self.reg = eng, eng.alloc_register(name)
        eng.reg_mov(self.reg, 0)

    def wait_ge(self, sem, value):
        self.eng.wait_ge(sem, value)
        self.step()

    def step(self):
        self.eng.reg_add(self.reg, self.reg, 0)


def rstd_of_all(nc, pool, g, means_ready, ready):
    pool.wait_ge(means_ready, 1)
    nc.gpsimd.tensor_scalar(g.var8[:, :], g.mv[:, :, 1], LN_EPS, None, ALU.add).then_inc(ready, 1)
    pool.wait_ge(ready, 1)
    nc.gpsimd.tensor_tensor(g.rstd[:, :], g.var8[:, :], g.neg_half[:, 0:B], ALU.pow).then_inc(ready, 1)


def means_of_all(nc, g, ready):
    for b in range(B):
        ins = nc.vector.bn_aggr(g.mv[:, b, :], g.stats[:, b, :])
    ins.then_inc(ready, 1)


def load_and_prepare(nc, g, a):
    with Stage(nc, "prep") as st:
        x_in, ctx_in = st.sem("x_in"), st.sem("ctx_in")
        turned, copied, stat_done = (st.sem(n) for n in ("turned", "copied", "stat_done"))
        half_set = st.sem("half_set")
        ps = st.ps("ps", [P, 2, 512])
        with nc.Block() as block:

            @block.sync
            def _(sp):
                sp.dma_start(g.ident[:, :], a.by_name["ident"]).then_inc(g.const_in, 16)
                sp.dma_start(g.ctx[:, :, :], a.by_name["ctx_2048"].rearrange("b s d -> s b d")).then_inc(ctx_in, 16)
                sp.dma_start(g.X[:, :, :], a.by_name["x"].rearrange("b s d -> s b d")).then_inc(x_in, 16)
                sp.dma_start(g.skip[:, :], a.by_name["fside_S2_0"].partition_broadcast(P)).then_inc(g.skip_in, 16)
                for w in g.w0 + g.w1:
                    sp.dma_start(w.tile[:, :, :], w.source).then_inc(w.landed, 16)
                for layer, w in (("L1", g.wa1), ("L2", g.wa2)):
                    for n in ("wq", "wk", "wv", "wo"):
                        m = w.weights[n]
                        sp.dma_start(m.tile[:, :, :], m.source).then_inc(m.landed, 16)
                    sp.dma_start(w.head_mask[:, :], a.by_name[f"{layer}_head_mask"]).then_inc(g.head_mask_in, 16)
                    sp.dma_start(w.bk[:, :], a.by_name[f"{layer}_bk_cols"]).then_inc(g.head_mask_in, 16)
                    sp.dma_start(w.bq[:, :], a.by_name[f"{layer}_bq_cols"]).then_inc(g.head_mask_in, 16)
                    for tile, row in ((w.bv_row, "bv"), (w.bo_row, "bo"), (w.bq_row, "bq")):
                        sp.dma_start(tile[:, :], a.by_name[f"{layer}_{row}"].partition_broadcast(P)).then_inc(g.rows_in, 16)
                for m in (g.m2, g.m3):
                    sp.dma_start(m.router[:, :, :], m.router_source).then_inc(m.router_landed, 16)
                sp.dma_start(g.earlier[:, :], a.by_name["earlier"]).then_inc(g.earlier_in, 16)
                sp.dma_start(g.route_bias[:, :], a.by_name["L3_ffn_bias"].partition_broadcast(P)).then_inc(g.earlier_in, 16)
                sp.dma_start(g.slot_base[:, :], a.by_name["slot_base"].partition_broadcast(P)).then_inc(g.earlier_in, 16)
                sp.dma_start(g.tile_numbers[:, :], a.by_name["tile_numbers"]).then_inc(g.earlier_in, 16)
                sp.dma_start(g.odd_heads[:, :], a.by_name["odd_heads"]).then_inc(g.cos_in, 16)
                sp.dma_start(g.head_of_row[:, :], a.by_name["head_of_row"]).then_inc(g.cos_in, 16)
                sp.dma_start(g.spread_heads[:, :, :], a.by_name["spread_heads"]).then_inc(g.cos_in, 16)
                sp.dma_start(g.mask_causal_words[:, :], a.by_name["mask_causal"]).then_inc(g.masks_in, 16)
                sp.dma_start(g.mask_padding_words[:, :],
                             a.by_name["mask_padding"].partition_broadcast(P)).then_inc(g.masks_in, 16)
                sp.dma_start(g.b1[:, :], a.by_name["L1_ffn_b1"].partition_broadcast(P)).then_inc(g.b1_in, 16)
                sp.dma_start(g.b2[:, :], a.by_name["L1_ffn_b2"].partition_broadcast(P)).then_inc(g.b2_in, 16)

            @block.gpsimd
            def _(pool):
                nc.gpsimd.memset(g.neg_half[:, :], -0.5)
                nc.gpsimd.memset(g.eps_ff[:, :], 1e-6 * FF)
                nc.gpsimd.memset(g.ones[:, :], 1.0).then_inc(half_set, 1)

            @block.tensor
            def _(pe):
                pe.wait_ge(g.const_in, 16)
                pe.wait_ge(ctx_in, 16)
                for b in range(B):
                    if b >= 2:
                        pe.wait_ge(copied, b - 1)
                    for c in range(DC):
                        mm = nc.tensor.transpose(ps[:, b % 2, c * P:(c + 1) * P], g.ctx[:, b, c * P:(c + 1) * P],
                                                 g.ident[:, :])
                    mm.then_inc(turned, 1)

            @block.scalar
            def _(act):
                for b in range(B):
                    act.wait_ge(turned, b + 1)
                    nc.scalar.copy(g.ctxT[:, :, b, :],
                                   ps[:, b % 2, 0:D].rearrange("p (c s) -> p c s", c=DC)).then_inc(copied, 1)

            @block.vector
            def _(dve):
                dve.wait_ge(g.const_in, 16)
                nc.vector.tensor_copy(g.ident16[:, :], g.ident[:, :])
                dve.wait_ge(x_in, 16)
                with dve.Fori(0, B) as b:
                    stats_of(nc, g, b).then_inc(stat_done, 1)
                dve.wait_ge(stat_done, B)


def norm_and_turn(nc, st, g):
    means_ready, rstd_ready = st.sem("means_ready"), st.sem("rstd_ready")
    z_ready, z_turned, zT_ready = st.sem("z_ready"), st.sem("z_turned"), st.sem("zT_ready")
    z = st.sb("z", [P, 2, D])
    ps = st.ps("ps_z", [P, 2, 512])

    def pool_part(pool):
        rstd_of_all(nc, pool, g, means_ready, rstd_ready)

    def dve_part(dve):
        means_of_all(nc, g, means_ready)
        dve.wait_ge(rstd_ready, 2)
        with dve.Fori(0, B // 2) as i:
            for k in range(2):
                b = i * 2 + k
                dve.wait_ge(z_turned, i * 2)
                nc.vector.tensor_scalar(z[:, k, :], g.X[:, b, :], g.mv[:, b, 0:1], g.rstd[:, bass.ds(b, 1)],
                                        ALU.subtract, ALU.mult).then_inc(z_ready, 1)

    def pe_part(pe):
        with pe.Fori(0, B // 2) as i:
            for k in range(2):
                b = i * 2 + k
                pe.wait_ge(z_ready, b + 1)
                pe.wait_ge(zT_ready, b)
                for c in range(DC):
                    mm = nc.tensor.transpose(ps[:, k, c * P:(c + 1) * P], z[:, k, c * P:(c + 1) * P], g.ident[:, :])
                mm.then_inc(z_turned, 1)

    def act_part(act):
        with act.Fori(0, B // 2) as i:
            for k in range(2):
                b = i * 2 + k
                act.wait_ge(z_turned, b + 1)
                nc.scalar.copy(g.zT[:, :, b, :],
                               ps[:, k, 0:D].rearrange("p (c s) -> p c s", c=DC)).then_inc(zT_ready, 1)

    return pool_part, dve_part, pe_part, act_part, zT_ready


class Slots:

    def __init__(self, nc, name, experts, top, capacity=None):
        self.experts, self.top, self.capacity = experts, top, capacity
        self.tiles = (T * top - experts) // P + experts
        self.rows = experts * capacity if capacity else self.tiles * P
        self.zero_row = self.rows
        self.z = nc.dram_tensor(f"{name}_z_slots", (self.rows, D), F32, kind="Internal").ap()
        self.y = nc.dram_tensor(f"{name}_y_slots", (self.rows + (P if capacity else 0), D), F32, kind="Internal").ap()

    def clear(self, sp, zeros, cleared):
        blocks = [self.z[n:min(n + 4 * P, self.rows), :] for n in range(0, self.rows, 4 * P)]
        blocks += [self.y[self.rows:self.rows + P, :]] if self.capacity else []
        for block in blocks:
            each = block.shape[0] // P
            sp.dma_start(block.rearrange("(p r) d -> p (r d)", p=P), zeros[:, 0:each * D]).then_inc(cleared, 16)
        return len(blocks)


def long_convolution(nc, g, a):
    with Stage(nc, "conv") as st:
        pool_ln, dve_ln, pe_ln, act_ln, zT_ready = norm_and_turn(nc, st, g)
        toep_in = [st.sem(f"toep_in{k}") for k in range(2)]
        kv_ready, y_ready, y_read, kv_used = (st.sem(n) for n in ("kv_ready", "y_ready", "y_read", "kv_used"))
        chain_sem, pool_chain = st.sem("chain"), st.sem("pool_chain")
        out_ready, out_turned, x_done = st.sem("out_ready"), st.sem("out_turned"), st.sem("x_done")
        skip_terms = st.sem("skip_terms")
        zeros_set, cleared = st.sem("zeros_set"), st.sem("cleared")
        zeros = st.sb("zeros", [P, 4 * D])
        toep = st.sb("toep", [P, 2, 2 * P])
        kv = st.sb("kv", [P, 2, DC, B * 64])
        prod = st.sb("prod", [P, 2, DC, B * 64])
        outT = st.sb("outT", [P, DC, B, S])
        skipz = st.sb("skipz", [P, DC, B * S])
        gate = st.sb("gate", [P, DC * B * CONV_HEADS])
        y = st.ps("y", [P, 2, DC, 512])
        ps_o = st.ps("ps_o", [P, 2, 512])

        def rows_of(t, c, h):
            return t[:, c, :, bass.ds(h * CONV_I, CONV_I)]

        with nc.Block() as block:

            @block.sync
            def _(sp):
                with sp.Fori(0, CONV_HEADS // 2) as i:
                    for k in range(2):
                        sp.wait_ge(y_ready, i * 2)
                        sp.dma_start(toep[:, k, :], a.by_name["toeplitz"][bass.ds(i * 2 + k, 1)].rearrange("a m l -> m (a l)")
                                     ).then_inc(toep_in[k], 16)
                sp.wait_ge(zeros_set, 1)
                clears = sum(slots.clear(sp, zeros, cleared) for slots in (g.slots2, g.slots3))
                sp.wait_ge(cleared, 16 * clears)

            @block.gpsimd
            def _(pool):
                nc.gpsimd.memset(zeros[:, :], 0.0).then_inc(zeros_set, 1)
                pool_ln(pool)
                pool.wait_ge(zT_ready, B)
                with pool.Fori(0, CONV_HEADS // 2) as i:
                    for k in range(2):
                        h = i * 2 + k
                        pool.wait_ge(y_ready, i * 2)
                        for c in range(DC):
                            out = kv[:, k, c, :].rearrange("p (b i j) -> p b i j", b=B, i=CONV_I)
                            shape = [P, B, CONV_I, CONV_I]
                            ins = nc.gpsimd.tensor_tensor(out, rows_of(g.zT, c, h).unsqueeze(3).to_broadcast(shape),
                                                          rows_of(g.ctxT, c, h).unsqueeze(2).to_broadcast(shape),
                                                          ALU.mult)
                        ins.then_inc(kv_ready, 1)
                pool.wait_ge(g.skip_in, 16)
                flat = [t[:, :, :, :].rearrange("p c b s -> p (c b s)") for t in (g.zT, g.ctxT)]
                nc.gpsimd.tensor_tensor(skipz[:, :, :].rearrange("p c t -> p (c t)"), flat[0], flat[1], ALU.mult
                                        ).then_inc(pool_chain, 1)
                pool.wait_ge(pool_chain, 1)
                sz = skipz[:, :, :].rearrange("p c (b s) -> p (c b) s", s=S)
                nc.gpsimd.tensor_tensor(sz, sz, g.skip[:, :].unsqueeze(1).to_broadcast([P, DC * B, S]), ALU.mult
                                        ).then_inc(skip_terms, 1)

            @block.tensor
            def _(pe):
                pe_ln(pe)
                with pe.Fori(0, CONV_HEADS // 2) as i:
                    for k in range(2):
                        pe.wait_ge(toep_in[k], i * 16 + 16)
                        pe.wait_ge(kv_ready, i * 2 + k + 1)
                        pe.wait_ge(y_read, i * 2)
                        nc.tensor.matmul(y[:, k, 0, :], toep[:, k, 0:P], kv[:, k, 0, :], start=True, stop=True)
                        nc.tensor.matmul(y[:, k, 1, :], toep[:, k, 0:P], kv[:, k, 1, :], start=True, stop=False)
                        nc.tensor.matmul(y[:, k, 1, :], toep[:, k, P:2 * P], kv[:, k, 0, :], start=False, stop=True
                                         ).then_inc(y_ready, 1)
                pe.wait_ge(out_ready, 1)
                for b in range(B):
                    if b >= 2:
                        pe.wait_ge(x_done, b - 1)
                    for c in range(DC):
                        mm = nc.tensor.transpose(ps_o[:, b % 2, c * P:(c + 1) * P], outT[:, c, b, :], g.ident[:, :])
                    mm.then_inc(out_turned, 1)

            @block.scalar
            def _(act):
                act_ln(act)

            @block.vector
            def _(dve):
                dve_ln(dve)
                chain = Chain(dve, chain_sem, 1)
                with dve.Fori(0, CONV_HEADS // 2) as i:
                    for k in range(2):
                        h = i * 2 + k
                        dve.wait_ge(y_ready, h + 1)
                        chain.start(h)
                        for c in range(DC):
                            shape = [P, B, CONV_I, CONV_I]
                            ins = nc.vector.tensor_tensor(
                                prod[:, k, c, :].rearrange("p (b i j) -> p b i j", b=B, i=CONV_I),
                                y[:, k, c, :].rearrange("p (b i j) -> p b i j", b=B, i=CONV_I),
                                rows_of(g.ctxT, c, h).unsqueeze(3).to_broadcast(shape), ALU.mult)
                        chain.link(ins)
                        for c in range(DC):
                            ins = nc.vector.tensor_reduce(
                                rows_of(outT, c, h),
                                prod[:, k, c, :].rearrange("p (b i j) -> p b j i", b=B, i=CONV_I), AX.X, ALU.add)
                        ins.then_inc(y_read, 1)
                        chain.end()
                dve.wait_ge(skip_terms, 1)
                dve.wait_ge(y_read, CONV_HEADS)
                tail = Chain(dve, chain_sem, 2)
                tail.base, tail.n = CONV_HEADS, 0
                tail.link(nc.vector.tensor_reduce(gate[:, :], skipz[:, :, :].rearrange("p c (n i) -> p (c n) i", i=CONV_I),
                                                  AX.X, ALU.add))
                sz = skipz[:, :, :].rearrange("p c (n i) -> p (c n) i", i=CONV_I)
                tail.link(nc.vector.tensor_tensor(
                    sz, g.ctxT[:, :, :, :].rearrange("p c b (h i) -> p (c b h) i", i=CONV_I),
                    gate[:, :].unsqueeze(2).to_broadcast([P, DC * B * CONV_HEADS, CONV_I]), ALU.mult))
                flat = outT[:, :, :, :].rearrange("p c b s -> p (c b s)")
                nc.vector.tensor_tensor(flat, flat, skipz[:, :, :].rearrange("p c t -> p (c t)"), ALU.add
                                        ).then_inc(out_ready, 1)
                add_to_residual(nc, dve, st, g, out_turned, x_done, lambda k: ps_o[:, k, 0:D])


def add_to_residual(nc, dve, st, g, ready, done, source):
    stats_done = st.sem("stats_done")
    settled = Settled(dve, f"{st.name}_settled")
    with dve.Fori(0, B // 2) as i:
        for k in range(2):
            b = i * 2 + k
            dve.wait_ge(ready, b + 1)
            nc.vector.tensor_tensor(g.X[:, b, :], g.X[:, b, :], source(k), ALU.add).then_inc(done, 1)
            settled.wait_ge(done, b + 1)
            stats_of(nc, g, b).then_inc(stats_done, 1)
    dve.wait_ge(stats_done, B)


def ternary_weights(nc, st, g, w, wq, rms_norm):
    sums_ready, total_ready, root_ready, unit_ready, wq_ready, chain_sem = (
        st.sem(n) for n in ("w_sums", "w_total", "w_root", "w_unit", "wq_ready", "w_chain"))
    junk = st.sb("w_junk", [P, FF * DC])
    over = st.sb("w_over", [P, FF * DC], BF16)
    under = st.sb("w_under", [P, FF * DC], BF16)
    sums, mean, root, unit = (st.sb(n, [P, 2]) for n in ("w_sums", "w_mean", "w_root", "w_unit"))

    def act_part(act):
        for n in range(2):
            act.wait_ge(w[n].landed, 16)
            if n:
                act.wait_ge(sums_ready, n)
            ins = nc.scalar.activation(junk[:, :], w[n].flat, ACT.Abs if rms_norm else ACT.Square,
                                       accum_out=sums[:, n:n + 1])
            ins.then_inc(sums_ready, 1)

    def pe_part(pe, ps):
        pe.wait_ge(sums_ready, 2)
        nc.tensor.matmul(ps, g.ones[:, :], sums[:, :], start=True, stop=True).then_inc(total_ready, 1)

    def pool_part(pool):
        if not rms_norm:
            pool.wait_ge(unit_ready, 1)
            nc.gpsimd.tensor_tensor(root[:, :], mean[:, :], g.neg_half[:, 0:2], ALU.pow).then_inc(root_ready, 1)

    def dve_part(dve, ps):
        chain = Chain(dve, chain_sem, 7 if not rms_norm else 6)
        chain.start(0)
        dve.wait_ge(total_ready, 1)
        if rms_norm:
            chain.link(nc.vector.tensor_scalar(mean[:, :], ps, 1.0 / (FF * D), None, ALU.mult))
            chain.link(nc.vector.tensor_scalar(unit[:, :], mean[:, :], 1.0 / 127.0, None, ALU.mult))
        else:
            nc.vector.tensor_scalar(mean[:, :], ps, 1.0 / (FF * D), 1e-5, ALU.mult, ALU.max).then_inc(unit_ready, 1)
            dve.wait_ge(root_ready, 1)
            chain.link(nc.vector.reciprocal(mean[:, :], root[:, :]))
            chain.link(nc.vector.tensor_scalar(unit[:, :], mean[:, :], 1.0 / 127.0, None, ALU.mult))
        for n in range(2):
            dve.wait_ge(w[n].landed, 16)
            if rms_norm:
                nc.vector.tensor_scalar(over[:, :], w[n].flat, 0.0, None, ALU.is_gt)
                chain.link(nc.vector.tensor_scalar(under[:, :], w[n].flat, 0.0, None, ALU.is_lt))
            else:
                nc.vector.tensor_scalar(over[:, :], w[n].flat, root[:, n:n + 1], 0.5, ALU.mult, ALU.is_gt)
                chain.link(nc.vector.tensor_scalar(under[:, :], w[n].flat, root[:, n:n + 1], -0.5, ALU.mult, ALU.is_lt))
            ins = nc.vector.tensor_tensor(wq[n].flat, over[:, :], under[:, :], ALU.subtract)
            if n == 0:
                chain.link(ins)
        ins.then_inc(wq_ready, 1)
        dve.wait_ge(wq_ready, 1)
        return chain

    return act_part, pe_part, pool_part, dve_part, wq_ready, unit, mean


def quantised_ffn(nc, g, a, name, w, rms_norm):
    with Stage(nc, name) as st:
        means_ready, rstd_ready, r1_ready = st.sem("means"), st.sem("rstd"), st.sem("r1")
        (q1_ready, q1_turned, q1T_ready, h_ready, hb_ready, gelu_ready, square_ready, r2_ready, q2_ready, q2_turned,
         q2T_ready, y_ready, x_done, stats_done) = (st.sem(n) for n in (
             "q1_ready", "q1_turned", "q1T_ready", "h_ready", "hb_ready", "gelu_ready", "square_ready", "r2_ready",
             "q2_ready", "q2_turned", "q2T_ready", "y_ready", "x_done", "stats_done"))
        factor_ready = st.sem("factor_ready")
        if rms_norm:
            u_ready, sem_g = st.sem("u_ready"), st.sem("chain_g")
            u, usq, erf_p, erf_q = (st.sb(n, [P, FF]) for n in ("u", "usq", "erf_p", "erf_q"))
        sem_a, sem_b, sem_r = st.sem("chain_a"), st.sem("chain_b"), st.sem("chain_r")
        z, t1 = st.sb("z", [P, 2, D]), st.sb("t1", [P, 2, D])
        q1, q1T = st.sb("q1", [P, 2, D], BF16), st.sb("q1T", [P, 2, DC, P], BF16)
        h, q2 = st.sb("h", [P, 2, FF]), st.sb("q2", [P, 2, FF], BF16)
        h_t = st.sb("h_t", [P, 2, FF])
        q2T = st.sb("q2T", [P, 2, FC, P], BF16)
        small = st.sb("small", [P, 2, 12])
        r1, r2 = st.sb("r1", [P, B]), st.sb("r2", [P, 2])
        mean_square, r2_chain = st.sb("mean_square", [P, 2]), st.sem("r2_chain")
        w1q, w2q = st.sb("w1q", [P, DC, FF], BF16), st.sb("w2q", [P, FC, D], BF16)
        ps_h = st.ps("ps_h", [P, 2, FF])
        ps_t1 = st.ps("ps_t1", [P, 1024], BF16)
        ps_t2 = st.ps("ps_t2", [P, FF], BF16)
        ps_y = st.ps("ps_y", [P, 2, 512])
        wq = [Names(), Names()]
        wq[0].flat, wq[1].flat = w1q[:, :, :].rearrange("p c f -> p (c f)"), w2q[:, :, :].rearrange("p c f -> p (c f)")
        w_act, w_pe, w_pool, w_dve, wq_ready, unit, w_mean = ternary_weights(nc, st, g, w, wq, rms_norm)

        def steps(eng, step):
            step(0, 0, True, False)
            with eng.Fori(0, (B - 2) // 2) as i:
                for k in range(2):
                    step(i * 2 + 1 + k, (1 + k) % 2, False, False)
            step(B - 1, (B - 1) % 2, False, True)

        with nc.Block() as block:

            @block.sync
            def _(sp):
                pass

            @block.gpsimd
            def _(pool):
                rstd_of_all(nc, pool, g, means_ready, rstd_ready)
                w_pool(pool)
                if rms_norm:
                    pool.wait_ge(rstd_ready, 2)
                    chain = Chain(pool, sem_r, 5)
                    chain.start(0)
                    chain.link(nc.gpsimd.tensor_tensor(r1[:, :], g.rstd[:, :], g.rstd[:, :], ALU.mult))
                    chain.link(nc.gpsimd.tensor_tensor(r1[:, :], r1[:, :], g.mv[:, :, 1], ALU.mult))
                    chain.link(nc.gpsimd.tensor_scalar(r1[:, :], r1[:, :], 1e-6, None, ALU.add))
                    chain.link(nc.gpsimd.tensor_tensor(g.var8[:, :], r1[:, :], g.neg_half[:, :], ALU.pow))
                    chain.link(nc.gpsimd.tensor_scalar(r1[:, :], g.var8[:, :], float(D) ** -0.5, None, ALU.mult))
                    chain.end()
                    nc.gpsimd.sem_inc(r1_ready, 1)
                    with pool.Fori(0, B // 2) as i:
                        for k in range(2):
                            b = i * 2 + k
                            pool.wait_ge(square_ready, b + 1)
                            nc.gpsimd.tensor_tensor(mean_square[:, k:k + 1], small[:, k, 7:8], g.eps_ff[:, :], ALU.add
                                                    ).then_inc(r2_chain, 1)
                            pool.wait_ge(r2_chain, b + 1)
                            nc.gpsimd.tensor_tensor(r2[:, k:k + 1], mean_square[:, k:k + 1], g.neg_half[:, 0:1], ALU.pow
                                                    ).then_inc(r2_ready, 1)

            @block.tensor
            def _(pe):
                w_pe(pe, ps_y[:, 0, 0:2])

                def first_product(b, k):
                    pe.wait_ge(q1_ready, b + 1)
                    for c in range(DC):
                        mm = nc.tensor.transpose(ps_t1[:, c * P:(c + 1) * P], q1[:, k, c * P:(c + 1) * P], g.ident16[:, :])
                    mm.then_inc(q1_turned, 1)
                    pe.wait_ge(q1T_ready, b + 1)
                    for n in range(2):
                        for c in range(DC):
                            mm = nc.tensor.matmul(ps_h[:, k, n * 512:(n + 1) * 512], q1T[:, k, c, :],
                                                  w1q[:, c, n * 512:(n + 1) * 512], start=(c == 0), stop=(c == DC - 1))
                    mm.then_inc(h_ready, 1)

                def step(b, k, first, last):
                    if not last:
                        first_product(b + 1, 1 - k)
                    pe.wait_ge(q2_ready, b + 1)
                    for c in range(FC):
                        mm = nc.tensor.transpose(ps_t2[:, c * P:(c + 1) * P], q2[:, k, c * P:(c + 1) * P], g.ident16[:, :])
                    mm.then_inc(q2_turned, 1)
                    pe.wait_ge(q2T_ready, b + 1)
                    for c in range(FC):
                        mm = nc.tensor.matmul(ps_y[:, k, 0:D], q2T[:, k, c, :], w2q[:, c, :],
                                              start=(c == 0), stop=(c == FC - 1))
                    mm.then_inc(y_ready, 1)

                pe.wait_ge(wq_ready, 1)
                first_product(0, 0)
                steps(pe, step)

            @block.scalar
            def _(act):
                w_act(act)
                settled = Settled(act, f"{name}_act_settled")

                def inner(b, k):
                    act.wait_ge(q1_turned, b + 1)
                    nc.scalar.copy(q1T[:, k, :, :].rearrange("p c t -> p (c t)"), ps_t1[:, 0:D]).then_inc(q1T_ready, 1)
                    if rms_norm:
                        act.wait_ge(hb_ready, b + 1)
                        nc.scalar.activation(u[:, :], h[:, k, :], ACT.Identity, scale=0.5 ** 0.5)
                        nc.scalar.activation(usq[:, :], h[:, k, :], ACT.Square, scale=0.5 ** 0.5).then_inc(u_ready, 1)
                        act.wait_ge(gelu_ready, b + 1)
                        nc.scalar.activation(h_t[:, k, :], h[:, k, :], ACT.Square, accum_out=small[:, k, 7:8]
                                             ).then_inc(square_ready, 1)
                    else:
                        act.wait_ge(h_ready, b + 1)
                        nc.scalar.activation(h[:, k, :], ps_h[:, k, :], ACT.Gelu, scale=small[:, k, 3:4]
                                             ).then_inc(gelu_ready, 1)

                def step(b, k, first, last):
                    if not last:
                        inner(b + 1, 1 - k)
                    act.wait_ge(q2_turned, b + 1)
                    nc.scalar.copy(q2T[:, k, :, :].rearrange("p c t -> p (c t)"), ps_t2[:, :]).then_inc(q2T_ready, 1)

                inner(0, 0)
                steps(act, step)

            @block.vector
            def _(dve):
                means_of_all(nc, g, means_ready)
                w_dve(dve, ps_y[:, 0, 0:2])
                dve.wait_ge(rstd_ready, 2)
                if rms_norm:
                    dve.wait_ge(r1_ready, 1)
                    dve.wait_ge(g.b1_in, 16)
                    dve.wait_ge(g.b2_in, 16)
                chain_a = Chain(dve, sem_a, 9 if rms_norm else 6)
                chain_b = Chain(dve, sem_b, 5 if rms_norm else 4)
                if rms_norm:
                    chain_g = Chain(dve, sem_g, 16)
                settled = Settled(dve, f"{name}_settled")

                def quantise(chain, s, m, source, scaled, out, r):
                    if r is None:
                        chain.link(nc.vector.tensor_scalar(s[:, m + 1:m + 2], s[:, m:m + 1], 1e-5, None, ALU.max))
                    else:
                        chain.link(nc.vector.tensor_scalar(s[:, m + 1:m + 2], s[:, m:m + 1], r, 1e-5, ALU.mult, ALU.max))
                    chain.link(nc.vector.reciprocal(s[:, m + 2:m + 3], s[:, m + 1:m + 2]))
                    if r is None:
                        chain.link(nc.vector.tensor_scalar(scaled, source, 127.0, s[:, m + 2:m + 3], ALU.mult, ALU.mult))
                        return nc.vector.tensor_scalar(out, scaled, MAGIC, MAGIC, ALU.add, ALU.subtract)
                    chain.link(nc.vector.tensor_scalar(s[:, m + 2:m + 3], s[:, m + 2:m + 3], 127.0, None, ALU.mult))
                    chain.link(nc.vector.tensor_scalar(scaled, source, r, s[:, m + 2:m + 3], ALU.mult, ALU.mult))
                    return nc.vector.tensor_scalar(out, scaled, MAGIC, MAGIC, ALU.add, ALU.subtract)

                def phase_a(b, k):
                    s = small[:, k, :]
                    chain_a.start(b)
                    chain_a.link(nc.vector.tensor_scalar(z[:, k, :], g.X[:, b, :], g.mv[:, b, 0:1],
                                                         g.rstd[:, bass.ds(b, 1)], ALU.subtract, ALU.mult))
                    chain_a.link(nc.vector.tensor_reduce(s[:, 0:1], z[:, k, :], AX.X, ALU.max, apply_absolute_value=True))
                    r = None
                    if rms_norm:
                        chain_a.link(nc.vector.tensor_copy(s[:, 10:11], r1[:, bass.ds(b, 1)]))
                        r = s[:, 10:11]
                    ins = quantise(chain_a, s, 0, z[:, k, :], t1[:, k, :], q1[:, k, :], r)
                    chain_a.link(ins)
                    if rms_norm:
                        chain_a.link(nc.vector.reciprocal(s[:, 3:4], s[:, 2:3]))
                        nc.vector.tensor_tensor(s[:, 3:4], s[:, 3:4], w_mean[:, 0:1], ALU.mult).then_inc(q1_ready, 1)
                    else:
                        nc.vector.tensor_tensor(s[:, 3:4], s[:, 1:2], unit[:, 0:1], ALU.mult).then_inc(q1_ready, 1)
                    chain_a.end()

                def bias(b, k):
                    dve.wait_ge(h_ready, b + 1)
                    nc.vector.scalar_tensor_tensor(h[:, k, :], ps_h[:, k, :], small[:, k, 3:4], g.b1[:, :],
                                                   ALU.mult, ALU.add).then_inc(hb_ready, 1)

                def gelu(b, k):
                    dve.wait_ge(u_ready, b + 1)
                    chain_g.start(b)
                    exact_gelu(nc, chain_g, h[:, k, :], u[:, :], usq[:, :], erf_p[:, :], erf_q[:, :], gelu_ready)
                    chain_g.end()

                def phase_b(b, k):
                    s = small[:, k, :]
                    dve.wait_ge(gelu_ready, b + 1)
                    chain_b.start(b)
                    chain_b.link(nc.vector.tensor_reduce(s[:, 4:5], h[:, k, :], AX.X, ALU.max, apply_absolute_value=True))
                    r = None
                    if rms_norm:
                        dve.wait_ge(r2_ready, b + 1)
                        r = r2[:, k:k + 1]
                    quantise(chain_b, s, 4, h[:, k, :], h_t[:, k, :], q2[:, k, :], r).then_inc(q2_ready, 1)
                    chain_b.end()
                    nc.vector.tensor_tensor(s[:, 11:12], s[:, 5:6], unit[:, 1:2], ALU.mult).then_inc(factor_ready, 1)

                def phase_c(b, k):
                    dve.wait_ge(factor_ready, b + 1)
                    dve.wait_ge(y_ready, b + 1)
                    nc.vector.scalar_tensor_tensor(g.X[:, b, :], ps_y[:, k, 0:D], small[:, k, 11:12], g.X[:, b, :],
                                                   ALU.mult, ALU.add).then_inc(x_done, 1)
                    if rms_norm:
                        dve.wait_ge(x_done, b * 2 + 1)
                        nc.vector.tensor_tensor(g.X[:, b, :], g.X[:, b, :], g.b2[:, :], ALU.add).then_inc(x_done, 1)
                        settled.wait_ge(x_done, b * 2 + 2)
                    else:
                        settled.wait_ge(x_done, b + 1)
                    stats_of(nc, g, b).then_inc(stats_done, 1)

                def step(b, k, first, last):
                    if not last:
                        phase_a(b + 1, 1 - k)
                    phase_b(b, k)
                    if rms_norm and not last:
                        bias(b + 1, 1 - k)
                    if not first:
                        phase_c(b - 1, 1 - k)
                    if rms_norm and not last:
                        gelu(b + 1, 1 - k)

                phase_a(0, 0)
                if rms_norm:
                    bias(0, 0)
                    gelu(0, 0)
                steps(dve, step)
                phase_c(B - 1, (B - 1) % 2)
                dve.wait_ge(stats_done, B)


def load_exp_and_ln(nc, act):
    act.add_instruction(mybir.InstLoadActFuncSet(name=nc.get_next_instruction_name(), act_func_set_id=EXP_AND_LN,
                                                 ins=[], outs=[]))


def normed_quantised_ffn(nc, g, a, name, w):
    with Stage(nc, name) as st:
        means_ready, rstd_ready, r1_ready = st.sem("means"), st.sem("rstd"), st.sem("r1")
        (q1_ready, q1_turned, q1T_ready, h_ready, hb_ready, u_ready, p_ready, q_ready, ln_ready, recip_ready,
         gelu_ready, square_ready, r2_ready, q2_ready, q2_turned, q2T_ready, y_ready, x_done, stats_done,
         factor_ready) = (st.sem(n) for n in (
             "q1_ready", "q1_turned", "q1T_ready", "h_ready", "hb_ready", "u_ready", "p_ready", "q_ready", "ln_ready",
             "recip_ready", "gelu_ready", "square_ready", "r2_ready", "q2_ready", "q2_turned", "q2T_ready", "y_ready",
             "x_done", "stats_done", "factor_ready"))
        usq_ready, squares_ready, q_begun, quotient_ready, shifts_ready = (
            st.sem(n) for n in ("usq_ready", "squares_ready", "q_begun", "quotient_ready", "shifts_ready"))
        sem_a, sem_q, sem_g, sem_b, sem_r1, sem_r2, sem_p = (
            st.sem(f"chain_{n}") for n in ("a", "q", "g", "b", "r1", "r2", "p"))
        biased = st.sem("biased")
        z, t1 = st.sb("z", [P, 2, D]), st.sb("t1", [P, 2, D])
        q1, q1T = st.sb("q1", [P, 2, D], BF16), st.sb("q1T", [P, 2, DC, P], BF16)
        h, q2, q2T = st.sb("h", [P, 2, FF]), st.sb("q2", [P, 2, FF], BF16), st.sb("q2T", [P, 2, FC, P], BF16)
        clamped, squared = st.sb("clamped", [P, FF]), st.sb("squared", [P, FF], BF16)
        u, usq = st.sb("u", [P, FF]), st.sb("usq", [P, FF])
        erf_squares, shifts = st.sb("erf_squares", [P, 2, FF]), st.sb("shifts", [P, 2])
        erf_p, erf_q = st.sb("erf_p", [P, 2, FF]), st.sb("erf_q", [P, 2, FF])
        factor, recip, scaled = (st.sb(n, [P, FF]) for n in ("factor", "recip", "scaled"))
        small = st.sb("small", [P, 2, 12])
        r1, r2, sum_eps = st.sb("r1", [P, B]), st.sb("r2", [P, 2]), st.sb("sum_eps", [P, 2])
        w1q, w2q = st.sb("w1q", [P, DC, FF], BF16), st.sb("w2q", [P, FC, D], BF16)
        ps_h = st.ps("ps_h", [P, 2, FF])
        ps_t1 = st.ps("ps_t1", [P, 1024], BF16)
        ps_t2 = st.ps("ps_t2", [P, FF], BF16)
        ps_y = st.ps("ps_y", [P, 2, 512])
        wq = [Names(), Names()]
        wq[0].flat, wq[1].flat = w1q[:, :, :].rearrange("p c f -> p (c f)"), w2q[:, :, :].rearrange("p c f -> p (c f)")
        w_act, w_pe, _, w_dve, wq_ready, unit, w_mean = ternary_weights(nc, st, g, w, wq, True)

        def steps(eng, step):
            step(0, 0, True, False)
            with eng.Fori(0, (B - 2) // 2) as i:
                for k in range(2):
                    step(i * 2 + 1 + k, (1 + k) % 2, False, False)
            step(B - 1, (B - 1) % 2, False, True)

        with nc.Block(no_gpsimd_drain=True) as block:

            @block.gpsimd
            def _(pool):
                rstd_of_all(nc, pool, g, means_ready, rstd_ready)
                pool.wait_ge(rstd_ready, 2)
                chain = Chain(pool, sem_r1, 5)
                chain.start(0)
                chain.link(nc.gpsimd.tensor_tensor(r1[:, :], g.rstd[:, :], g.rstd[:, :], ALU.mult))
                chain.link(nc.gpsimd.tensor_tensor(r1[:, :], r1[:, :], g.mv[:, :, 1], ALU.mult))
                chain.link(nc.gpsimd.tensor_scalar(r1[:, :], r1[:, :], 1e-6, None, ALU.add))
                chain.link(nc.gpsimd.tensor_tensor(g.var8[:, :], r1[:, :], g.neg_half[:, :], ALU.pow))
                chain.link(nc.gpsimd.tensor_scalar(r1[:, :], g.var8[:, :], float(D) ** -0.5, None, ALU.mult))
                chain.end()
                nc.gpsimd.sem_inc(r1_ready, 1)

                def rms(b, k):
                    pool.wait_ge(square_ready, b + 1)
                    nc.gpsimd.tensor_tensor(sum_eps[:, k:k + 1], small[:, k, 7:8], g.eps_ff[:, :], ALU.add
                                            ).then_inc(sem_r2, 1)
                    pool.wait_ge(sem_r2, b + 1)
                    nc.gpsimd.tensor_tensor(r2[:, k:k + 1], sum_eps[:, k:k + 1], g.neg_half[:, 0:1], ALU.pow
                                            ).then_inc(r2_ready, 1)

                for n, (a_n, _) in enumerate(ERF_SQUARES):
                    ins = nc.gpsimd.memset(shifts[:, n:n + 1], a_n)
                ins.then_inc(shifts_ready, 1)
                p_lead = ERF_P[0]
                for b in range(B):
                    k = b % 2
                    chain = Chain(pool, sem_p, 4)
                    chain.start(b)
                    pool.wait_ge(usq_ready, b + 1)
                    chain.link(nc.gpsimd.tensor_scalar(erf_q[:, k, :], usq[:, :], ERF_Q[0], ERF_Q[1], ALU.mult, ALU.add))
                    nc.gpsimd.tensor_tensor(erf_q[:, k, :], erf_q[:, k, :], usq[:, :], ALU.mult).then_inc(q_begun, 1)
                    if b:
                        rms(b - 1, 1 - k)
                    pool.wait_ge(squares_ready, b + 1)
                    nc.gpsimd.tensor_scalar(factor[:, :], erf_squares[:, 0, :], -0.5 * p_lead, -0.5 * p_lead * ERF_SQUARES[0][1],
                                            ALU.mult, ALU.add)
                    chain.link(nc.gpsimd.tensor_scalar(erf_p[:, k, :], erf_squares[:, 1, :], 1.0, ERF_SQUARES[1][1],
                                                       ALU.mult, ALU.add))
                    chain.link(nc.gpsimd.tensor_tensor(erf_p[:, k, :], erf_p[:, k, :], factor[:, :], ALU.mult))
                    chain.link(nc.gpsimd.tensor_tensor(erf_p[:, k, :], erf_p[:, k, :], u[:, :], ALU.mult))
                    chain.end()
                    nc.gpsimd.sem_inc(p_ready, 1)
                    pool.wait_ge(recip_ready, b + 1)
                    nc.gpsimd.tensor_tensor(erf_p[:, k, :], erf_p[:, k, :], recip[:, :], ALU.mult).then_inc(quotient_ready, 1)
                rms(B - 1, (B - 1) % 2)

            @block.tensor
            def _(pe):
                w_pe(pe, ps_y[:, 0, 0:2])

                def first_product(b, k):
                    pe.wait_ge(q1_ready, b + 1)
                    for c in range(DC):
                        mm = nc.tensor.transpose(ps_t1[:, c * P:(c + 1) * P], q1[:, k, c * P:(c + 1) * P], g.ident16[:, :])
                    mm.then_inc(q1_turned, 1)
                    pe.wait_ge(q1T_ready, b + 1)
                    for n in range(2):
                        for c in range(DC):
                            mm = nc.tensor.matmul(ps_h[:, k, n * 512:(n + 1) * 512], q1T[:, k, c, :],
                                                  w1q[:, c, n * 512:(n + 1) * 512], start=(c == 0), stop=(c == DC - 1))
                    mm.then_inc(h_ready, 1)

                def second_product(b, k):
                    pe.wait_ge(q2_ready, b + 1)
                    for c in range(FC):
                        mm = nc.tensor.transpose(ps_t2[:, c * P:(c + 1) * P], q2[:, k, c * P:(c + 1) * P], g.ident16[:, :])
                    mm.then_inc(q2_turned, 1)
                    pe.wait_ge(q2T_ready, b + 1)
                    for c in range(FC):
                        mm = nc.tensor.matmul(ps_y[:, k, 0:D], q2T[:, k, c, :], w2q[:, c, :],
                                              start=(c == 0), stop=(c == FC - 1))
                    mm.then_inc(y_ready, 1)

                def step(b, k, first, last):
                    if not last:
                        first_product(b + 1, 1 - k)
                    if not first:
                        second_product(b - 1, 1 - k)

                pe.wait_ge(wq_ready, 1)
                first_product(0, 0)
                steps(pe, step)
                second_product(B - 1, (B - 1) % 2)

            @block.scalar
            def _(act):
                w_act(act)

                def turn_in(b, k):
                    act.wait_ge(q1_turned, b + 1)
                    nc.scalar.copy(q1T[:, k, :, :].rearrange("p c t -> p (c t)"), ps_t1[:, 0:D]).then_inc(q1T_ready, 1)

                def erf_argument(b, k):
                    act.wait_ge(hb_ready, b + 1)
                    nc.scalar.activation(usq[:, :], clamped[:, :], ACT.Square, scale=0.5 ** 0.5).then_inc(usq_ready, 1)
                    act.wait_ge(usq_ready, b + 1)
                    for n in range(2):
                        nc.scalar.activation(erf_squares[:, n, :], usq[:, :], ACT.Square, bias=shifts[:, n:n + 1])
                    nc.scalar.activation(u[:, :], clamped[:, :], ACT.Identity, scale=0.5 ** 0.5).then_inc(squares_ready, 1)

                def reciprocal_start(b, k):
                    act.wait_ge(q_ready, b + 1)
                    nc.scalar.activation(recip[:, :], erf_q[:, k, :], ACT.Ln, bias=1.0).then_inc(ln_ready, 1)
                    act.wait_ge(ln_ready, b + 1)
                    nc.scalar.activation(recip[:, :], recip[:, :], ACT.Exp, scale=-1.0).then_inc(recip_ready, 1)

                def squares(b, k):
                    act.wait_ge(gelu_ready, b + 1)
                    nc.scalar.activation(squared[:, :], h[:, k, :], ACT.Square, accum_out=small[:, k, 7:8]
                                         ).then_inc(square_ready, 1)

                def turn_out(b, k):
                    act.wait_ge(q2_turned, b + 1)
                    nc.scalar.copy(q2T[:, k, :, :].rearrange("p c t -> p (c t)"), ps_t2[:, :]).then_inc(q2T_ready, 1)

                def step(b, k, first, last):
                    if not last:
                        turn_in(b + 1, 1 - k)
                    reciprocal_start(b, k)
                    if not first:
                        turn_out(b - 1, 1 - k)
                    if not last:
                        act.wait_ge(p_ready, b + 1)
                        erf_argument(b + 1, 1 - k)
                    squares(b, k)

                load_exp_and_ln(nc, act)
                turn_in(0, 0)
                act.wait_ge(shifts_ready, 1)
                erf_argument(0, 0)
                steps(act, step)
                turn_out(B - 1, (B - 1) % 2)

            @block.vector
            def _(dve):
                means_of_all(nc, g, means_ready)
                w_dve(dve, ps_y[:, 0, 0:2])
                dve.wait_ge(rstd_ready, 2)
                dve.wait_ge(r1_ready, 1)
                dve.wait_ge(g.b1_in, 16)
                dve.wait_ge(g.b2_in, 16)
                chain_a, chain_q = Chain(dve, sem_a, 9), Chain(dve, sem_q, len(ERF_Q) - 4)
                chain_g, chain_b = Chain(dve, sem_g, 2), Chain(dve, sem_b, 5)
                settled = Settled(dve, f"{name}_settled")

                def quantise(chain, s, m, source, scaled, out, r):
                    chain.link(nc.vector.tensor_scalar(s[:, m + 1:m + 2], s[:, m:m + 1], r, 1e-5, ALU.mult, ALU.max))
                    chain.link(nc.vector.reciprocal(s[:, m + 2:m + 3], s[:, m + 1:m + 2]))
                    chain.link(nc.vector.tensor_scalar(s[:, m + 2:m + 3], s[:, m + 2:m + 3], 127.0, None, ALU.mult))
                    chain.link(nc.vector.tensor_scalar(scaled, source, r, s[:, m + 2:m + 3], ALU.mult, ALU.mult))
                    return nc.vector.tensor_scalar(out, scaled, MAGIC, MAGIC, ALU.add, ALU.subtract)

                def phase_a(b, k):
                    s = small[:, k, :]
                    chain_a.start(b)
                    chain_a.link(nc.vector.tensor_scalar(z[:, k, :], g.X[:, b, :], g.mv[:, b, 0:1],
                                                         g.rstd[:, bass.ds(b, 1)], ALU.subtract, ALU.mult))
                    chain_a.link(nc.vector.tensor_reduce(s[:, 0:1], z[:, k, :], AX.X, ALU.max, apply_absolute_value=True))
                    r = s[:, 10:11]
                    chain_a.link(nc.vector.tensor_copy(r, r1[:, bass.ds(b, 1)]))
                    chain_a.link(quantise(chain_a, s, 0, z[:, k, :], t1[:, k, :], q1[:, k, :], r))
                    chain_a.link(nc.vector.reciprocal(s[:, 3:4], s[:, 2:3]))
                    nc.vector.tensor_tensor(s[:, 3:4], s[:, 3:4], w_mean[:, 0:1], ALU.mult).then_inc(q1_ready, 1)
                    chain_a.end()

                def bias(b, k):
                    dve.wait_ge(h_ready, b + 1)
                    nc.vector.scalar_tensor_tensor(h[:, k, :], ps_h[:, k, :], small[:, k, 3:4], g.b1[:, :],
                                                   ALU.mult, ALU.add).then_inc(biased, 1)
                    dve.wait_ge(biased, b + 1)
                    nc.vector.tensor_scalar(clamped[:, :], h[:, k, :], ERF_EDGE, -ERF_EDGE, ALU.min, ALU.max
                                            ).then_inc(hb_ready, 1)

                def erf_denominator(b, k):
                    dve.wait_ge(q_begun, b + 1)
                    chain_q.start(b)
                    for c in ERF_Q[2:-2]:
                        chain_q.link(nc.vector.scalar_tensor_tensor(erf_q[:, k, :], erf_q[:, k, :], c, usq[:, :],
                                                                    ALU.add, ALU.mult))
                    nc.vector.scalar_tensor_tensor(erf_q[:, k, :], erf_q[:, k, :], ERF_Q[-2], usq[:, :], ALU.add, ALU.mult
                                                   ).then_inc(q_ready, 1)
                    chain_q.end()

                def gelu(b, k):
                    dve.wait_ge(recip_ready, b + 1)
                    dve.wait_ge(q_ready, b + 1)
                    chain_g.start(b)
                    chain_g.link(nc.vector.scalar_tensor_tensor(erf_q[:, k, :], erf_q[:, k, :], 1.0, recip[:, :],
                                                                ALU.add, ALU.mult))
                    dve.wait_ge(quotient_ready, b + 1)
                    chain_g.link(nc.vector.scalar_tensor_tensor(erf_q[:, k, :], erf_q[:, k, :], 2.0, erf_p[:, k, :],
                                                                ALU.subtract, ALU.mult))
                    nc.vector.scalar_tensor_tensor(h[:, k, :], erf_q[:, k, :], 0.5, h[:, k, :], ALU.add, ALU.mult
                                                   ).then_inc(gelu_ready, 1)
                    chain_g.end()

                def phase_b(b, k):
                    s = small[:, k, :]
                    dve.wait_ge(gelu_ready, b + 1)
                    chain_b.start(b)
                    chain_b.link(nc.vector.tensor_reduce(s[:, 4:5], h[:, k, :], AX.X, ALU.max, apply_absolute_value=True))
                    dve.wait_ge(r2_ready, b + 1)
                    quantise(chain_b, s, 4, h[:, k, :], scaled[:, :], q2[:, k, :], r2[:, k:k + 1]).then_inc(q2_ready, 1)
                    chain_b.end()
                    nc.vector.tensor_tensor(s[:, 11:12], s[:, 5:6], unit[:, 1:2], ALU.mult).then_inc(factor_ready, 1)

                def phase_c(b, k):
                    dve.wait_ge(factor_ready, b + 1)
                    dve.wait_ge(y_ready, b + 1)
                    nc.vector.scalar_tensor_tensor(g.X[:, b, :], ps_y[:, k, 0:D], small[:, k, 11:12], g.X[:, b, :],
                                                   ALU.mult, ALU.add).then_inc(x_done, 1)
                    dve.wait_ge(x_done, b * 2 + 1)
                    nc.vector.tensor_tensor(g.X[:, b, :], g.X[:, b, :], g.b2[:, :], ALU.add).then_inc(x_done, 1)
                    settled.wait_ge(x_done, b * 2 + 2)
                    stats_of(nc, g, b).then_inc(stats_done, 1)

                def step(b, k, first, last):
                    if not last:
                        phase_a(b + 1, 1 - k)
                    erf_denominator(b, k)
                    if not first:
                        phase_b(b - 1, 1 - k)
                    if not last:
                        bias(b + 1, 1 - k)
                    gelu(b, k)
                    if not first:
                        phase_c(b - 1, 1 - k)

                phase_a(0, 0)
                bias(0, 0)
                steps(dve, step)
                phase_b(B - 1, (B - 1) % 2)
                phase_c(B - 1, (B - 1) % 2)
                dve.wait_ge(stats_done, B)


class Attention:

    def __init__(self, name, rows, v_heads, scale, quantised):
        self.name, self.rows, self.v_heads, self.scale, self.quantised = name, rows, v_heads, scale, quantised
        self.heads = D // rows
        self.k_rows = 4 * rows
        self.units = self.heads // 4
        self.per_v = self.heads // v_heads


def int8_weights(nc, st, g, w, wT, unit_row, ps16, ps32):
    wq_chain, w_turned, w_read, spread_ready, int8_ready = (
        st.sem(n) for n in ("w_chain", "w_turned", "w_read", "w_spread", "int8_ready"))
    t, q = st.sb("w_t", [P, 2, DC, D]), st.sb("w_q", [P, 2, DC, D], BF16)
    s, spread = st.sb("w_s", [P, 2, DC, 3]), st.sb("w_spread", [P, 2, DC, P])
    ROUNDED = 4 + 2 * DC

    def dve_part(dve):
        chain = Chain(dve, wq_chain, ROUNDED)
        chain.start(0)
        for n in range(2):
            dve.wait_ge(w[n].landed, 16)
            ins = nc.vector.tensor_reduce(s[:, n, :, 0], w[n].tile[:, :, :], AX.X, ALU.max, apply_absolute_value=True)
        chain.link(ins)
        chain.link(nc.vector.tensor_scalar(s[:, :, :, 1], s[:, :, :, 0], 1.0 / 127.0, 1e-8, ALU.mult, ALU.max))
        chain.link(nc.vector.reciprocal(s[:, :, :, 2], s[:, :, :, 1]))
        for n in range(2):
            for c in range(DC):
                nc.vector.tensor_scalar(spread[:, n, c, :], g.ones[:, :], s[:, n, c, 1:2], None, ALU.mult)
                chain.link(nc.vector.tensor_scalar(t[:, n, c, :], w[n].tile[:, c, :], s[:, n, c, 2:3], MAGIC,
                                                   ALU.mult, ALU.add))
        chain.link(nc.vector.tensor_scalar(q[:, :, :, :].rearrange("p n c i -> p (n c i)"),
                                           t[:, :, :, :].rearrange("p n c i -> p (n c i)"), MAGIC, None, ALU.subtract))
        chain.end()
        for n in range(2):
            dve.wait_ge(w_turned, 2 * n + 1)
            nc.vector.tensor_copy(wT[n][:, :, :].rearrange("p c o -> p (c o)"), ps16[:, 0:DC * D])
            nc.vector.tensor_copy(unit_row[n][:, :], ps32[:, 0:D]).then_inc(w_read, 1)
        dve.wait_ge(w_read, 2)

    def pe_part(pe):
        pe.wait_ge(wq_chain, ROUNDED)
        for n in range(2):
            if n:
                pe.wait_ge(w_read, n)
            for o in range(DC):
                nc.tensor.matmul(ps32[:, o * P:(o + 1) * P], spread[:, n, o, :], g.ident[:, :], start=True, stop=True)
                for c in range(DC):
                    mm = nc.tensor.transpose(ps16[:, c * D + o * P:c * D + (o + 1) * P], q[:, n, o, c * P:(c + 1) * P],
                                             g.ident16[:, :])
            mm.then_inc(w_turned, 2 if n == 0 else 1)

    return dve_part, pe_part, w_read


def attention(nc, g, a, cfg, w):
    U, H, KR, R = cfg.units, cfg.heads, cfg.k_rows, cfg.rows
    VW = R + 1
    quant = cfg.quantised
    tail1, front1, tail2, front2 = (0, 0, 1, 1) if U == 4 else (1, 3, 2, 4)
    with Stage(nc, cfg.name) as st:
        names = ("means", "rstd", "ctx_copied", "z_ready", "z_turned", "zT_ready", "q_ready", "qT_ready", "kv_made",
                 "kT_ready", "kbd_ready", "v_ready", "s_ready", "e_ready", "p_ready", "pt_turned", "pt_ready",
                 "pv_done", "o_ready", "o_turned", "oT_ready", "y_ready", "x_done", "stats_done", "mask_ready",
                 "weights_ready", "qf_ready")
        sems = dict(zip(names, [st.sem(n) for n in names]))
        (means_ready, rstd_ready, ctx_copied, z_ready, z_turned, zT_ready, q_ready, qT_ready, kv_made, kT_ready,
         kbd_ready, v_ready, s_ready, e_ready, p_ready, pt_turned, pt_ready, pv_done, o_ready, o_turned, oT_ready,
         y_ready, x_done, stats_done, mask_ready, weights_ready, qf_ready) = sems.values()
        sem_f, sem_u, sem_t, sem_m = st.sem("chain_front"), st.sem("chain_unit"), st.sem("chain_tail"), st.sem("chain_mask")
        z, zTs = st.sb("z", [P, 2, D]), st.sb("zTs", [P, 2, DC, P])
        zq, zqT = st.sb("zq", [P, 2, D], BF16), st.sb("zqT", [P, 2, DC, P], BF16)
        qf = st.sb("qf", [P, 2, D])
        small = st.sb("small", [P, 2, 8])
        ctxs = st.sb("ctxs", [P, 2, DC, P])
        qT, kT = st.sb("qT", [P, 2, DC, P]), st.sb("kT", [P, 2, DC, P])
        kbd = st.sb("kbd", [P, 2, DC, 4, P])
        v = st.sb("v", [P, 2, cfg.v_heads, VW])
        top = st.sb("top", [P, 2, 4])
        e = st.sb("e", [P, 4, 4 * P])
        pt = st.sb("pt", [P, 2, 4 * P])
        rec = st.sb("rec", [P, 2, H])
        o, oT = st.sb("o", [P, 2, D]), st.sb("oT", [P, 2, DC, P], BF16 if quant else F32)
        oq = st.sb("oq", [P, 2, D], BF16)
        ps_s = st.ps("ps_s", [P, 2, 512])
        ps_t = st.ps("ps_t", [P, 2, 512])
        ps_o = st.ps("ps_o", [P, 2, 512])
        ps_m = st.ps("ps_m", [P, 2, 512])
        turned16 = ps_m[:, 0, 0:P].bitcast(BF16)
        if quant:
            wqT, woT = st.sb("wqT", [P, DC, D], BF16), st.sb("woT", [P, DC, D], BF16)
            rows = [st.sb("unit_q", [P, D]), st.sb("unit_o", [P, D])]
            w_dve, w_pe, _ = int8_weights(nc, st, g, [w.wq, w.wo], [wqT, woT], rows,
                                          ps_m[:, 0, 0:D].bitcast(BF16), ps_m[:, 1, 0:D])
            mask = st.sb("mask", [P, B, P])
            mask_in = st.sem("mask_in")
        else:
            maskneg = st.sb("maskneg", [P, B, P], BF16)
            mask_t = st.sb("mask_t", [P, P])

        def steps(eng, step):
            step(0, 0, True, False)
            with eng.Fori(0, (B - 2) // 2) as i:
                for k in range(2):
                    step(i * 2 + 1 + k, (1 + k) % 2, False, False)
            step(B - 1, (B - 1) % 2, False, True)

        def wait_past(eng, sem, value):
            if not isinstance(value, int) or value > 0:
                eng.wait_ge(sem, value)

        with nc.Block(no_gpsimd_drain=True) as block:

            @block.sync
            def _(sp):
                if quant:
                    sp.dma_start(mask[:, :, :], a.by_name["mask_ff"].rearrange("b q k -> q b k")).then_inc(mask_in, 16)

            @block.gpsimd
            def _(pool):
                rstd_of_all(nc, pool, g, means_ready, rstd_ready)
                for k in range(2):
                    ins = nc.gpsimd.memset(v[:, k, :, R:VW], 1.0)
                ins.then_inc(weights_ready, 1)

                def ctx_slot(b, k):
                    wait_past(pool, kv_made, b - 1)
                    nc.gpsimd.tensor_copy(ctxs[:, k, :, :], g.ctxT[:, :, b, :]).then_inc(ctx_copied, 1)

                def spread_k(b, k):
                    pool.wait_ge(kT_ready, b + 1)
                    wait_past(pool, s_ready, (b - 1) * U)
                    for c in range(DC):
                        ins = nc.gpsimd.tensor_tensor(
                            kbd[:, k, c, :, :], kT[:, k, c, :].unsqueeze(1).to_broadcast([P, 4, P]),
                            w.head_mask[:, :].unsqueeze(2).to_broadcast([P, 4, P]), ALU.mult)
                    ins.then_inc(kbd_ready, 1)

                def step(b, k, first, last):
                    if first:
                        ctx_slot(b, k)
                        spread_k(b, k)
                    if not last:
                        ctx_slot(b + 1, 1 - k)
                        spread_k(b + 1, 1 - k)

                pool.wait_ge(g.head_mask_in, 16 * 6)
                steps(pool, step)

            @block.tensor
            def _(pe):
                if quant:
                    w_pe(pe)
                    pe.wait_ge(weights_ready, 2)
                for ws in ((w.wk, w.wv) if quant else (w.wq, w.wk, w.wv, w.wo)):
                    pe.wait_ge(ws.landed, 16)
                if not quant:
                    pe.wait_ge(mask_ready, 1)

                def project_front(b, k):
                    pe.wait_ge(z_ready, b + 1)
                    for c in range(DC):
                        if quant:
                            mm = nc.tensor.transpose(turned16[:, c * P:(c + 1) * P], zq[:, k, c * P:(c + 1) * P],
                                                     g.ident16[:, :])
                        else:
                            mm = nc.tensor.transpose(ps_m[:, 0, c * P:(c + 1) * P], z[:, k, c * P:(c + 1) * P],
                                                     g.ident[:, :])
                    mm.then_inc(z_turned, 1)
                    pe.wait_ge(ctx_copied, b + 1)
                    wait_past(pe, x_done, b - 1)
                    wait_past(pe, v_ready, b)
                    for o_ in range(DC):
                        for c in range(DC):
                            nc.tensor.matmul(ps_m[:, 1, o_ * P:(o_ + 1) * P], w.wk.tile[:, c, o_ * P:(o_ + 1) * P],
                                             ctxs[:, k, c, :], start=(c == 0), stop=(c == DC - 1))
                    VN = cfg.v_heads * R
                    for c in range(DC):
                        mm = nc.tensor.matmul(ps_m[:, 1, D:D + VN], ctxs[:, k, c, :], w.wv.tile[:, c, :],
                                              start=(c == 0), stop=(c == DC - 1))
                    mm.then_inc(kv_made, 1)
                    pe.wait_ge(zT_ready, b + 1)
                    if quant:
                        for c in range(DC):
                            mm = nc.tensor.matmul(ps_m[:, 0, D:2 * D], zqT[:, k, c, :], wqT[:, c, :],
                                                  start=(c == 0), stop=(c == DC - 1))
                    else:
                        for o_ in range(DC):
                            for c in range(DC):
                                mm = nc.tensor.matmul(ps_m[:, 0, D + o_ * P:D + (o_ + 1) * P],
                                                      w.wq.tile[:, c, o_ * P:(o_ + 1) * P], zTs[:, k, c, :],
                                                      start=(c == 0), stop=(c == DC - 1))
                    mm.then_inc(q_ready, 1)

                def project_back(b, k):
                    if quant:
                        pe.wait_ge(qf_ready, b + 1)
                        for c in range(DC):
                            mm = nc.tensor.transpose(ps_m[:, 0, c * P:(c + 1) * P], qf[:, k, c * P:(c + 1) * P],
                                                     g.ident[:, :])
                        mm.then_inc(z_turned, 1)

                def scores(b, k, u):
                    n = b * U + u + 1
                    if u == 0:
                        pe.wait_ge(qT_ready, b + 1)
                        pe.wait_ge(kbd_ready, b + 1)
                    wait_past(pe, e_ready, n - 2)
                    c, r0 = u * KR // P, u * KR % P
                    mm = nc.tensor.matmul(ps_s[:, u % 2, :], qT[r0:r0 + KR, k, c, :],
                                          kbd[r0:r0 + KR, k, c, :, :].rearrange("p r t -> p (r t)"),
                                          start=True, stop=quant)
                    if not quant:
                        mm = nc.tensor.matmul(ps_s[:, u % 2, :].rearrange("p (r t) -> p r t", r=4), g.ident16[:, :],
                                              maskneg[:, b, :].unsqueeze(1).to_broadcast([P, 4, P]),
                                              start=False, stop=True)
                    mm.then_inc(s_ready, 1)

                def turn(b, k, u):
                    pe.wait_ge(p_ready, b * U + u + 1)
                    for r in range(4):
                        mm = nc.tensor.transpose(ps_t[:, u % 2, r * P:(r + 1) * P], e[:, u % 4, r * P:(r + 1) * P],
                                                 g.ident[:, :])
                    mm.then_inc(pt_turned, 1)

                def values(b, k, u):
                    pe.wait_ge(pt_ready, b * U + u + 1)
                    if u == 0:
                        pe.wait_ge(v_ready, b + 1)
                        wait_past(pe, o_ready, b - 1)
                    for r in range(4):
                        h = u * 4 + r
                        mm = nc.tensor.matmul(ps_o[:, k, h * VW:(h + 1) * VW], pt[:, u % 2, r * P:(r + 1) * P],
                                              v[:, k, h // cfg.per_v, :], start=True, stop=True)
                    mm.then_inc(pv_done, 1)

                def output_turn(b, k):
                    pe.wait_ge(o_ready, b + 1)
                    for c in range(DC):
                        if quant:
                            mm = nc.tensor.transpose(turned16[:, c * P:(c + 1) * P], oq[:, k, c * P:(c + 1) * P],
                                                     g.ident16[:, :])
                        else:
                            mm = nc.tensor.transpose(ps_m[:, 0, c * P:(c + 1) * P], o[:, k, c * P:(c + 1) * P],
                                                     g.ident[:, :])
                    mm.then_inc(o_turned, 1)

                def output_product(b, k):
                    pe.wait_ge(oT_ready, b + 1)
                    for c in reversed(range(DC)):
                        mm = nc.tensor.matmul(ps_m[:, 1, 0:D], oT[:, k, c, :], (woT if quant else w.wo.tile)[:, c, :],
                                              start=(c == DC - 1), stop=(c == 0))
                    mm.then_inc(y_ready, 1)

                def step(b, k, first, last):
                    for u in range(U):
                        if u + 2 < U:
                            scores(b, k, u + 2)
                        elif not last:
                            scores(b + 1, 1 - k, u + 2 - U)
                        turn(b, k, u)
                        if u > 0:
                            values(b, k, u - 1)
                        elif not first:
                            values(b - 1, 1 - k, U - 1)
                        if not first and u == tail1:
                            output_turn(b - 1, 1 - k)
                            output_product(b - 1, 1 - k)
                        if not last and u == front1:
                            project_front(b + 1, 1 - k)
                        if not last and u == front2:
                            project_back(b + 1, 1 - k)

                project_front(0, 0)
                project_back(0, 0)
                scores(0, 0, 0)
                scores(0, 0, 1)
                steps(pe, step)
                values(B - 1, 1, U - 1)
                output_turn(B - 1, 1)
                output_product(B - 1, 1)

            @block.scalar
            def _(act):
                act.wait_ge(g.head_mask_in, 16 * 6)

                def project_front(b, k):
                    if quant:
                        act.wait_ge(z_turned, b * 2 + 1)
                        nc.scalar.copy(zqT[:, k, :, :].rearrange("p c t -> p (c t)"), turned16).then_inc(zT_ready, 1)
                    else:
                        act.wait_ge(z_turned, b + 1)
                        nc.scalar.copy(zTs[:, k, :, :].rearrange("p c t -> p (c t)"), ps_m[:, 0, 0:D]).then_inc(zT_ready, 1)
                    act.wait_ge(kv_made, b + 1)
                    wait_past(act, kbd_ready, b - 1)
                    for c in range(DC):
                        ins = nc.scalar.activation(kT[:, k, c, :], ps_m[:, 1, c * P:(c + 1) * P], ACT.Identity,
                                                   bias=w.bk[:, c:c + 1])
                    ins.then_inc(kT_ready, 1)
                    if not quant:
                        act.wait_ge(q_ready, b + 1)
                        for c in range(DC):
                            ins = nc.scalar.activation(qT[:, k, c, :], ps_m[:, 0, D + c * P:D + (c + 1) * P],
                                                       ACT.Identity, bias=w.bq[:, c:c + 1])
                        ins.then_inc(qT_ready, 1)

                def project_back(b, k):
                    if quant:
                        act.wait_ge(z_turned, b * 2 + 2)
                        nc.scalar.copy(qT[:, k, :, :].rearrange("p c t -> p (c t)"), ps_m[:, 0, 0:D]).then_inc(qT_ready, 1)

                def exponent(b, k, u):
                    act.wait_ge(e_ready, b * U + u + 1)
                    nc.scalar.activation(e[:, u % 4, :], e[:, u % 4, :], ACT.Exp, scale=cfg.scale).then_inc(p_ready, 1)

                def copy_turned(b, k, u):
                    act.wait_ge(pt_turned, b * U + u + 1)
                    nc.scalar.copy(pt[:, u % 2, :], ps_t[:, u % 2, :]).then_inc(pt_ready, 1)

                def output_copy(b, k):
                    act.wait_ge(o_turned, b + 1)
                    nc.scalar.copy(oT[:, k, :, :].rearrange("p c t -> p (c t)"), turned16 if quant else ps_m[:, 0, 0:D]
                                   ).then_inc(oT_ready, 1)

                def step(b, k, first, last):
                    for u in range(U):
                        exponent(b, k, u)
                        if u > 0:
                            copy_turned(b, k, u - 1)
                        elif not first:
                            copy_turned(b - 1, 1 - k, U - 1)
                        if not first and u == tail1:
                            output_copy(b - 1, 1 - k)
                        if not last and u == front1:
                            project_front(b + 1, 1 - k)
                        if not last and u == front2:
                            project_back(b + 1, 1 - k)

                project_front(0, 0)
                project_back(0, 0)
                steps(act, step)
                copy_turned(B - 1, 1, U - 1)
                output_copy(B - 1, 1)

            @block.vector
            def _(dve):
                means_of_all(nc, g, means_ready)
                if quant:
                    w_dve(dve)
                    nc.vector.engine_nop().then_inc(weights_ready, 1)
                    dve.wait_ge(mask_in, 16)
                    dve.wait_ge(g.rows_in, 16 * 6)
                else:
                    dve.wait_ge(g.masks_in, 32)
                    dve.wait_ge(g.rows_in, 16 * 6)
                    masks = Chain(dve, sem_m, 2)
                    for b in range(B):
                        masks.start(b)
                        masks.link(nc.vector.tensor_tensor(mask_t[:, :], g.mask_causal, g.mask_padding[:, b, :],
                                                           ALU.max))
                        masks.link(nc.vector.tensor_scalar(maskneg[:, b, :], mask_t[:, :], -1e30, None, ALU.mult))
                        masks.end()
                    nc.vector.engine_nop().then_inc(mask_ready, 1)
                dve.wait_ge(rstd_ready, 2)
                dve.wait_ge(weights_ready, 2 if quant else 1)
                front = Chain(dve, sem_f, 6)
                units = Chain(dve, sem_u, 2 * U if quant else U)
                tail = Chain(dve, sem_t, 7 if quant else 1)
                settled = Settled(dve, f"{cfg.name}_settled")

                def project_front(b, k):
                    s = small[:, k, :]
                    if not quant:
                        nc.vector.tensor_scalar(z[:, k, :], g.X[:, b, :], g.mv[:, b, 0:1], g.rstd[:, bass.ds(b, 1)],
                                                ALU.subtract, ALU.mult).then_inc(z_ready, 1)
                        return
                    front.start(b)
                    front.link(nc.vector.tensor_scalar(z[:, k, :], g.X[:, b, :], g.mv[:, b, 0:1],
                                                       g.rstd[:, bass.ds(b, 1)], ALU.subtract, ALU.mult))
                    front.link(nc.vector.tensor_reduce(s[:, 0:1], z[:, k, :], AX.X, ALU.max, apply_absolute_value=True))
                    front.link(nc.vector.tensor_scalar(s[:, 1:2], s[:, 0:1], 1.0 / 127.0, 1e-8, ALU.mult, ALU.max))
                    front.link(nc.vector.reciprocal(s[:, 2:3], s[:, 1:2]))
                    front.link(nc.vector.tensor_scalar(qf[:, k, :], z[:, k, :], s[:, 2:3], MAGIC, ALU.mult, ALU.add))
                    nc.vector.tensor_scalar(zq[:, k, :], qf[:, k, :], MAGIC, None, ALU.subtract).then_inc(z_ready, 1)

                def project_mid(b, k):
                    if not quant:
                        return
                    dve.wait_ge(q_ready, b + 1)
                    front.link(nc.vector.scalar_tensor_tensor(qf[:, k, :], ps_m[:, 0, D:2 * D], small[:, k, 1:2],
                                                              rows[0][:, :], ALU.mult, ALU.mult))
                    nc.vector.tensor_tensor(qf[:, k, :], qf[:, k, :], w.bq_row[:, :], ALU.add).then_inc(qf_ready, 1)
                    dve.wait_ge(qf_ready, b + 1)

                def project_back(b, k):
                    dve.wait_ge(kT_ready, b + 1)
                    VN = cfg.v_heads * R
                    nc.vector.tensor_tensor(v[:, k, :, 0:R], ps_m[:, 1, D:D + VN].rearrange("p (h r) -> p h r", r=R),
                                            w.bv_row[:, :].rearrange("p (h r) -> p h r", r=R), ALU.add
                                            ).then_inc(v_ready, 1)

                def softmax_shift(b, k, u):
                    dve.wait_ge(s_ready, b * U + u + 1)
                    source = ps_s[:, u % 2, :].rearrange("p (r t) -> p r t", r=4)
                    room = e[:, u % 4, :].rearrange("p (r t) -> p r t", r=4)
                    if quant:
                        wait_past(dve, pt_turned, b * U + u - 3)
                        units.link(nc.vector.scalar_tensor_tensor(
                            room, source, 1.0 / 4.0, mask[:, b, :].unsqueeze(1).to_broadcast([P, 4, P]),
                            ALU.mult, ALU.add))
                        source = room
                    units.link(nc.vector.tensor_reduce(top[:, u % 2, :], source, AX.X, ALU.max))
                    if not quant:
                        wait_past(dve, pt_turned, b * U + u - 3)
                    nc.vector.tensor_tensor(room, source, top[:, u % 2, :].unsqueeze(2).to_broadcast([P, 4, P]),
                                            ALU.subtract).then_inc(e_ready, 1)

                def normalise(b, k):
                    s = small[:, k, :]
                    tail.start(b)
                    dve.wait_ge(pv_done, b * U + U)
                    heads = ps_o[:, k, 0:H * VW].rearrange("p (h w) -> p h w", w=VW)
                    tail.link(nc.vector.reciprocal(rec[:, k, :], heads[:, :, R]))
                    ins = nc.vector.tensor_tensor(o[:, k, :].rearrange("p (h r) -> p h r", r=R), heads[:, :, 0:R],
                                                  rec[:, k, :].unsqueeze(2).to_broadcast([P, H, R]), ALU.mult)
                    if not quant:
                        ins.then_inc(o_ready, 1)
                        return
                    tail.link(ins)
                    tail.link(nc.vector.tensor_reduce(s[:, 4:5], o[:, k, :], AX.X, ALU.max, apply_absolute_value=True))
                    tail.link(nc.vector.tensor_scalar(s[:, 5:6], s[:, 4:5], 1.0 / 127.0, 1e-8, ALU.mult, ALU.max))
                    tail.link(nc.vector.reciprocal(s[:, 6:7], s[:, 5:6]))
                    tail.link(nc.vector.tensor_scalar(o[:, k, :], o[:, k, :], s[:, 6:7], MAGIC, ALU.mult, ALU.add))
                    nc.vector.tensor_scalar(oq[:, k, :], o[:, k, :], MAGIC, None, ALU.subtract).then_inc(o_ready, 1)

                def add_output(b, k):
                    dve.wait_ge(y_ready, b + 1)
                    if quant:
                        dve.wait_ge(o_ready, b + 1)
                        tail.link(nc.vector.scalar_tensor_tensor(o[:, k, :], ps_m[:, 1, 0:D], small[:, k, 5:6],
                                                                 rows[1][:, :], ALU.mult, ALU.mult))
                        nc.vector.tensor_tensor(o[:, k, :], o[:, k, :], w.bo_row[:, :], ALU.add).then_inc(x_done, 1)
                    else:
                        nc.vector.tensor_tensor(o[:, k, :], ps_m[:, 1, 0:D], w.bo_row[:, :], ALU.add).then_inc(x_done, 1)
                    dve.wait_ge(x_done, b + 1)
                    nc.vector.tensor_tensor(g.X[:, b, :], g.X[:, b, :], o[:, k, :], ALU.add).then_inc(stats_done, 1)
                    settled.wait_ge(stats_done, b * 2 + 1)
                    stats_of(nc, g, b).then_inc(stats_done, 1)
                    tail.end()

                def step(b, k, first, last):
                    for u in range(U):
                        softmax_shift(b, k, u)
                        if not first and u == tail1:
                            normalise(b - 1, 1 - k)
                        if not last and u == front1:
                            project_front(b + 1, 1 - k)
                        if not first and u == tail2:
                            add_output(b - 1, 1 - k)
                        if not last and u == front2:
                            project_mid(b + 1, 1 - k)
                            project_back(b + 1, 1 - k)
                    units.end()

                project_front(0, 0)
                project_mid(0, 0)
                project_back(0, 0)
                def step_of(b, k, first, last):
                    units.start(b)
                    step(b, k, first, last)
                steps(dve, step_of)
                normalise(B - 1, 1)
                add_output(B - 1, 1)
                dve.wait_ge(stats_done, 2 * B)


class Experts:

    def __init__(self, name, routed, top, inner):
        self.name, self.routed, self.top, self.inner = name, routed, top, inner
        self.chunks = inner // P


def choose_top(nc, dve, st, g, cfg, value, sel, chain_sem):
    E, K = cfg.routed, cfg.top
    best, over, same = st.sb("best", [P, B, 8]), st.sb("over", [P, B, E]), st.sb("same", [P, B, E])
    rank, room = st.sb("rank", [P, B, E]), st.sb("room", [P, B])
    chain = Chain(dve, chain_sem, 6)
    chain.start(0)
    for b in range(B):
        ins = nc.vector.max(best[:, b, :], value[:, b, :])
    chain.link(ins)
    last = best[:, :, K - 1:K].to_broadcast([P, B, E])
    nc.vector.tensor_tensor(over[:, :, :], value, last, ALU.is_gt)
    chain.link(nc.vector.tensor_tensor(same[:, :, :], value, last, ALU.is_equal))
    nc.vector.tensor_reduce(room[:, :], over[:, :, :], AX.X, ALU.add)
    for b in range(B):
        ins = nc.vector.tensor_tensor_scan(rank[:, b, :], same[:, b, :], same[:, b, :], 0.0, ALU.add, ALU.bypass)
    chain.link(ins)
    chain.link(nc.vector.tensor_scalar(room[:, :], room[:, :], -1.0, float(K), ALU.mult, ALU.add))
    chain.link(nc.vector.tensor_tensor(rank[:, :, :], rank[:, :, :], room[:, :].unsqueeze(2).to_broadcast([P, B, E]),
                                       ALU.is_le))
    chain.link(nc.vector.tensor_tensor(same[:, :, :], same[:, :, :], rank[:, :, :], ALU.mult))
    chain.end()
    return nc.vector.tensor_tensor(sel, over[:, :, :], same[:, :, :], ALU.add)


def route_with_capacity(nc, st, g, cfg, pos, slots, slot, weight, total_scale):
    E, K = cfg.routed, cfg.top
    e_wanted, e_ready, l_wanted, l_ready, s_wanted, s_ready, sel_ready, pos_ready = (
        st.sem(f"r_{n}") for n in ("e_wanted", "e_ready", "l_wanted", "l_ready", "s_wanted", "s_ready", "sel_ready", "pos"))
    chain_sem, top_sem = st.sem("r_chain"), st.sem("r_top")
    mag, ex, w, lg, soft, score = (st.sb(f"r_{n}", [P, B, E]) for n in ("mag", "ex", "w", "lg", "soft", "score"))
    value, sel = st.sb("r_value", [P, B, E]), st.sb("r_sel", [P, B, E])
    before, sel16 = st.sb("r_before", [P, B, E], BF16), st.sb("r_sel16", [P, B, E], BF16)
    total, one = st.sb("r_total", [P, B]), st.sb("r_one", [P, B])
    pick, place = st.sb("r_pick", [P, B, E]), st.sb("r_place", [P, B, E])
    of_pick, slot_f = st.sb("r_of_pick", [P, K, B, E]), st.sb("r_slot", [P, K * B])

    def act_part(act):
        act.wait_ge(e_wanted, 1)
        nc.scalar.activation(ex[:, :, :], mag[:, :, :], ACT.Exp, scale=-1.0).then_inc(e_ready, 1)
        act.wait_ge(l_wanted, 1)
        nc.scalar.activation(lg[:, :, :], w[:, :, :], ACT.Ln).then_inc(l_ready, 1)
        act.wait_ge(s_wanted, 1)
        nc.scalar.activation(score[:, :, :], soft[:, :, :], ACT.Sqrt).then_inc(s_ready, 1)

    def pe_part(pe):
        pe.wait_ge(sel_ready, 1)
        pe.wait_ge(g.earlier_in, 64)
        nc.tensor.matmul(pos, g.earlier16[:, :], sel16[:, :, :].rearrange("p b e -> p (b e)"), start=True, stop=False)
        nc.tensor.matmul(pos, g.ones16[:, :], before[:, :, :].rearrange("p b e -> p (b e)"), start=False, stop=True
                         ).then_inc(pos_ready, 1)

    def dve_part(dve, logits, picked):
        chain = Chain(dve, chain_sem, 0)
        chain.start(0)
        nc.vector.tensor_copy(g.earlier16[:, :], g.earlier[:, :])
        nc.vector.tensor_copy(g.ones16[:, :], g.ones[:, :])
        chain.link(nc.vector.tensor_copy(soft[:, :, :], logits))
        nc.vector.scalar_tensor_tensor(mag[:, :, :], soft[:, :, :], -1.0, soft[:, :, :], ALU.mult, ALU.max
                                       ).then_inc(e_wanted, 1)
        dve.wait_ge(e_ready, 1)
        nc.vector.tensor_scalar(w[:, :, :], ex[:, :, :], 1.0, None, ALU.add).then_inc(l_wanted, 1)
        chain.link(nc.vector.tensor_scalar(sel[:, :, :], ex[:, :, :], 1.0 / 5.0, None, ALU.mult))
        for c in (-1.0 / 4.0, 1.0 / 3.0, -1.0 / 2.0, 1.0):
            chain.link(nc.vector.scalar_tensor_tensor(sel[:, :, :], sel[:, :, :], c, ex[:, :, :], ALU.add, ALU.mult))
        chain.link(nc.vector.scalar_tensor_tensor(sel[:, :, :], ex[:, :, :], SERIES_BELOW, sel[:, :, :],
                                                  ALU.is_lt, ALU.mult))
        dve.wait_ge(l_ready, 1)
        chain.link(nc.vector.scalar_tensor_tensor(value[:, :, :], ex[:, :, :], SERIES_BELOW, lg[:, :, :],
                                                  ALU.is_ge, ALU.mult))
        chain.link(nc.vector.tensor_tensor(sel[:, :, :], sel[:, :, :], value[:, :, :], ALU.add))
        chain.link(nc.vector.tensor_scalar(soft[:, :, :], soft[:, :, :], 0.0, None, ALU.max))
        nc.vector.tensor_tensor(soft[:, :, :], soft[:, :, :], sel[:, :, :], ALU.add).then_inc(s_wanted, 1)
        dve.wait_ge(s_ready, 1)
        chain.link(nc.vector.tensor_tensor(value[:, :, :], score[:, :, :], g.route_bias[:, :].unsqueeze(1)
                                           .to_broadcast([P, B, E]), ALU.add))
        chain.link(choose_top(nc, dve, st, g, cfg, value[:, :, :], sel[:, :, :], top_sem))
        nc.vector.tensor_copy(sel16[:, :, :], sel[:, :, :])
        chain.link(nc.vector.memset(before[:, 0, :], 0.0))
        for b in range(1, B):
            chain.link(nc.vector.tensor_tensor(before[:, b, :], before[:, b - 1, :], sel16[:, b - 1, :], ALU.add))
        nc.vector.engine_nop().then_inc(sel_ready, 1)
        chain.link(nc.vector.tensor_tensor(score[:, :, :], score[:, :, :], sel[:, :, :], ALU.mult))
        chain.link(nc.vector.tensor_reduce(total[:, :], score[:, :, :], AX.X, ALU.add))
        chain.link(nc.vector.reciprocal(one[:, :], total[:, :]))
        chain.link(nc.vector.tensor_tensor(score[:, :, :], score[:, :, :], one[:, :].unsqueeze(2)
                                           .to_broadcast([P, B, E]), ALU.mult))
        for b in range(B):
            ins = nc.vector.tensor_tensor_scan(pick[:, b, :], sel[:, b, :], sel[:, b, :], 0.0, ALU.add, ALU.bypass)
        chain.link(ins)
        chain.link(nc.vector.tensor_tensor(pick[:, :, :], pick[:, :, :], sel[:, :, :], ALU.mult))
        dve.wait_ge(pos_ready, 1)
        pos3 = pos.rearrange("p (b e) -> p b e", e=E)
        nc.vector.tensor_tensor(place[:, :, :], pos3, g.slot_base[:, :].unsqueeze(1).to_broadcast([P, B, E]), ALU.add)
        chain.link(nc.vector.tensor_scalar(value[:, :, :], pos3, float(slots.capacity), None, ALU.is_lt))
        chain.link(nc.vector.scalar_tensor_tensor(place[:, :, :], place[:, :, :], -float(slots.zero_row),
                                                  value[:, :, :], ALU.add, ALU.mult))
        chain.link(nc.vector.scalar_tensor_tensor(score[:, :, :], score[:, :, :], total_scale, value[:, :, :],
                                                  ALU.mult, ALU.mult))
        for source, out in ((place, slot_f[:, :]), (score, weight[:, :, :].rearrange("p k b -> p (k b)"))):
            for k in range(K):
                ins = nc.vector.scalar_tensor_tensor(of_pick[:, k, :, :], pick[:, :, :], float(k + 1), source[:, :, :],
                                                     ALU.is_equal, ALU.mult)
            chain.link(ins)
            chain.link(nc.vector.tensor_reduce(out, of_pick[:, :, :, :].rearrange("p k b e -> p (k b) e"), AX.X, ALU.add))
        nc.vector.tensor_scalar(slot[:, :, :].rearrange("p k b -> p (k b)"), slot_f[:, :], float(slots.zero_row), None,
                                ALU.add).then_inc(picked, 1)

    return act_part, pe_part, dve_part


def route_to_experts(nc, st, g, cfg, slots, pos, counts, slot, weight, expert_of_tile):
    E, K, N = cfg.routed, cfg.top, slots.tiles
    shifted, shares, sel_ready, pos_ready = (st.sem(f"r_{n}") for n in ("shifted", "shares", "sel_ready", "pos"))
    chain_sem, top_sem = st.sem("r_chain"), st.sem("r_top")
    value, sel = st.sb("r_value", [P, B, E]), st.sb("r_sel", [P, B, E])
    one, total = st.sb("r_one", [P, B]), st.sb("r_total", [P, B])
    before, sel16 = st.sb("r_before", [P, B + 1, E], BF16), st.sb("r_sel16", [P, B, E], BF16)
    tiles, ends, start = (st.sb(f"r_{n}", [P, E]) for n in ("tiles", "ends", "start"))
    past, expert = st.sb("r_past", [1, N, E]), st.sb("r_expert", [1, N])
    pick, of_pick, slot_f = st.sb("r_pick", [P, B, E]), st.sb("r_of_pick", [P, K, B, E]), st.sb("r_slot", [P, K * B])

    def act_part(act):
        act.wait_ge(shifted, 1)
        nc.scalar.activation(value[:, :, :], value[:, :, :], ACT.Exp).then_inc(shares, 1)

    def pe_part(pe):
        pe.wait_ge(sel_ready, 1)
        pe.wait_ge(g.earlier_in, 64)
        nc.tensor.matmul(pos, g.earlier16[:, :], sel16[:, :, :].rearrange("p b e -> p (b e)"), start=True, stop=False)
        nc.tensor.matmul(pos, g.ones16[:, :], before[:, 0:B, :].rearrange("p b e -> p (b e)"), start=False, stop=True)
        nc.tensor.matmul(counts, g.ones16[:, :], before[:, B, :], start=True, stop=True).then_inc(pos_ready, 1)

    def dve_part(dve, logits, picked, experts_known):
        chain = Chain(dve, chain_sem, 0)
        chain.start(0)
        nc.vector.tensor_copy(g.earlier16[:, :], g.earlier[:, :])
        nc.vector.tensor_copy(g.ones16[:, :], g.ones[:, :])
        chain.link(nc.vector.tensor_reduce(one[:, :], logits, AX.X, ALU.max))
        nc.vector.tensor_tensor(value[:, :, :], logits, one[:, :].unsqueeze(2).to_broadcast([P, B, E]), ALU.subtract
                                ).then_inc(shifted, 1)
        dve.wait_ge(shares, 1)
        chain.link(choose_top(nc, dve, st, g, cfg, value[:, :, :], sel[:, :, :], top_sem))
        nc.vector.tensor_copy(sel16[:, :, :], sel[:, :, :])
        chain.link(nc.vector.memset(before[:, 0, :], 0.0))
        for b in range(1, B + 1):
            ins = nc.vector.tensor_tensor(before[:, b, :], before[:, b - 1, :], sel16[:, b - 1, :], ALU.add)
            if b < B:
                chain.link(ins)
        ins.then_inc(sel_ready, 1)
        chain.link(nc.vector.tensor_tensor(value[:, :, :], sel[:, :, :], value[:, :, :], ALU.mult))
        chain.link(nc.vector.tensor_reduce(total[:, :], value[:, :, :], AX.X, ALU.add))
        chain.link(nc.vector.reciprocal(one[:, :], total[:, :]))
        chain.link(nc.vector.tensor_tensor(value[:, :, :], value[:, :, :], one[:, :].unsqueeze(2)
                                           .to_broadcast([P, B, E]), ALU.mult))
        for b in range(B):
            ins = nc.vector.tensor_tensor_scan(pick[:, b, :], sel[:, b, :], sel[:, b, :], 0.0, ALU.add, ALU.bypass)
        chain.link(ins)
        chain.link(nc.vector.tensor_tensor(pick[:, :, :], pick[:, :, :], sel[:, :, :], ALU.mult))
        dve.wait_ge(pos_ready, 1)
        chain.link(nc.vector.tensor_scalar(tiles[:, :], counts, 1.0 / P, 0.5 - 0.5 / P, ALU.mult, ALU.add))
        chain.link(nc.vector.tensor_scalar(tiles[:, :], tiles[:, :], MAGIC, MAGIC, ALU.add, ALU.subtract))
        chain.link(nc.vector.tensor_tensor_scan(ends[:, :], tiles[:, :], tiles[:, :], 0.0, ALU.add, ALU.bypass))
        chain.link(nc.vector.tensor_tensor(start[:, :], ends[:, :], tiles[:, :], ALU.subtract))
        chain.link(nc.vector.tensor_scalar(start[:, :], start[:, :], float(P), None, ALU.mult))
        chain.link(nc.vector.tensor_tensor(sel[:, :, :], pos.rearrange("p (b e) -> p b e", e=E),
                                           start[:, :].unsqueeze(1).to_broadcast([P, B, E]), ALU.add))
        for source, out in ((sel, slot_f[:, :]), (value, weight[:, :, :].rearrange("p k b -> p (k b)"))):
            for k in range(K):
                ins = nc.vector.scalar_tensor_tensor(of_pick[:, k, :, :], pick[:, :, :], float(k + 1), source[:, :, :],
                                                     ALU.is_equal, ALU.mult)
            chain.link(ins)
            chain.link(nc.vector.tensor_reduce(out, of_pick[:, :, :, :].rearrange("p k b e -> p (k b) e"), AX.X, ALU.add))
            if source is sel:
                nc.vector.tensor_copy(slot[:, :, :].rearrange("p k b -> p (k b)"), slot_f[:, :]).then_inc(picked, 1)
        chain.link(nc.vector.tensor_tensor(past[:, :, :], ends[0:1, :].unsqueeze(1).to_broadcast([1, N, E]),
                                           g.tile_numbers[0:1, :].unsqueeze(2).to_broadcast([1, N, E]), ALU.is_le))
        chain.link(nc.vector.tensor_reduce(expert[:, :], past[:, :, :], AX.X, ALU.add))
        nc.vector.tensor_scalar(expert_of_tile[:, :], expert[:, :], float(E - 1), None, ALU.min).then_inc(experts_known, 1)

    return act_part, pe_part, dve_part


def sorted_mixture(nc, g, a, cfg, w, slots):
    E, K, M, N, BY_POOL = cfg.routed, cfg.top, cfg.chunks, slots.tiles, 4
    assert N % 2 and E % 2 == 0
    with Stage(nc, cfg.name) as st:
        means_ready, rstd_ready = st.sem("means_ready"), st.sem("rstd_ready")
        z_ready, z_turned, zT_ready = st.sem("z_ready"), st.sem("z_turned"), st.sem("zT_ready")
        logits_ready, picked, experts_known = st.sem("logits_ready"), st.sem("picked"), st.sem("experts_known")
        scattered, added = st.sem("scattered"), st.sem("added")
        gathered = [st.sem(f"gathered{k}") for k in range(B // K)]
        rows_in, y_stored = ([st.sem(f"{n}{k}") for k in range(2)] for n in ("rows_in", "y_stored"))
        base_in, w_in = st.sem("base_in"), st.sem("w_in")
        b_gu_ready, b_silu_ready, b_h_ready, b_y_ready, b_y_read = (
            st.sem(f"base_{n}") for n in ("gu_ready", "silu_ready", "h_ready", "y_ready", "y_read"))
        turned, rowsT_ready, gu_ready, silu_ready, h_ready, h_turned, hT_ready, y_ready, y_copied = (
            st.sem(n) for n in ("turned", "rowsT_ready", "gu_ready", "silu_ready", "h_ready", "h_turned", "hT_ready",
                                "y_ready", "y_copied"))
        stats_done = st.sem("stats_done")
        Z = st.sb("Z", [P, B, D])
        gate_up, down = st.sb("gate_up", [P, E, DC, 2, cfg.inner]), st.sb("down", [P, E, M, D])
        b_gate_up, b_down = st.sb("base_gate_up", [P, DC, 2, cfg.inner]), st.sb("base_down", [P, M, D])
        b_h = st.sb("base_h", [P, 2, M, 512])
        rows, rowsT = st.sb("rows", [P, 2, D]), st.sb("rowsT", [P, 2, DC, P])
        silu, up = st.sb("silu", [P, 2, 512]), st.sb("up", [P, 2, 512])
        h, hT, y = st.sb("h", [P, 2, M * P]), st.sb("hT", [P, 2, M * P]), st.sb("y", [P, 2, D])
        got = Z[:, :, :].rearrange("p (k t) d -> p k t d", k=K)
        slot, weight = st.sb("slot", [P, K, B], U32), st.sb("weight", [P, K, B])
        expert_of_tile = st.sb("expert_of_tile", [1, N], I32)
        ps_t = st.ps("ps_t", [P, 2, 512])
        ps_gu = st.ps("ps_gu", [P, 2, 2, 512])
        ps_y = st.ps("ps_y", [P, 2, 512])
        logits, pos, counts = ps_y[:, 0, 0:B * E], ps_y[:, 1, 0:B * E], ps_y[:, 1, B * E:(B + 1) * E]
        r_act, r_pe, r_dve = route_to_experts(nc, st, g, cfg, slots, pos, counts, slot, weight, expert_of_tile)

        gate_up_flat = gate_up[:, :, :, :, :].rearrange("p e c g i -> p (e c g i)")
        down_flat = down[:, :, :, :].rearrange("p e m d -> p (e m d)")

        def gate_up_at(e, c, which):
            return gate_up_flat[:, bass.ds(e * (DC * 2 * cfg.inner) + (c * 2 + which) * cfg.inner, cfg.inner)]

        def down_at(e, m):
            return down_flat[:, bass.ds(e * (M * D) + m * D, D)]

        def steps(eng, step):
            step(0, 0, True, False)
            step(1, 1, False, False)
            step(2, 0, False, False)
            with eng.Fori(0, (N - 5) // 2) as i:
                for k in (1, 0):
                    step(i * 2 + (4 - k), k, False, False)
            step(N - 2, (N - 2) % 2, False, False)
            step(N - 1, (N - 1) % 2, False, True)

        def row_block(t, n):
            return t[n * P:(n + 1) * P, :] if isinstance(n, int) else t[bass.ds(n * P, P), :]

        with nc.Block(no_gpsimd_drain=True) as block:

            @block.sync
            def _(sp):
                sp.dma_start(b_gate_up[:, :, :, :], w.gate_up[E].rearrange("(c p) g i -> p c g i", p=P)
                             ).then_inc(base_in, 16)
                sp.dma_start(b_down[:, :, :], w.down[E].rearrange("(m p) d -> p m d", p=P)).then_inc(base_in, 16)
                for e in range(E):
                    sp.dma_start(gate_up[:, e, :, :, :], w.gate_up[e].rearrange("(c p) g i -> p c g i", p=P)
                                 ).then_inc(w_in, 16)
                    sp.dma_start(down[:, e, :, :], w.down[e].rearrange("(m p) d -> p m d", p=P)).then_inc(w_in, 16)
                sp.wait_ge(scattered, 16 * K * B)
                for n in range(2):
                    sp.dma_start(rows[:, n, :], row_block(slots.z, n)).then_inc(rows_in[n], 16)

                def store_rows(n, k):
                    sp.wait_ge(y_copied, n + 1)
                    sp.dma_start(row_block(slots.y, n), y[:, k, :]).then_inc(y_stored[k], 16)

                def step(n, k, first, last):
                    if not (first or last):
                        sp.wait_ge(turned, n)
                        sp.dma_start(rows[:, 1 - k, :], row_block(slots.z, n + 1)).then_inc(rows_in[1 - k], 16)
                    if not isinstance(n, int) or n >= 2:
                        store_rows(n - 2, k)

                steps(sp, step)
                for n in (N - 2, N - 1):
                    store_rows(n, n % 2)

            def base_inner(eng, on, j):
                eng.wait_ge(b_silu_ready, j + 1)
                if j:
                    eng.wait_ge(b_h_ready, j)
                on.tensor_tensor(b_h[:, j // M, j % M, :], silu[:, j % 2, :], up[:, j % 2, :], ALU.mult
                                 ).then_inc(b_h_ready, 1)

            @block.gpsimd
            def _(pool):
                rstd_of_all(nc, pool, g, means_ready, rstd_ready)
                for j in range(BY_POOL):
                    base_inner(pool, nc.gpsimd, j)
                pool.wait_ge(z_ready, B)
                pool.wait_ge(picked, 1)
                for b in range(B):
                    for k in range(K):
                        pool.indirect_dma_start(slots.z, bass.IndirectOffsetOnAxis(slot[:, k, b:b + 1], 0), Z[:, b, :],
                                                None, bounds_check=slots.rows - 1, oob_is_err=False
                                                ).then_inc(scattered, 16)
                pool.wait_ge(y_stored[0], 16 * ((N + 1) // 2))
                pool.wait_ge(y_stored[1], 16 * (N // 2))
                for b in range(B):
                    if b >= B // K:
                        pool.wait_ge(added, (b - B // K + 1) * K)
                    for k in range(K):
                        pool.indirect_dma_start(got[:, k, b % (B // K), :], None, slots.y,
                                                bass.IndirectOffsetOnAxis(slot[:, k, b:b + 1], 0),
                                                ).then_inc(gathered[b % (B // K)], 16)

            @block.tensor
            def _(pe):
                for b in range(B):
                    pe.wait_ge(z_ready, b + 1)
                    if b >= 2:
                        pe.wait_ge(zT_ready, b - 1)
                    for c in range(DC):
                        mm = nc.tensor.transpose(ps_t[:, b % 2, c * P:(c + 1) * P], Z[:, b, c * P:(c + 1) * P],
                                                 g.ident[:, :])
                    mm.then_inc(z_turned, 1)
                pe.wait_ge(zT_ready, B)
                pe.wait_ge(w.router_landed, 16)
                for b in range(B):
                    for c in range(DC):
                        mm = nc.tensor.matmul(logits[:, b * E:(b + 1) * E], g.zT[:, c, b, :], w.router[:, c, :],
                                              start=(c == 0), stop=(c == DC - 1))
                mm.then_inc(logits_ready, 1)
                pe.wait_ge(base_in, 32)
                for j in range(2 * M):
                    half, m = j // M, j % M
                    if j == 1:
                        r_pe(pe)
                    if j >= 2:
                        pe.wait_ge(b_silu_ready, j - 1)
                    for which in range(2):
                        for c in range(DC):
                            mm = nc.tensor.matmul(ps_gu[:, j % 2, which, :], b_gate_up[:, c, which, m * P:(m + 1) * P],
                                                  g.zT[:, c, half * 4:half * 4 + 4, :].rearrange("p b s -> p (b s)"),
                                                  start=(c == 0), stop=(c == DC - 1))
                    mm.then_inc(b_gu_ready, 1)
                pe.wait_ge(experts_known, 1)
                for t in range(B):
                    pe.wait_ge(b_h_ready, (t // 4 + 1) * M)
                    if t >= 2:
                        pe.wait_ge(b_y_read, t - 1)
                    for m in range(M):
                        mm = nc.tensor.matmul(ps_y[:, t % 2, 0:D], b_h[:, t // 4, m, (t % 4) * P:(t % 4 + 1) * P],
                                              b_down[:, m, :], start=(m == 0), stop=(m == M - 1))
                    mm.then_inc(b_y_ready, 1)
                pe.wait_ge(b_y_read, B)
                pe.wait_ge(b_silu_ready, 2 * M)
                pe.wait_ge(w_in, 32 * E)

                ps_rows, ps_h = ps_t[:, 0, :], ps_t[:, 1, :]

                def turn_rows(n, k):
                    pe.wait_ge(rows_in[k], (n - k) * 8 + 16)
                    if not isinstance(n, int) or n >= 1:
                        pe.wait_ge(rowsT_ready, n)
                    for c in range(DC):
                        mm = nc.tensor.transpose(ps_rows[:, c * P:(c + 1) * P], rows[:, k, c * P:(c + 1) * P], g.ident[:, :])
                    mm.then_inc(turned, 1)

                def turn_h(n, k):
                    pe.wait_ge(h_ready, n + 1)
                    if not isinstance(n, int) or n >= 1:
                        pe.wait_ge(hT_ready, n)
                    for m in range(M):
                        mm = nc.tensor.transpose(ps_h[:, m * P:(m + 1) * P], h[:, k, m * P:(m + 1) * P], g.ident[:, :])
                    mm.then_inc(h_turned, 1)

                def expert_of(n):
                    at = expert_of_tile[0:1, n:n + 1] if isinstance(n, int) else expert_of_tile[0:1, bass.ds(n, 1)]
                    return pe.value_load(at, min_val=0, max_val=E - 1)

                def inner(n, k, e):
                    pe.wait_ge(rowsT_ready, n + 1)
                    if not isinstance(n, int) or n >= 2:
                        pe.wait_ge(h_ready, n - 1)
                    for which in range(2):
                        for c in range(DC):
                            mm = nc.tensor.matmul(ps_gu[:, k, which, :], rowsT[:, k, c, :], gate_up_at(e, c, which),
                                                  start=(c == 0), stop=(c == DC - 1))
                    mm.then_inc(gu_ready, 1)

                def outer(n, k, e):
                    pe.wait_ge(hT_ready, n + 1)
                    if not isinstance(n, int) or n >= 2:
                        pe.wait_ge(y_copied, n - 1)
                    for m in range(M):
                        mm = nc.tensor.matmul(ps_y[:, k, 0:D], hT[:, k, m * P:(m + 1) * P], down_at(e, m),
                                              start=(m == 0), stop=(m == M - 1))
                    mm.then_inc(y_ready, 1)

                def step(n, k, first, last):
                    if not first:
                        turn_h(n - 1, 1 - k)
                    if not last:
                        turn_rows(n + 1, 1 - k)
                    inner(n, k, expert_of(n))
                    if not first:
                        outer(n - 1, 1 - k, expert_of(n - 1))

                turn_rows(0, 0)
                steps(pe, step)
                turn_h(N - 1, (N - 1) % 2)
                outer(N - 1, (N - 1) % 2, expert_of(N - 1))

            @block.scalar
            def _(act):
                for b in range(B):
                    act.wait_ge(z_turned, b + 1)
                    nc.scalar.copy(g.zT[:, :, b, :], ps_t[:, b % 2, 0:D].rearrange("p (c s) -> p c s", c=DC)
                                   ).then_inc(zT_ready, 1)
                r_act(act)
                for j in range(2 * M):
                    act.wait_ge(b_gu_ready, j + 1)
                    if j >= 2:
                        act.wait_ge(b_h_ready, j - 1)
                    nc.scalar.activation(silu[:, j % 2, :], ps_gu[:, j % 2, 0, :], ACT.Silu)
                    nc.scalar.copy(up[:, j % 2, :], ps_gu[:, j % 2, 1, :]).then_inc(b_silu_ready, 1)
                act.wait_ge(b_h_ready, 2 * M)

                def rows_out(n, k):
                    act.wait_ge(turned, n + 1)
                    if not isinstance(n, int) or n >= 2:
                        act.wait_ge(gu_ready, n - 1)
                    nc.scalar.copy(rowsT[:, k, :, :].rearrange("p c s -> p (c s)"), ps_t[:, 0, 0:D]).then_inc(rowsT_ready, 1)

                def h_out(n, k):
                    act.wait_ge(h_turned, n + 1)
                    if not isinstance(n, int) or n >= 2:
                        act.wait_ge(y_ready, n - 1)
                    nc.scalar.copy(hT[:, k, :], ps_t[:, 1, :]).then_inc(hT_ready, 1)

                def step(n, k, first, last):
                    if not last:
                        rows_out(n + 1, 1 - k)
                    if not first:
                        h_out(n - 1, 1 - k)
                    act.wait_ge(gu_ready, n + 1)
                    if not isinstance(n, int) or n >= 2:
                        act.wait_ge(h_ready, n - 1)
                    nc.scalar.activation(silu[:, k, :], ps_gu[:, k, 0, :], ACT.Silu).then_inc(silu_ready, 1)

                rows_out(0, 0)
                steps(act, step)
                h_out(N - 1, (N - 1) % 2)

            @block.vector
            def _(dve):
                means_of_all(nc, g, means_ready)
                dve.wait_ge(rstd_ready, 2)
                for b in range(B):
                    nc.vector.tensor_scalar(Z[:, b, :], g.X[:, b, :], g.mv[:, b, 0:1], g.rstd[:, b:b + 1],
                                            ALU.subtract, ALU.mult).then_inc(z_ready, 1)
                dve.wait_ge(g.earlier_in, 64)
                dve.wait_ge(logits_ready, 1)
                r_dve(dve, logits.rearrange("p (b e) -> p b e", e=E), picked, experts_known)
                for j in range(BY_POOL, 2 * M):
                    base_inner(dve, nc.vector, j)
                for t in range(B):
                    dve.wait_ge(b_y_ready, t + 1)
                    nc.vector.tensor_tensor(g.X[:, t, :], g.X[:, t, :], ps_y[:, t % 2, 0:D], ALU.add
                                            ).then_inc(b_y_read, 1)

                def copy_out(n, k):
                    dve.wait_ge(y_ready, n + 1)
                    if not isinstance(n, int) or n >= 2:
                        dve.wait_ge(y_stored[k], (n - k) * 8)
                    nc.vector.tensor_copy(y[:, k, :], ps_y[:, k, 0:D]).then_inc(y_copied, 1)

                def step(n, k, first, last):
                    dve.wait_ge(silu_ready, n + 1)
                    if not isinstance(n, int) or n >= 2:
                        dve.wait_ge(h_turned, n - 1)
                    nc.vector.tensor_tensor(h[:, k, :], silu[:, k, :], ps_gu[:, k, 1, :],
                                            ALU.mult).then_inc(h_ready, 1)
                    if not first:
                        copy_out(n - 1, 1 - k)

                steps(dve, step)
                copy_out(N - 1, (N - 1) % 2)
                dve.wait_ge(b_y_read, B)
                for b in range(B):
                    dve.wait_ge(gathered[b % (B // K)], 16 * K * (b // (B // K) + 1))
                    for k in range(K):
                        if k:
                            dve.wait_ge(added, b * K + k)
                        nc.vector.scalar_tensor_tensor(g.X[:, b, :], got[:, k, b % (B // K), :], weight[:, k, b:b + 1],
                                                       g.X[:, b, :], ALU.mult, ALU.add).then_inc(added, 1)
                    dve.wait_ge(added, (b + 1) * K)
                    ins = stats_of(nc, g, b)
                ins.then_inc(stats_done, 1)
                dve.wait_ge(stats_done, 1)


def capacity_mixture(nc, g, a, cfg, w, slots, clip, total_scale):
    E, K, GROUP, WSLOTS = cfg.routed, cfg.top, 4, 3
    G, C = E // GROUP, slots.capacity
    with Stage(nc, cfg.name) as st:
        means_ready, rstd_ready = st.sem("means_ready"), st.sem("rstd_ready")
        z_ready, z_turned, zT_ready = st.sem("z_ready"), st.sem("z_turned"), st.sem("zT_ready")
        logits_ready, picked = st.sem("logits_ready"), st.sem("picked")
        scattered = st.sem("scattered")
        rows_in = [st.sem(f"rows_in{k}") for k in range(2)]
        w_in = [st.sem(f"w_in{k}") for k in range(WSLOTS)]
        shared_in = st.sem("shared_in")
        gathered = [st.sem(f"gathered{k}") for k in range(GATHERS)]
        s_gu_ready, s_silu_ready, s_clip, s_h_ready, s_y_ready, s_y_read = (
            st.sem(f"shared_{n}") for n in ("gu_ready", "silu_ready", "clip", "h_ready", "y_ready", "y_read"))
        turned, rowsT_ready, gu_ready, silu_ready, h_ready, y_ready, y_copied = (
            st.sem(n) for n in ("turned", "rowsT_ready", "gu_ready", "silu_ready", "h_ready", "y_ready", "y_copied"))
        y_stored = [st.sem(f"y_stored{k}") for k in range(2)]
        added, stats_done = st.sem("added"), st.sem("stats_done")
        Z = st.sb("Z", [P, B, D])
        gate_up = st.sb("gate_up", [P, WSLOTS, GROUP, DC, 2 * P])
        down = st.sb("down", [P, WSLOTS, GROUP, D])
        s_gate_up, s_down = st.sb("shared_gate_up", [P, DC, 2, P]), st.sb("shared_down", [P, D])
        s_silu, s_h = st.sb("shared_silu", [P, 2, 512]), st.sb("shared_h", [P, 2, 512])
        rows = st.sb("rows", [C, 2, GROUP, D])
        rowsT = st.sb("rowsT", [P, 2, DC, GROUP * C])
        silu, h = st.sb("silu", [P, 2, GROUP * C]), st.sb("h", [P, 2, GROUP * C])
        y = st.sb("y", [C, 2, GROUP, D])
        got = gate_up[:, :, :, :, :].rearrange("p w e c i -> p (w e c i)")[:, 0:GATHERS * K * D].rearrange(
            "p (n k d) -> p n k d", n=GATHERS, k=K)
        slot, weight = st.sb("slot", [P, K, B], U32), st.sb("weight", [P, K, B])
        ps_t = st.ps("ps_t", [P, 2, 512])
        ps_gu = st.ps("ps_gu", [P, 2, 2, 512])
        ps_y = st.ps("ps_y", [P, 2, 512])
        logits, pos = ps_y[:, 0, 0:B * E], ps_y[:, 1, 0:B * E]
        r_act, r_pe, r_dve = route_with_capacity(nc, st, g, cfg, pos, slots, slot, weight, total_scale)

        with nc.Block(no_gpsimd_drain=True) as block:

            @block.sync
            def _(sp):
                sp.dma_start(s_gate_up[:, :, :, :], w.gate_up[E].rearrange("(c p) g i -> p c g i", p=P)
                             ).then_inc(shared_in, 16)
                sp.dma_start(s_down[:, :], w.down[E]).then_inc(shared_in, 16)

                def load_weights(n):
                    if n >= WSLOTS:
                        sp.wait_ge(y_ready, n - WSLOTS + 1)
                    k, at = n % WSLOTS, slice(n * GROUP, (n + 1) * GROUP)
                    for c in range(DC):
                        sp.dma_start(gate_up[:, k, :, c, :],
                                     w.gate_up[at, c * P:(c + 1) * P].rearrange("e p g i -> p e (g i)")
                                     ).then_inc(w_in[k], 16)
                    sp.dma_start(down[:, k, :, :], w.down[at].rearrange("e p d -> p e d")).then_inc(w_in[k], 16)

                def load_rows(n):
                    if n >= 2:
                        sp.wait_ge(turned, n - 1)
                    sp.dma_start(rows[:, n % 2, :, :], slots.z[n * GROUP * C:(n + 1) * GROUP * C, :]
                                 .rearrange("(e s) d -> s e d", s=C)).then_inc(rows_in[n % 2], 16)

                for n in range(WSLOTS):
                    load_weights(n)
                sp.wait_ge(scattered, 16 * K * B)
                load_rows(0)
                load_rows(1)
                for n in range(G):
                    if n + 2 < G:
                        load_rows(n + 2)
                    if n + WSLOTS < G:
                        load_weights(n + WSLOTS)

            @block.gpsimd
            def _(pool):
                rstd_of_all(nc, pool, g, means_ready, rstd_ready)
                pool.wait_ge(z_ready, B)
                pool.wait_ge(picked, 1)
                for b in range(B):
                    for k in range(K):
                        pool.indirect_dma_start(slots.z, bass.IndirectOffsetOnAxis(slot[:, k, b:b + 1], 0), Z[:, b, :],
                                                None, bounds_check=slots.rows - 1, oob_is_err=False
                                                ).then_inc(scattered, 16)
                for k in range(2):
                    pool.wait_ge(y_stored[k], 16 * (G // 2))
                for b in range(B):
                    if b >= GATHERS:
                        pool.wait_ge(added, (b - GATHERS + 1) * K)
                    for k in range(K):
                        pool.indirect_dma_start(got[:, b % GATHERS, k, :], None, slots.y,
                                                bass.IndirectOffsetOnAxis(slot[:, k, b:b + 1], 0),
                                                ).then_inc(gathered[b % GATHERS], 16)

            @block.tensor
            def _(pe):
                for b in range(B):
                    pe.wait_ge(z_ready, b + 1)
                    if b >= 2:
                        pe.wait_ge(zT_ready, b - 1)
                    for c in range(DC):
                        mm = nc.tensor.transpose(ps_t[:, b % 2, c * P:(c + 1) * P], Z[:, b, c * P:(c + 1) * P],
                                                 g.ident[:, :])
                    mm.then_inc(z_turned, 1)
                pe.wait_ge(zT_ready, B)
                pe.wait_ge(w.router_landed, 16)
                for b in range(B):
                    for c in range(DC):
                        mm = nc.tensor.matmul(logits[:, b * E:(b + 1) * E], g.zT[:, c, b, :], w.router[:, c, :],
                                              start=(c == 0), stop=(c == DC - 1))
                mm.then_inc(logits_ready, 1)
                pe.wait_ge(shared_in, 32)
                for half in range(2):
                    for which in range(2):
                        for c in range(DC):
                            mm = nc.tensor.matmul(ps_gu[:, half, which, :], s_gate_up[:, c, which, :],
                                                  g.zT[:, c, half * 4:half * 4 + 4, :].rearrange("p b s -> p (b s)"),
                                                  start=(c == 0), stop=(c == DC - 1))
                    mm.then_inc(s_gu_ready, 1)
                r_pe(pe)
                pe.wait_ge(picked, 1)
                for t in range(B):
                    pe.wait_ge(s_h_ready, t // 4 + 1)
                    if t >= 2:
                        pe.wait_ge(s_y_read, t - 1)
                    nc.tensor.matmul(ps_y[:, t % 2, 0:D], s_h[:, t // 4, (t % 4) * P:(t % 4 + 1) * P], s_down[:, :],
                                     start=True, stop=True).then_inc(s_y_ready, 1)

                def turn(n):
                    pe.wait_ge(rows_in[n % 2], 16 * (n // 2 + 1))
                    if n >= 1:
                        pe.wait_ge(rowsT_ready, n)
                    for c in range(DC):
                        for j in range(GROUP):
                            mm = nc.tensor.transpose(ps_t[:, c, j * C:(j + 1) * C],
                                                     rows[:, n % 2, j, c * P:(c + 1) * P], g.ident[0:C, 0:C])
                    mm.then_inc(turned, 1)

                def inner(n):
                    pe.wait_ge(w_in[n % WSLOTS], 48 * (n // WSLOTS + 1))
                    pe.wait_ge(rowsT_ready, n + 1)
                    if n >= 2:
                        pe.wait_ge(h_ready, n - 1)
                    else:
                        pe.wait_ge(s_h_ready, 2)
                    for j in range(GROUP):
                        for which in range(2):
                            for c in range(DC):
                                mm = nc.tensor.matmul(ps_gu[:, n % 2, which, j * C:(j + 1) * C],
                                                      gate_up[:, n % WSLOTS, j, c, which * P:(which + 1) * P],
                                                      rowsT[:, n % 2, c, j * C:(j + 1) * C],
                                                      start=(c == 0), stop=(c == DC - 1))
                    mm.then_inc(gu_ready, 1)

                def outer(n):
                    pe.wait_ge(h_ready, n + 1)
                    if n >= 1:
                        pe.wait_ge(y_copied, n)
                    else:
                        pe.wait_ge(s_y_read, B)
                    for j in range(GROUP):
                        mm = nc.tensor.matmul(ps_y[0:C, j // 2, (j % 2) * D:(j % 2 + 1) * D],
                                              h[:, n % 2, j * C:(j + 1) * C], down[:, n % WSLOTS, j, :],
                                              start=True, stop=True)
                    mm.then_inc(y_ready, 1)

                turn(0)
                for n in range(G):
                    inner(n)
                    if n + 1 < G:
                        turn(n + 1)
                    outer(n)

            @block.scalar
            def _(act):
                for b in range(B):
                    act.wait_ge(z_turned, b + 1)
                    nc.scalar.copy(g.zT[:, :, b, :], ps_t[:, b % 2, 0:D].rearrange("p (c s) -> p c s", c=DC)
                                   ).then_inc(zT_ready, 1)
                def store_rows(n):
                    act.wait_ge(y_copied, n + 1)
                    act.dma_start(slots.y[n * GROUP * C:(n + 1) * GROUP * C, :].rearrange("(e s) d -> s e d", s=C),
                                  y[:, n % 2, :, :]).then_inc(y_stored[n % 2], 16)

                r_act(act)
                for half in range(2):
                    act.wait_ge(s_gu_ready, half + 1)
                    nc.scalar.activation(s_silu[:, half, :], ps_gu[:, half, 0, :], ACT.Silu).then_inc(s_silu_ready, 1)
                for n in range(G):
                    act.wait_ge(turned, n + 1)
                    if n >= 2:
                        act.wait_ge(gu_ready, n - 1)
                    nc.scalar.copy(rowsT[:, n % 2, :, :], ps_t[:, :, 0:GROUP * C]).then_inc(rowsT_ready, 1)
                    act.wait_ge(gu_ready, n + 1)
                    if n >= 2:
                        act.wait_ge(h_ready, n - 1)
                    nc.scalar.activation(silu[:, n % 2, :], ps_gu[:, n % 2, 0, 0:GROUP * C], ACT.Silu
                                         ).then_inc(silu_ready, 1)
                    if n:
                        store_rows(n - 1)
                store_rows(G - 1)

            @block.vector
            def _(dve):
                means_of_all(nc, g, means_ready)
                dve.wait_ge(rstd_ready, 2)
                for b in range(B):
                    nc.vector.tensor_scalar(Z[:, b, :], g.X[:, b, :], g.mv[:, b, 0:1], g.rstd[:, b:b + 1],
                                            ALU.subtract, ALU.mult).then_inc(z_ready, 1)
                dve.wait_ge(g.earlier_in, 64)
                dve.wait_ge(logits_ready, 1)
                r_dve(dve, logits.rearrange("p (b e) -> p b e", e=E), picked)
                for half in range(2):
                    dve.wait_ge(s_silu_ready, half + 1)
                    nc.vector.tensor_tensor(s_h[:, half, :], s_silu[:, half, :], ps_gu[:, half, 1, :], ALU.mult
                                            ).then_inc(s_clip, 1)
                    dve.wait_ge(s_clip, half + 1)
                    nc.vector.tensor_scalar(s_h[:, half, :], s_h[:, half, :], -clip, clip, ALU.max, ALU.min
                                            ).then_inc(s_h_ready, 1)
                for t in range(B):
                    dve.wait_ge(s_y_ready, t + 1)
                    nc.vector.tensor_tensor(g.X[:, t, :], g.X[:, t, :], ps_y[:, t % 2, 0:D], ALU.add
                                            ).then_inc(s_y_read, 1)
                for n in range(G):
                    dve.wait_ge(silu_ready, n + 1)
                    if n >= 2:
                        dve.wait_ge(y_ready, n - 1)
                    nc.vector.tensor_tensor(h[:, n % 2, :], silu[:, n % 2, :], ps_gu[:, n % 2, 1, 0:GROUP * C], ALU.mult
                                            ).then_inc(h_ready, 1)
                    dve.wait_ge(y_ready, n + 1)
                    if n >= 2:
                        dve.wait_ge(y_stored[n % 2], 16 * (n // 2))
                    nc.vector.tensor_copy(y[:, n % 2, :, :].rearrange("p (u v) d -> p u (v d)", u=2),
                                          ps_y[0:C, :, :]).then_inc(y_copied, 1)
                dve.wait_ge(s_y_read, B)
                for b in range(B):
                    dve.wait_ge(gathered[b % GATHERS], 16 * K * (b // GATHERS + 1))
                    for k in range(K):
                        if k:
                            dve.wait_ge(added, b * K + k)
                        nc.vector.scalar_tensor_tensor(g.X[:, b, :], got[:, b % GATHERS, k, :], weight[:, k, b:b + 1],
                                                       g.X[:, b, :], ALU.mult, ALU.add).then_inc(added, 1)
                    dve.wait_ge(added, (b + 1) * K)
                    ins = stats_of(nc, g, b)
                ins.then_inc(stats_done, 1)
                dve.wait_ge(stats_done, 1)

def cosine_attention(nc, g, a):
    HEADS, R, ALPHA, EPS = 8, S // 8, 5.0, 1e-12
    VW = R + 1
    with Stage(nc, "cos") as st:
        means_ready, rstd_ready, z_ready, squares_ready, norms_ready, roots_ready, rq_ready, rq_turned, rqT_ready = (
            st.sem(n) for n in ("means", "rstd", "z_ready", "squares", "norms", "roots", "rq_ready", "rq_turned", "rqT"))
        spread_ready, qn_ready, slots_ready, s_ready, p_ready, o_ready, on_ready, o_turned, x_done, stats_done = (
            st.sem(n) for n in ("spread", "qn_ready", "slots", "s_ready", "p_ready", "o_ready", "on_ready", "o_turned",
                                "x_done", "stats_done"))
        sem_c, sem_t, ones_set, pool_sem = st.sem("chain"), st.sem("chain_tail"), st.sem("ones_set"), st.sem("pool_chain")
        Z = st.sb("Z", [P, B, D])
        zz, cc = st.sb("zz", [P, B, D]), st.sb("cc", [P, B, D])
        root = st.sb("root", [P, 2, DC * B * HEADS])
        rk, rq = st.sb("rk", [P, DC, B, HEADS]), st.sb("rq", [P, DC, B * HEADS])
        rqT = st.sb("rqT", [B * HEADS, D])
        ks, qs = st.sb("ks", [P, 2, 2, D]), st.sb("qs", [P, 2, D])
        vs = st.sb("vs", [P, 2, DC, HEADS, VW])
        e = st.sb("e", [P, 4, DC, D])
        rec = st.sb("rec", [P, 2, DC * HEADS])
        on = st.sb("on", [P, 2, DC, S])
        ps_s = st.ps("ps_s", [P, 4, 512])
        ps_o = st.ps("ps_o", [P, 2, 512])
        ps_t = st.ps("ps_t", [P, 2, 512])
        N = DC * B * HEADS

        def steps(eng, step):
            step(0, 0, True, False)
            with eng.Fori(0, (B - 2) // 2) as i:
                for k in range(2):
                    step(i * 2 + 1 + k, (1 + k) % 2, False, False)
            step(B - 1, (B - 1) % 2, False, True)

        def wait_past(eng, sem, value):
            if not isinstance(value, int) or value > 0:
                eng.wait_ge(sem, value)

        with nc.Block(no_gpsimd_drain=True) as block:

            @block.gpsimd
            def _(pool):
                rstd_of_all(nc, pool, g, means_ready, rstd_ready)
                for k in range(2):
                    ins = nc.gpsimd.memset(vs[:, k, :, :, R:VW], 1.0)
                ins.then_inc(ones_set, 1)
                pool.wait_ge(ones_set, 1)
                pool.wait_ge(g.cos_in, 48)

                def slots(b, k):
                    wait_past(pool, o_ready, b - 1)
                    for c in range(DC):
                        nc.gpsimd.tensor_copy(vs[:, k, c, :, 0:R],
                                              g.ctxT[:, c, b, :].rearrange("p (h r) -> p h r", r=R))
                    for odd in range(2):
                        nc.gpsimd.tensor_tensor(ks[:, k, odd, :], g.ctx[:, b, :],
                                                g.odd_heads[:, odd:odd + 1].to_broadcast([P, D]), ALU.mult)
                    if isinstance(b, int) and b == 0:
                        pool.wait_ge(qn_ready, B)
                    nc.gpsimd.tensor_copy(qs[:, k, :], Z[:, b, :]).then_inc(slots_ready, 1)

                def step(b, k, first, last):
                    if first:
                        slots(b, k)
                    if not last:
                        slots(b + 1, 1 - k)

                steps(pool, step)

            @block.tensor
            def _(pe):
                pe.wait_ge(g.cos_in, 48)
                pe.wait_ge(squares_ready, 2)
                for which, sq in ((0, cc), (1, zz)):
                    for c in range(DC):
                        for b in range(B):
                            col = which * N + (c * B + b) * HEADS
                            mm = nc.tensor.matmul(ps_t[:, 0, col:col + HEADS], sq[:, b, c * P:(c + 1) * P],
                                                  g.head_of_row[:, :], start=True, stop=True)
                mm.then_inc(norms_ready, 1)
                pe.wait_ge(rq_ready, 1)
                for c in range(DC):
                    mm = nc.tensor.transpose(ps_t[0:B * HEADS, 1, c * P:(c + 1) * P], rq[:, c, :], g.ident[:, :])
                mm.then_inc(rq_turned, 1)
                pe.wait_ge(rqT_ready, 1)
                for b in range(B):
                    if b >= 4:
                        pe.wait_ge(qn_ready, b - 3)
                    nc.tensor.matmul(ps_s[:, b % 4, 0:D], g.spread_heads[:, b, :], rqT[:, :], start=True, stop=True
                                     ).then_inc(spread_ready, 1)
                pe.wait_ge(qn_ready, B)

                def scores(b, k, u):
                    n = b * HEADS + u + 1
                    if u == 0:
                        pe.wait_ge(slots_ready, b + 1)
                    wait_past(pe, p_ready, n - 4)
                    r0 = u // 2 * 2 * R
                    for c in range(DC):
                        mm = nc.tensor.matmul(ps_s[:, u % 4, c * D:(c + 1) * D], ks[r0:r0 + 2 * R, k, u % 2, c * P:(c + 1) * P],
                                              qs[r0:r0 + 2 * R, k, :], start=True, stop=True)
                    mm.then_inc(s_ready, 1)

                def values(b, k, u):
                    pe.wait_ge(p_ready, b * HEADS + u + 1)
                    if u == 0:
                        wait_past(pe, on_ready, b - 1)
                    for qc in range(DC):
                        for c in range(DC):
                            col = (qc * HEADS + u) * VW
                            mm = nc.tensor.matmul(ps_o[:, k, col:col + VW], e[:, u % 4, c, qc * P:(qc + 1) * P],
                                                  vs[:, k, c, u, :], start=(c == 0), stop=(c == DC - 1))
                    if u == HEADS - 1:
                        mm.then_inc(o_ready, 1)

                def turn_output(b, k):
                    pe.wait_ge(on_ready, b + 1)
                    for c in range(DC):
                        mm = nc.tensor.transpose(ps_t[:, k, c * P:(c + 1) * P], on[:, k, c, :], g.ident[:, :])
                    mm.then_inc(o_turned, 1)

                def step(b, k, first, last):
                    for u in range(HEADS):
                        if u + 2 < HEADS:
                            scores(b, k, u + 2)
                        elif not last:
                            scores(b + 1, 1 - k, u + 2 - HEADS)
                        values(b, k, u)
                        if not first and u == 2:
                            turn_output(b - 1, 1 - k)

                scores(0, 0, 0)
                scores(0, 0, 1)
                steps(pe, step)
                turn_output(B - 1, 1)

            @block.scalar
            def _(act):
                act.wait_ge(z_ready, B)
                nc.scalar.activation(cc[:, :, :], g.ctx[:, :, :], ACT.Square).then_inc(squares_ready, 1)
                nc.scalar.activation(zz[:, :, :], Z[:, :, :], ACT.Square).then_inc(squares_ready, 1)
                act.wait_ge(norms_ready, 1)
                nc.scalar.activation(root[:, :, :].rearrange("p w n -> p (w n)"), ps_t[:, 0, 0:2 * N], ACT.Sqrt
                                     ).then_inc(roots_ready, 1)
                act.wait_ge(rq_turned, 1)
                nc.scalar.copy(rqT[:, :], ps_t[0:B * HEADS, 1, 0:D]).then_inc(rqT_ready, 1)
                settled = Settled(act, "cos_act_settled")

                def step(b, k, first, last):
                    for u in range(HEADS):
                        settled.wait_ge(s_ready, b * HEADS + u + 1)
                        for c in range(DC):
                            ins = nc.scalar.activation(e[:, u % 4, c, :], ps_s[:, u % 4, c * D:(c + 1) * D], ACT.Exp,
                                                       scale=rk[:, c, b, u:u + 1])
                        ins.then_inc(p_ready, 1)

                steps(act, step)

            @block.vector
            def _(dve):
                means_of_all(nc, g, means_ready)
                dve.wait_ge(rstd_ready, 2)
                with dve.Fori(0, B) as b:
                    nc.vector.tensor_scalar(Z[:, b, :], g.X[:, b, :], g.mv[:, b, 0:1], g.rstd[:, bass.ds(b, 1)],
                                            ALU.subtract, ALU.mult).then_inc(z_ready, 1)
                chain = Chain(dve, sem_c, 2)
                chain.start(0)
                dve.wait_ge(roots_ready, 1)
                chain.link(nc.vector.tensor_scalar(root[:, :, :], root[:, :, :], EPS, None, ALU.max))
                chain.link(nc.vector.reciprocal(root[:, :, :], root[:, :, :]))
                chain.end()
                nc.vector.tensor_copy(rq[:, :, :].rearrange("p c n -> p (c n)"), root[:, 1, :]).then_inc(rq_ready, 1)
                nc.vector.tensor_scalar(rk[:, :, :, :].rearrange("p c b h -> p (c b h)"), root[:, 0, :], ALPHA, None,
                                        ALU.mult).then_inc(rq_ready, 1)
                for b in range(B):
                    dve.wait_ge(spread_ready, b + 1)
                    nc.vector.tensor_tensor(Z[:, b, :], Z[:, b, :], ps_s[:, b % 4, 0:D], ALU.mult).then_inc(qn_ready, 1)
                tail = Chain(dve, sem_t, 1)
                settled = Settled(dve, "cos_settled")

                def normalise(b, k):
                    dve.wait_ge(o_ready, b + 1)
                    tail.start(b)
                    heads = ps_o[:, k, 0:DC * HEADS * VW].rearrange("p (n w) -> p n w", w=VW)
                    tail.link(nc.vector.reciprocal(rec[:, k, :], heads[:, :, R]))
                    nc.vector.tensor_tensor(on[:, k, :, :].rearrange("p c (h r) -> p (c h) r", r=R), heads[:, :, 0:R],
                                            rec[:, k, :].unsqueeze(2).to_broadcast([P, DC * HEADS, R]), ALU.mult
                                            ).then_inc(on_ready, 1)
                    tail.end()

                def add_output(b, k):
                    dve.wait_ge(o_turned, b + 1)
                    nc.vector.tensor_tensor(g.X[:, b, :], g.X[:, b, :], ps_t[:, k, 0:D], ALU.add).then_inc(x_done, 1)
                    settled.wait_ge(x_done, b + 1)
                    stats_of(nc, g, b).then_inc(stats_done, 1)

                def step(b, k, first, last):
                    normalise(b, k)
                    add_output(b, k)

                steps(dve, step)
                dve.wait_ge(stats_done, B)


def store(nc, g, a):
    with Stage(nc, "store") as st:
        out_done = st.sem("out_done")
        with nc.Block() as block:

            @block.sync
            def _(sp):
                sp.dma_start(a.out.rearrange("b s d -> s b d"), g.X[:, :, :]).then_inc(out_done, 16)
                sp.wait_ge(out_done, 16)


class Names:
    pass


def a_len(a, name):
    return a.by_name[name].shape[0]


def program(nc, a):
    with ExitStack() as ctx:
        g = Names()

        def sb(name, shape, dt=F32):
            return ctx.enter_context(nc.sbuf_tensor(name, shape, dt))

        g.X = sb("X", [P, B, D])
        g.ctx = sb("ctx", [P, B, D])
        g.ctxT = sb("ctxT", [P, DC, B, S])
        g.zT = sb("zT", [P, DC, B, S])
        g.ident = sb("ident", [P, P])
        g.skip = sb("skip", [P, S])
        g.stats = sb("stats", [P, B, 6])
        g.mv = sb("mv", [P, B, 2])
        g.var8 = sb("var8", [P, B])
        g.rstd = sb("rstd", [P, B])
        g.neg_half = sb("neg_half", [P, B])
        g.eps_ff = sb("eps_ff", [P, 1])
        g.ident16 = sb("ident16", [P, P], BF16)
        g.ones = sb("ones", [P, P])
        g.mask_causal_words = sb("mask_causal", [P, P // 4], mybir.dt.int32)
        g.mask_padding_words = sb("mask_padding", [P, B * P // 4], mybir.dt.int32)
        g.mask_causal = g.mask_causal_words[:, :].bitcast(U8)
        g.mask_padding = g.mask_padding_words[:, :].bitcast(U8).rearrange("p (b k) -> p b k", b=B)
        g.m2, g.m3 = Names(), Names()
        for layer, m, e in (("L2", g.m2, 8), ("L3", g.m3, 32)):
            m.gate_up, m.down = a.by_name[f"{layer}_gate_up"], a.by_name[f"{layer}_down"]
            m.router = sb(f"{layer}_router", [P, DC, e])
            m.router_source = a.by_name[f"{layer}_router"].rearrange("(c p) e -> p c e", p=P)
            m.router_landed = nc.alloc_semaphore(f"{layer}_router_in")
        g.earlier, g.earlier16, g.ones16 = sb("earlier", [P, P]), sb("earlier16", [P, P], BF16), sb("ones16", [P, P], BF16)
        g.route_bias, g.slot_base = sb("route_bias", [P, 32]), sb("slot_base", [P, 32])
        g.slots2, g.slots3 = Slots(nc, "moe2", 8, 2), Slots(nc, "moe3", 32, 6, L3_CAPACITY)
        g.tile_numbers = sb("tile_numbers", [1, g.slots2.tiles])
        g.earlier_in = nc.alloc_semaphore("earlier_in")
        g.odd_heads, g.head_of_row = sb("odd_heads", [P, 2]), sb("head_of_row", [P, 8])
        g.spread_heads = sb("spread_heads", [B * 8, B, P])
        g.cos_in = nc.alloc_semaphore("cos_in")
        g.masks_in, g.rows_in, g.head_mask_in = (nc.alloc_semaphore(n) for n in ("masks_in", "rows_in", "head_mask_in"))
        g.b1_in, g.b2_in = nc.alloc_semaphore("b1_in"), nc.alloc_semaphore("b2_in")
        g.const_in = nc.alloc_semaphore("const_in")
        g.skip_in = nc.alloc_semaphore("skip_in")

        def scoped(stack):
            return lambda name, shape, dt=F32: stack.enter_context(nc.sbuf_tensor(name, shape, dt))

        until5 = ctx.enter_context(ExitStack())
        until4 = ctx.enter_context(ExitStack())
        sb5, sb4 = scoped(until5), scoped(until4)
        g.wa1, g.wa2 = Names(), Names()
        ones = ("wq", "wk", "wv", "wo")
        for layer, w, sb in (("L2", g.wa2, sb5), ("L1", g.wa1, sb4)):
            w.weights = {}
            for n in ones:
                src = a.by_name[f"{layer}_{n}"]
                m = w.weights[n] = Names()
                m.tile = sb(f"{layer}_{n}", [P, DC, src.shape[1]])
                m.landed = nc.alloc_semaphore(f"{layer}_{n}_in")
                m.source = src.rearrange("(c p) f -> p c f", p=P)
            w.wq, w.wk, w.wv, w.wo = (w.weights[n] for n in ones)
            w.head_mask = sb(f"{layer}_head_mask", [P, 4])
            w.bq, w.bk = sb(f"{layer}_bq", [P, DC]), sb(f"{layer}_bk", [P, DC])
            w.bv_row, w.bo_row = sb(f"{layer}_bv", [P, a_len(a, f"{layer}_bv")]), sb(f"{layer}_bo", [P, D])
            w.bq_row = sb(f"{layer}_bq_row", [P, D])
        g.b1, g.b2 = sb4("b1", [P, FF]), sb4("b2", [P, D])
        g.w0, g.w1 = [Names(), Names()], [Names(), Names()]
        for layer, w in (("L0", g.w0), ("L1", g.w1)):
            for n, (chunks, width) in enumerate(((DC, FF), (FC, D))):
                w[n].tile = sb4(f"{layer}_ffn_w{n + 1}", [P, chunks, width])
                w[n].flat = w[n].tile[:, :, :].rearrange("p c f -> p (c f)")
                w[n].landed = nc.alloc_semaphore(f"{layer}_ffn_w{n + 1}_in")
                w[n].source = a.by_name[f"{layer}_ffn_w{n + 1}T"].rearrange("(c p) f -> p c f", p=P)
        load_and_prepare(nc, g, a)
        long_convolution(nc, g, a)
        quantised_ffn(nc, g, a, "ffn0", g.w0, False)
        attention(nc, g, a, Attention("att1", 8, 8, 8 ** -0.5, False), g.wa1)
        normed_quantised_ffn(nc, g, a, "ffn1", g.w1)
        until4.close()
        attention(nc, g, a, Attention("att2", 16, 16, 1.0, True), g.wa2)
        until5.close()
        sorted_mixture(nc, g, a, Experts("moe2", 8, 2, 512), g.m2, g.slots2)
        cosine_attention(nc, g, a)
        capacity_mixture(nc, g, a, Experts("moe3", 32, 6, 128), g.m3, g.slots3, 10.0, 1.5)
        store(nc, g, a)


def kernel(**inputs):
    import concourse.bacc as _bacc
    from concourse.bass_utils import run_bass_kernel_spmd as _run

    nc = _bacc.Bacc("TRN2", target_bir_lowering=False, num_devices=1)
    f = {k: np.asarray(v) for k, v in inputs.items()}
    k = f["L0_xattn_k"]
    padded = np.concatenate([np.zeros((CONV_HEADS, P - 1), k.dtype), k], axis=1)
    at = (P - 1) + np.arange(2 * P)[None, :] - np.arange(P)[:, None]
    shared = (np.arange(D) // 8 // 4) * 8 + np.arange(D) % 8
    cols = lambda v: v.reshape(DC, P).T
    head_mask = lambda rows: (np.arange(P)[:, None] // rows % 4 == np.arange(4)[None, :]).astype(np.float32)
    split = lambda gu: gu.reshape(*gu.shape[:-1], 2, gu.shape[-1] // 2)
    both = lambda gate, up: np.stack([np.swapaxes(gate, -1, -2), np.swapaxes(up, -1, -2)], axis=-2)
    joined = lambda routed, shared: np.concatenate([routed, shared[None]], axis=0)
    laid = {
        "L2_gate_up": split(joined(f["L2_ffn_expert_gate_up"], f["L2_ffn_base_gate_up"])),
        "L2_down": joined(f["L2_ffn_expert_down"], f["L2_ffn_base_down"]),
        "L2_router": f["L2_ffn_gate_w"],
        "L3_gate_up": both(joined(f["L3_ffn_w_gate"], f["L3_ffn_sg"]), joined(f["L3_ffn_w_up"], f["L3_ffn_su"])),
        "L3_down": np.swapaxes(joined(f["L3_ffn_w_down"], f["L3_ffn_sd"]), 1, 2),
        "L3_router": f["L3_ffn_gate_w"].T, "L3_ffn_bias": f["L3_ffn_bias"],
        "odd_heads": (np.arange(P)[:, None] // 16 % 2 == np.arange(2)[None, :]).astype(np.float32),
        "head_of_row": (np.arange(P)[:, None] // 16 == np.arange(8)[None, :]).astype(np.float32),
        "spread_heads": (np.eye(B)[:, None, :, None] * (np.arange(8)[:, None] == np.arange(P)[None, :] // 16)[None, :, None, :]
                         ).reshape(B * 8, B, P).astype(np.float32),
        "tile_numbers": np.arange(23, dtype=np.float32)[None, :],
        "slot_base": (np.arange(32) * L3_CAPACITY).astype(np.float32),
        "earlier": np.triu(np.ones((P, P), np.float32), 1),
        "L1_wq": f["L1_xattn_Wq"].T, "L1_wk": f["L1_xattn_Wk"][shared].T, "L1_wv": f["L1_xattn_Wv"].T,
        "L1_wo": f["L1_xattn_Wo"].T,
        "L1_bq": f["L1_xattn_bq"], "L1_bv": f["L1_xattn_bv"], "L1_bo": f["L1_xattn_bo"],
        "L1_bq_cols": cols(f["L1_xattn_bq"]), "L1_bk_cols": cols(f["L1_xattn_bk"][shared]), "L1_head_mask": head_mask(8),
        "L2_wq": f["L2_xattn_wq"], "L2_wk": f["L2_xattn_wk"].T, "L2_wv": f["L2_xattn_wv"].T, "L2_wo": f["L2_xattn_wo"],
        "L2_bq": f["L2_xattn_bq"], "L2_bv": f["L2_xattn_bv"], "L2_bo": f["L2_xattn_bo"],
        "L2_bq_cols": cols(f["L2_xattn_bq"]), "L2_bk_cols": cols(f["L2_xattn_bk"]), "L2_head_mask": head_mask(16),
        "mask_causal": f["mask_SxS2_bc0"].view(np.int32), "mask_padding": f["mask_BxS2_bk0"].view(np.int32).reshape(-1),
        "mask_ff": f["mask_BxSxS2_ff0"],
        "x": f["x"], "ctx_2048": f["ctx_2048"], "fside_S2_0": f["fside_S2_0"],
        "toeplitz": padded[:, at],
        "L0_ffn_w1T": f["L0_ffn_w1"].T, "L0_ffn_w2T": f["L0_ffn_w2"].T,
        "L1_ffn_w1T": f["L1_ffn_w1"].T, "L1_ffn_w2T": f["L1_ffn_w2"].T,
        "L1_ffn_b1": f["L1_ffn_b1"], "L1_ffn_b2": f["L1_ffn_b2"],
        "ident": np.eye(P, dtype=np.float32),
    }
    a, arrays = Names(), {}
    a.by_name = {}
    for name, v in laid.items():
        v = np.ascontiguousarray(v)
        arrays[f"in_{name}_dram"] = v
        a.by_name[name] = nc.dram_tensor(f"in_{name}_dram", v.shape, mybir.dt.from_np(v.dtype), kind="ExternalInput").ap()
    a.out = nc.dram_tensor("out_0_dram", (B, S, D), F32, kind="ExternalOutput").ap()
    program(nc, a)
    r = _run(nc, [arrays], core_ids=[0])
    return r.results[0]["out_0_dram"]
```
